# Optimizing a Trainium2 kernel written in Bass

```python
import numpy as np
import jax
import jax.numpy as jnp

def _softmax(x, axis=-1):
    return jax.nn.softmax(x, axis=axis)

def _gelu(x):
    return jax.nn.gelu(x, approximate=True)

def _silu(x):
    return jax.nn.silu(x)

def _sigmoid(x):
    return jax.nn.sigmoid(x)

def _layernorm(x, axis=-1, eps=1e-05):
    m = jnp.mean(x, axis=axis, keepdims=True)
    v = jnp.var(x, axis=axis, keepdims=True)
    return (x - m) / jnp.sqrt(v + eps)

def _scatter_add(tgt, idx, src, axis=0):
    return tgt.at[idx].add(src)

def _segment_sum(src, seg, n):
    return jax.ops.segment_sum(src, seg, n)
kernel_name = 'mk_adaln_attn_ffn_d2_seqx_r8_6e4ce1'

def setup_inputs(seed: int=0):
    np.random.seed(seed)
    _w = jnp.asarray

    def _rec_inputs():
        import jax
        import jax.numpy as jnp
        _rk = jax.random.key(seed)
        x = -0.000125 + 0.9999 * jax.random.normal(jax.random.fold_in(_rk, 1), (8, 256, 128), jnp.float32)
        _lenS = 256 - jax.random.randint(jax.random.fold_in(_rk, 7), (8,), 0, max(1, 256 // 4) + 1, jnp.int32)
        _lenS2 = 256 - jax.random.randint(jax.random.fold_in(_rk, 8), (8,), 0, max(1, 256 // 4) + 1, jnp.int32)
        cond_1024 = 0.00782532 + 1.00527 * jax.random.normal(jax.random.fold_in(_rk, 11), (8, 128), jnp.float32)
        return (x, cond_1024)
    x, cond_1024 = _rec_inputs()

    def _L0_cond_setup():
        import jax, jax.numpy as jnp
        import numpy as np
        NHID = 128
        NHEAD = 16
        HEAD_DIM = 64
        B, L = (8, 512)
        key = jax.random.key(seed)
        ks = jax.random.split(key, 12)
        s_in = 1.0 / np.sqrt(NHID)
        s_o = 1.0 / np.sqrt(NHEAD * HEAD_DIM)
        return {'x': jax.random.normal(ks[0], (B, L, NHID), dtype=jnp.float32), 'ax': jax.random.normal(ks[1], (B, NHID), dtype=jnp.float32), 'WQ_w': jax.random.normal(ks[2], (NHID, NHEAD * HEAD_DIM), dtype=jnp.float32) * s_in, 'WQ_b': jnp.zeros((NHEAD * HEAD_DIM,), dtype=jnp.float32), 'WK_w': jax.random.normal(ks[3], (NHID, NHEAD * HEAD_DIM), dtype=jnp.float32) * s_in, 'WK_b': jnp.zeros((NHEAD * HEAD_DIM,), dtype=jnp.float32), 'WV_w': jax.random.normal(ks[4], (NHID, NHEAD * HEAD_DIM), dtype=jnp.float32) * s_in, 'WV_b': jnp.zeros((NHEAD * HEAD_DIM,), dtype=jnp.float32), 'WO_w': jax.random.normal(ks[5], (NHEAD * HEAD_DIM, NHID), dtype=jnp.float32) * s_o, 'WO_b': jnp.zeros((NHID,), dtype=jnp.float32)}
    _L0_cond_all = _L0_cond_setup()
    _L0_cond_in = {k: v for k, v in _L0_cond_all.items() if k in ('WQ_w', 'WQ_b', 'WK_w', 'WK_b', 'WV_w', 'WV_b', 'WO_w', 'WO_b')}
    del _L0_cond_all

    def _L0_attn_setup():
        import jax, jax.numpy as jnp
        import numpy as np
        DIM = 128
        HEADS = 16
        DIM_HEAD = 64
        INNER = HEADS * DIM_HEAD
        EPS = 1e-06

        def elu_feature_map(t):
            return jnp.where(t > 0, t + 1.0, jnp.exp(t))
        key = jax.random.key(seed)
        k1, k2, k3, k4 = jax.random.split(key, 4)
        B, N = (4, 1024)
        x = jax.random.normal(k1, (B, N, DIM), dtype=jnp.float32)
        s_in = 1.0 / np.sqrt(DIM)
        s_out = 1.0 / np.sqrt(INNER)
        Wqkv = jax.random.uniform(k2, (DIM, 3 * INNER), dtype=jnp.float32, minval=-s_in, maxval=s_in)
        Wout = jax.random.uniform(k3, (INNER, DIM), dtype=jnp.float32, minval=-s_out, maxval=s_out)
        bout = jax.random.uniform(k4, (DIM,), dtype=jnp.float32, minval=-s_out, maxval=s_out)
        return {'x': x, 'Wqkv': Wqkv, 'Wout': Wout, 'bout': bout}
    _L0_attn_all = _L0_attn_setup()
    _L0_attn_in = {k: v for k, v in _L0_attn_all.items() if k in ('Wqkv', 'Wout', 'bout')}
    del _L0_attn_all

    def _L0_cond2_setup():
        import jax, jax.numpy as jnp
        import numpy as np
        B, T, D, H = (64, 64, 128, 128)
        SCALE = 0.02
        key = jax.random.key(seed)
        ks = jax.random.split(key, 9)
        return {'carry': jax.random.normal(ks[0], (B, H), jnp.float32), 'x': jax.random.normal(ks[1], (B, T, D), jnp.float32), 'W_ir': jax.random.normal(ks[2], (D, H), jnp.float32) * SCALE, 'W_iz': jax.random.normal(ks[3], (D, H), jnp.float32) * SCALE, 'W_in': jax.random.normal(ks[4], (D, H), jnp.float32) * SCALE, 'b_ir': jnp.zeros((H,), jnp.float32), 'b_iz': jnp.zeros((H,), jnp.float32), 'b_in': jnp.zeros((H,), jnp.float32), 'W_hr': jax.random.normal(ks[5], (H, H), jnp.float32) * SCALE, 'W_hz': jax.random.normal(ks[6], (H, H), jnp.float32) * SCALE, 'W_hn': jax.random.normal(ks[7], (H, H), jnp.float32) * SCALE, 'b_hn': jnp.zeros((H,), jnp.float32)}
    _L0_cond2_all = _L0_cond2_setup()
    _L0_cond2_in = {k: v for k, v in _L0_cond2_all.items() if k in ('W_ir', 'W_iz', 'W_in', 'b_ir', 'b_iz', 'b_in', 'W_hr', 'W_hz', 'W_hn', 'b_hn')}
    del _L0_cond2_all

    def _L0_ffn_setup():
        import math
        import jax, jax.numpy as jnp
        import numpy as np
        D_MODEL = 128
        D_FF = 512
        N_EXPERTS = 8
        CAPACITY_FACTOR = 1.25
        L, B = (64, 8)

        def _route(tokens, router_w):
            T = tokens.shape[0]
            E = router_w.shape[0]
            capacity = int(math.ceil(T / E * CAPACITY_FACTOR))
            logits = tokens @ router_w.T
            probs = jax.nn.softmax(logits, axis=-1)
            top1_idx = jnp.argmax(probs, axis=-1)
            top1_prob = jnp.max(probs, axis=-1)
            order = jnp.lexsort((-top1_prob, top1_idx))
            sorted_e = top1_idx[order]
            counts = jnp.bincount(top1_idx, length=E)
            start = jnp.cumsum(counts) - counts
            pos_in_group = jnp.arange(T) - start[sorted_e]
            keep_sorted = pos_in_group < capacity
            keep = jnp.zeros((T,), bool).at[order].set(keep_sorted)
            return jnp.where(keep, top1_idx, 0).astype(jnp.int32)
        key = jax.random.key(seed)
        ks = jax.random.split(key, 6)
        s_in = 1.0 / math.sqrt(D_MODEL)
        s_ff = 1.0 / math.sqrt(D_FF)
        return {'x': jax.random.normal(ks[0], (L, B, D_MODEL), dtype=jnp.float32), 'router_w': jax.random.uniform(ks[1], (N_EXPERTS, D_MODEL), minval=-s_in, maxval=s_in), 'W1': jax.random.uniform(ks[2], (N_EXPERTS, D_MODEL, D_FF), minval=-s_in, maxval=s_in), 'b1': jax.random.uniform(ks[3], (N_EXPERTS, D_FF), minval=-s_in, maxval=s_in), 'W2': jax.random.uniform(ks[4], (N_EXPERTS, D_FF, D_MODEL), minval=-s_ff, maxval=s_ff), 'b2': jax.random.uniform(ks[5], (N_EXPERTS, D_MODEL), minval=-s_ff, maxval=s_ff)}
    _L0_ffn_all = _L0_ffn_setup()
    _L0_ffn_in = {k: v for k, v in _L0_ffn_all.items() if k in ('router_w', 'W1', 'b1', 'W2', 'b2')}
    del _L0_ffn_all

    def _L1_cond_setup():
        import jax, jax.numpy as jnp
        import numpy as np
        LATENT = 128
        key = jax.random.key(seed)
        k1, k2, k3, k4 = jax.random.split(key, 4)
        B, T, D = (64, 64, LATENT)
        h_t = jax.random.normal(k1, (B, D), dtype=jnp.float32)
        z = jax.random.normal(k2, (B, T, D), dtype=jnp.float32)
        bound = 1.0 / np.sqrt(2 * D)
        W = jax.random.uniform(k3, (D, 2 * D), minval=-bound, maxval=bound, dtype=jnp.float32)
        b = jax.random.uniform(k4, (D,), minval=-bound, maxval=bound, dtype=jnp.float32)
        alpha = jnp.full((D,), 0.1, dtype=jnp.float32)
        return {'h_t': h_t, 'z': z, 'W': W, 'b': b, 'alpha': alpha}
    _L1_cond_all = _L1_cond_setup()
    _L1_cond_in = {k: v for k, v in _L1_cond_all.items() if k in ('W', 'b', 'alpha')}
    del _L1_cond_all

    def _L1_attn_setup():
        import jax, jax.numpy as jnp
        import numpy as np
        EMBED_DIM = 128
        LAMBDA_INIT = 0.8
        EPS = 1e-05
        key = jax.random.key(seed)
        ks = jax.random.split(key, 8)
        D = EMBED_DIM
        x = jax.random.normal(ks[0], (4, 256, D), dtype=jnp.float32)
        s = 1.0 / np.sqrt(D)
        w_q12 = jax.random.uniform(ks[1], (D, 2 * D), jnp.float32, -s, s)
        w_k12 = jax.random.uniform(ks[2], (D, 2 * D), jnp.float32, -s, s)
        w_v = jax.random.uniform(ks[3], (D, D), jnp.float32, -s, s)
        lambda_q1 = 0.1 * jax.random.normal(ks[4], (D,), jnp.float32)
        lambda_k1 = 0.1 * jax.random.normal(ks[5], (D,), jnp.float32)
        lambda_q2 = 0.1 * jax.random.normal(ks[6], (D,), jnp.float32)
        lambda_k2 = 0.1 * jax.random.normal(ks[7], (D,), jnp.float32)
        return {'x': x, 'w_q12': w_q12, 'w_k12': w_k12, 'w_v': w_v, 'lambda_q1': lambda_q1, 'lambda_k1': lambda_k1, 'lambda_q2': lambda_q2, 'lambda_k2': lambda_k2}
    _L1_attn_all = _L1_attn_setup()
    _L1_attn_in = {k: v for k, v in _L1_attn_all.items() if k in ('w_q12', 'w_k12', 'w_v', 'lambda_q1', 'lambda_k1', 'lambda_q2', 'lambda_k2')}
    del _L1_attn_all

    def _L1_cond2_setup():
        import jax, jax.numpy as jnp
        import numpy as np
        IN_FEATURES = 128
        OUT_FEATURES = 128
        BATCH = 32
        SEQ = 128
        EPS = 1e-08
        key = jax.random.key(seed)
        k1, k2, k3 = jax.random.split(key, 3)
        Efou = jax.random.normal(k1, (BATCH, SEQ, IN_FEATURES), dtype=jnp.float32)
        y = jax.random.normal(k2, (BATCH, IN_FEATURES), dtype=jnp.float32)
        weight = jax.random.normal(k3, (IN_FEATURES, OUT_FEATURES), dtype=jnp.float32)
        return {'Efou': Efou, 'y': y, 'weight': weight}
    _L1_cond2_all = _L1_cond2_setup()
    _L1_cond2_in = {k: v for k, v in _L1_cond2_all.items() if k in ('weight',)}
    del _L1_cond2_all

    def _L1_ffn_setup():
        import jax, jax.numpy as jnp
        import numpy as np
        B, S, H = (2, 256, 128)
        E, I, K = (8, 512, 2)

        def _moe_forward(x, gate_w, wg, wu, wd):
            b, s, h = x.shape
            x_flat = x.reshape(-1, h)
            logits = x_flat @ gate_w.T
            top_v, top_i = jax.lax.top_k(logits, K)
            probs = jax.nn.softmax(top_v.astype(jnp.float32), axis=-1).astype(logits.dtype)
            one_hot = jax.nn.one_hot(top_i, E, dtype=probs.dtype)
            combine = jnp.einsum('tk,tke->et', probs, one_hot)

            def body(acc, ws):
                wge, wue, wde, we = ws
                hidden = jax.nn.silu(x_flat @ wge.T) * (x_flat @ wue.T)
                return (acc + we[:, None] * (hidden @ wde.T), None)
            out, _ = jax.lax.scan(body, jnp.zeros_like(x_flat), (wg, wu, wd, combine))
            return out.reshape(b, s, h)
        key = jax.random.key(seed)
        ks = jax.random.split(key, 5)
        scale_h = 1.0 / np.sqrt(H)
        scale_i = 1.0 / np.sqrt(I)
        x = jax.random.normal(ks[0], (B, S, H), dtype=jnp.float32)
        gate_w = jax.random.normal(ks[1], (E, H), dtype=jnp.float32) * scale_h
        wg = jax.random.normal(ks[2], (E, I, H), dtype=jnp.float32) * scale_h
        wu = jax.random.normal(ks[3], (E, I, H), dtype=jnp.float32) * scale_h
        wd = jax.random.normal(ks[4], (E, H, I), dtype=jnp.float32) * scale_i
        return {'x': x, 'gate_w': gate_w, 'wg': wg, 'wu': wu, 'wd': wd}
    _L1_ffn_all = _L1_ffn_setup()
    _L1_ffn_in = {k: v for k, v in _L1_ffn_all.items() if k in ('gate_w', 'wg', 'wu', 'wd')}
    del _L1_ffn_all
    return {'x': x, 'cond_1024': cond_1024, 'L0_cond_WQ_w': _L0_cond_in['WQ_w'], 'L0_cond_WQ_b': _L0_cond_in['WQ_b'], 'L0_cond_WK_w': _L0_cond_in['WK_w'], 'L0_cond_WK_b': _L0_cond_in['WK_b'], 'L0_cond_WV_w': _L0_cond_in['WV_w'], 'L0_cond_WV_b': _L0_cond_in['WV_b'], 'L0_cond_WO_w': _L0_cond_in['WO_w'], 'L0_cond_WO_b': _L0_cond_in['WO_b'], 'L0_attn_Wqkv': _L0_attn_in['Wqkv'], 'L0_attn_Wout': _L0_attn_in['Wout'], 'L0_attn_bout': _L0_attn_in['bout'], 'L0_cond2_W_ir': _L0_cond2_in['W_ir'], 'L0_cond2_W_iz': _L0_cond2_in['W_iz'], 'L0_cond2_W_in': _L0_cond2_in['W_in'], 'L0_cond2_b_ir': _L0_cond2_in['b_ir'], 'L0_cond2_b_iz': _L0_cond2_in['b_iz'], 'L0_cond2_b_in': _L0_cond2_in['b_in'], 'L0_cond2_W_hr': _L0_cond2_in['W_hr'], 'L0_cond2_W_hz': _L0_cond2_in['W_hz'], 'L0_cond2_W_hn': _L0_cond2_in['W_hn'], 'L0_cond2_b_hn': _L0_cond2_in['b_hn'], 'L0_ffn_router_w': _L0_ffn_in['router_w'], 'L0_ffn_W1': _L0_ffn_in['W1'], 'L0_ffn_b1': _L0_ffn_in['b1'], 'L0_ffn_W2': _L0_ffn_in['W2'], 'L0_ffn_b2': _L0_ffn_in['b2'], 'L1_cond_W': _L1_cond_in['W'], 'L1_cond_b': _L1_cond_in['b'], 'L1_cond_alpha': _L1_cond_in['alpha'], 'L1_attn_w_q12': _L1_attn_in['w_q12'], 'L1_attn_w_k12': _L1_attn_in['w_k12'], 'L1_attn_w_v': _L1_attn_in['w_v'], 'L1_attn_lambda_q1': _L1_attn_in['lambda_q1'], 'L1_attn_lambda_k1': _L1_attn_in['lambda_k1'], 'L1_attn_lambda_q2': _L1_attn_in['lambda_q2'], 'L1_attn_lambda_k2': _L1_attn_in['lambda_k2'], 'L1_cond2_weight': _L1_cond2_in['weight'], 'L1_ffn_gate_w': _L1_ffn_in['gate_w'], 'L1_ffn_wg': _L1_ffn_in['wg'], 'L1_ffn_wu': _L1_ffn_in['wu'], 'L1_ffn_wd': _L1_ffn_in['wd']}

def reference(x, cond_1024, L0_cond_WQ_w, L0_cond_WQ_b, L0_cond_WK_w, L0_cond_WK_b, L0_cond_WV_w, L0_cond_WV_b, L0_cond_WO_w, L0_cond_WO_b, L0_attn_Wqkv, L0_attn_Wout, L0_attn_bout, L0_cond2_W_ir, L0_cond2_W_iz, L0_cond2_W_in, L0_cond2_b_ir, L0_cond2_b_iz, L0_cond2_b_in, L0_cond2_W_hr, L0_cond2_W_hz, L0_cond2_W_hn, L0_cond2_b_hn, L0_ffn_router_w, L0_ffn_W1, L0_ffn_b1, L0_ffn_W2, L0_ffn_b2, L1_cond_W, L1_cond_b, L1_cond_alpha, L1_attn_w_q12, L1_attn_w_k12, L1_attn_w_v, L1_attn_lambda_q1, L1_attn_lambda_k1, L1_attn_lambda_q2, L1_attn_lambda_k2, L1_cond2_weight, L1_ffn_gate_w, L1_ffn_wg, L1_ffn_wu, L1_ffn_wd):
    import jax
    import jax.numpy as jnp

    def _L0_cond_ref(x, ax, WQ_w, WQ_b, WK_w, WK_b, WV_w, WV_b, WO_w, WO_b):
        import jax, jax.numpy as jnp
        import numpy as np
        NHID = 128
        NHEAD = 16
        HEAD_DIM = 64
        B, L = (8, 512)
        Bx, Lx, H = x.shape
        nh, d = (NHEAD, HEAD_DIM)
        q = (x @ WQ_w + WQ_b).reshape(Bx, Lx, nh, d)
        k = (x @ WK_w + WK_b).reshape(Bx, Lx, nh, d)
        ak = (ax @ WK_w + WK_b).reshape(Bx, 1, nh, d)
        av = (ax @ WV_w + WV_b).reshape(Bx, 1, nh, d)
        pad_k = jnp.pad(k, ((0, 0), (1, 1), (0, 0), (0, 0)))
        k_shift = jnp.stack([pad_k[:, t:Lx + t] for t in range(3)], axis=3)
        akb = jnp.broadcast_to(ak, (Bx, Lx, nh, d))[:, :, :, None, :]
        avb = jnp.broadcast_to(av, (Bx, Lx, nh, d))[:, :, :, None, :]
        K = jnp.concatenate([akb, k_shift], axis=3)
        V = jnp.concatenate([avb, k_shift], axis=3)
        scores = jnp.einsum('blhd,blhjd->blhj', q, K) / jnp.sqrt(jnp.float32(d))
        alphas = jax.nn.softmax(scores, axis=-1)
        att = jnp.einsum('blhj,blhjd->blhd', alphas, V).reshape(Bx, Lx, nh * d)
        return att @ WO_w + WO_b

    def _L0_attn_ref(x, Wqkv, Wout, bout):
        import jax, jax.numpy as jnp
        import numpy as np
        DIM = 128
        HEADS = 16
        DIM_HEAD = 64
        INNER = HEADS * DIM_HEAD
        EPS = 1e-06

        def elu_feature_map(t):
            return jnp.where(t > 0, t + 1.0, jnp.exp(t))
        B, N, D = x.shape
        qkv = x @ Wqkv
        q, k, v = jnp.split(qkv, 3, axis=-1)
        resh = lambda t: t.reshape(B, N, HEADS, DIM_HEAD).transpose(0, 2, 1, 3)
        q, k, v = (resh(q), resh(k), resh(v))
        q = elu_feature_map(q)
        k = elu_feature_map(k)
        kv = jnp.einsum('bhnd,bhnf->bhdf', k, v)
        k_sum = k.sum(axis=-2)
        qkv_out = jnp.einsum('bhnd,bhdf->bhnf', q, kv)
        q_k_sum = jnp.einsum('bhnd,bhd->bhn', q, k_sum)
        out = qkv_out / (q_k_sum[..., None] + EPS)
        out = out.transpose(0, 2, 1, 3).reshape(B, N, INNER)
        return out @ Wout + bout

    def _L0_cond2_ref(carry, x, W_ir, W_iz, W_in, b_ir, b_iz, b_in, W_hr, W_hz, W_hn, b_hn):
        import jax, jax.numpy as jnp
        import numpy as np
        B, T, D, H = (64, 64, 128, 128)
        SCALE = 0.02
        xt = jnp.transpose(x, (1, 0, 2))
        xr = jnp.einsum('tbd,dh->tbh', xt, W_ir) + b_ir
        xz = jnp.einsum('tbd,dh->tbh', xt, W_iz) + b_iz
        xn = jnp.einsum('tbd,dh->tbh', xt, W_in) + b_in

        def step(h, inp):
            xr_t, xz_t, xn_t = inp
            r = jax.nn.sigmoid(xr_t + h @ W_hr)
            z = jax.nn.sigmoid(xz_t + h @ W_hz)
            n = jnp.tanh(xn_t + r * (h @ W_hn + b_hn))
            h_new = (1.0 - z) * n + z * h
            return (h_new, h_new)
        final_state, seq = jax.lax.scan(step, carry, (xr, xz, xn))
        return jnp.transpose(seq, (1, 0, 2))

    def _L0_ffn_ref(x, router_w, W1, b1, W2, b2):
        import math
        import jax, jax.numpy as jnp
        import numpy as np
        D_MODEL = 128
        D_FF = 512
        N_EXPERTS = 8
        CAPACITY_FACTOR = 1.25
        L, B = (64, 8)

        def _route(tokens, router_w):
            T = tokens.shape[0]
            E = router_w.shape[0]
            capacity = int(math.ceil(T / E * CAPACITY_FACTOR))
            logits = tokens @ router_w.T
            probs = jax.nn.softmax(logits, axis=-1)
            top1_idx = jnp.argmax(probs, axis=-1)
            top1_prob = jnp.max(probs, axis=-1)
            order = jnp.lexsort((-top1_prob, top1_idx))
            sorted_e = top1_idx[order]
            counts = jnp.bincount(top1_idx, length=E)
            start = jnp.cumsum(counts) - counts
            pos_in_group = jnp.arange(T) - start[sorted_e]
            keep_sorted = pos_in_group < capacity
            keep = jnp.zeros((T,), bool).at[order].set(keep_sorted)
            return jnp.where(keep, top1_idx, 0).astype(jnp.int32)
        Lx, Bx, D = x.shape
        T = Lx * Bx
        E = router_w.shape[0]
        tokens = x.reshape(T, D)
        final_e = _route(tokens, router_w)
        out = jnp.zeros_like(tokens)
        for e in range(E):
            h = jax.nn.relu(tokens @ W1[e] + b1[e])
            y = h @ W2[e] + b2[e]
            out = out + jnp.where((final_e == e)[:, None], y, 0.0)
        return out.reshape(Lx, Bx, D)

    def _L1_cond_ref(h_t, z, W, b, alpha):
        import jax, jax.numpy as jnp
        import numpy as np
        LATENT = 128
        D = h_t.shape[-1]
        Wh = W[:, :D]
        Wz = W[:, D:]
        leak = 1.0 - alpha

        def step(h, z_t):
            gate = jax.nn.sigmoid(h @ Wh.T + z_t @ Wz.T + b)
            h_new = jnp.tanh(h * leak + gate * z_t)
            return (h_new, h_new)
        _, hs = jax.lax.scan(step, h_t, jnp.swapaxes(z, 0, 1))
        return jnp.swapaxes(hs, 0, 1)

    def _L1_attn_ref(x, w_q12, w_k12, w_v, lambda_q1, lambda_k1, lambda_q2, lambda_k2):
        import jax, jax.numpy as jnp
        import numpy as np
        EMBED_DIM = 128
        LAMBDA_INIT = 0.8
        EPS = 1e-05
        D = x.shape[-1]
        scale = D ** (-0.25)
        q12 = jnp.einsum('bsd,de->bse', x, w_q12)
        k12 = jnp.einsum('bsd,de->bse', x, w_k12)
        q1, q2 = jnp.split(q12, 2, axis=-1)
        k1, k2 = jnp.split(k12, 2, axis=-1)
        v = jnp.einsum('bsd,de->bse', x, w_v)
        attn1 = jnp.einsum('bqd,bkd->bqk', q1, k1) * scale
        attn2 = jnp.einsum('bqd,bkd->bqk', q2, k2) * scale
        lam1 = jnp.exp(jnp.sum(lambda_q1 * lambda_k1))
        lam2 = jnp.exp(jnp.sum(lambda_q2 * lambda_k2))
        lam_full = lam1 - lam2 + LAMBDA_INIT
        diff = jax.nn.softmax(attn1, axis=-1) - lam_full * jax.nn.softmax(attn2, axis=-1)
        out = jnp.einsum('bqk,bkd->bqd', diff, v)
        rms = jnp.sqrt(jnp.mean(out * out, axis=-1, keepdims=True) + EPS)
        return out / rms * (1.0 - LAMBDA_INIT)

    def _L1_cond2_ref(Efou, y, weight):
        import jax, jax.numpy as jnp
        import numpy as np
        IN_FEATURES = 128
        OUT_FEATURES = 128
        BATCH = 32
        SEQ = 128
        EPS = 1e-08
        scale = 1.0 / np.sqrt(np.float32(weight.shape[0]))
        ys = y * scale
        d = jax.lax.rsqrt(jnp.einsum('bi,io->bo', ys * ys, weight * weight) + EPS)
        out = jnp.einsum('bsi,io->bso', Efou * ys[:, None, :], weight) * d[:, None, :]
        return out

    def _L1_ffn_ref(x, gate_w, wg, wu, wd):
        import jax, jax.numpy as jnp
        import numpy as np
        B, S, H = (2, 256, 128)
        E, I, K = (8, 512, 2)

        def _moe_forward(x, gate_w, wg, wu, wd):
            b, s, h = x.shape
            x_flat = x.reshape(-1, h)
            logits = x_flat @ gate_w.T
            top_v, top_i = jax.lax.top_k(logits, K)
            probs = jax.nn.softmax(top_v.astype(jnp.float32), axis=-1).astype(logits.dtype)
            one_hot = jax.nn.one_hot(top_i, E, dtype=probs.dtype)
            combine = jnp.einsum('tk,tke->et', probs, one_hot)

            def body(acc, ws):
                wge, wue, wde, we = ws
                hidden = jax.nn.silu(x_flat @ wge.T) * (x_flat @ wue.T)
                return (acc + we[:, None] * (hidden @ wde.T), None)
            out, _ = jax.lax.scan(body, jnp.zeros_like(x_flat), (wg, wu, wd, combine))
            return out.reshape(b, s, h)
        return _moe_forward(x, gate_w, wg, wu, wd)
    x = x + _L0_attn_ref(_L0_cond_ref(x, cond_1024, L0_cond_WQ_w, L0_cond_WQ_b, L0_cond_WK_w, L0_cond_WK_b, L0_cond_WV_w, L0_cond_WV_b, L0_cond_WO_w, L0_cond_WO_b), L0_attn_Wqkv, L0_attn_Wout, L0_attn_bout)
    x = x + _L0_ffn_ref(_L0_cond2_ref(cond_1024, x, L0_cond2_W_ir, L0_cond2_W_iz, L0_cond2_W_in, L0_cond2_b_ir, L0_cond2_b_iz, L0_cond2_b_in, L0_cond2_W_hr, L0_cond2_W_hz, L0_cond2_W_hn, L0_cond2_b_hn), L0_ffn_router_w, L0_ffn_W1, L0_ffn_b1, L0_ffn_W2, L0_ffn_b2)
    x = x + _L1_attn_ref(_L1_cond_ref(cond_1024, x, L1_cond_W, L1_cond_b, L1_cond_alpha), L1_attn_w_q12, L1_attn_w_k12, L1_attn_w_v, L1_attn_lambda_q1, L1_attn_lambda_k1, L1_attn_lambda_q2, L1_attn_lambda_k2)
    x = x + _L1_ffn_ref(_L1_cond2_ref(x, cond_1024, L1_cond2_weight), L1_ffn_gate_w, L1_ffn_wg, L1_ffn_wu, L1_ffn_wd)
    return x

_drawn_inputs = setup_inputs


def setup_inputs(seed=0):
    import zlib

    import numpy as np

    out = dict(_drawn_inputs(seed))
    spreads = {'L0_cond_WQ_b': (0.0, 0.271),
     'L0_cond_WK_b': (0.0, 0.1),
     'L0_cond_WV_b': (0.0, 0.1),
     'L0_cond_WO_b': (0.0, 0.1),
     'L0_cond2_b_ir': (0.0, 1.077),
     'L0_cond2_b_iz': (0.0, 0.327),
     'L0_cond2_b_in': (0.0, 0.1),
     'L0_cond2_b_hn': (0.0, 0.1),
     'L1_cond_alpha': (0.10000000149011612, 0.2)}
    factors = {'L0_cond2_W_ir': 3.259,
     'L0_cond2_W_hr': 21.007,
     'L0_cond2_W_hz': 3.216,
     'L1_cond_b': 2.899}
    for name, (base, spread) in spreads.items():
        noise = np.random.default_rng([zlib.crc32(name.encode()), seed]).standard_normal(out[name].shape)
        drawn = base * np.exp(spread * noise) if base else spread * noise
        out[name] = jnp.asarray(drawn.astype(out[name].dtype))
    for name, factor in factors.items():
        out[name] = (out[name] * factor).astype(out[name].dtype)
    return out
```

```python
from contextlib import ExitStack

import concourse.bass as bass
from concourse import mybir

F32 = mybir.dt.float32
BF16 = mybir.dt.bfloat16
I32 = mybir.dt.int32
ACT = mybir.ActivationFunctionType
ALU = mybir.AluOpType
AX = mybir.AxisListType

P = 128
B, T, D = 8, 256, 128
TOK = B * T
NBLK = TOK // P
HEADS, HD = 16, 64
INNER = HEADS * HD
NC = INNER // P
E = 8
FF = 512
NF = FF // P
CAPACITY = -(-TOK * 5 // (E * 4))

ROWS = {}
_at = 0
for _name, _count in (("bq", NC), ("bk", NC), ("bv", NC), ("bo", 1), ("bout", 1), ("b_l1", 1), ("alpha", 1),
                      ("lq1", 1), ("lk1", 1), ("lq2", 1), ("lk2", 1), ("b1", E * NF), ("cond", B),
                      ("router", E), ("gate", E)):
    ROWS[_name] = (_at, _count)
    _at += _count
NROWS = _at


class Net:
    pass


def setup(nc, ctx, a):
    n = Net()

    def sb(name, shape, dt=F32):
        return ctx.enter_context(nc.sbuf_tensor(name, shape, dt))

    n.sb = sb
    n.xT = sb("xT", [P, TOK])
    n.cols = sb("cols", [P, NROWS])
    n.ident = sb("ident", [P, P])
    n.identb = sb("identb", [P, P], BF16)
    n.gru_w = sb("gru_w", [P, 6, P])
    n.gru_b = sb("gru_b", [1, 4, P])
    n.ones_row = sb("ones_row", [1, P])
    n.l1w = sb("l1w", [P, 2 * D])
    n.wq12 = sb("wq12", [P, 2 * D])
    n.wk12 = sb("wk12", [P, 2 * D])
    n.wv1 = sb("wv1", [P, D])
    n.wmod = sb("wmod", [P, D])
    n.b2 = sb("b2", [E, D])
    n.iota8 = sb("iota8", [P, E])
    n.condT = n.cols[:, ROWS["cond"][0]:ROWS["cond"][0] + B]

    load_small = ctx.enter_context(nc.semaphore("load_small"))
    load_x = ctx.enter_context(nc.semaphore("load_x"))
    n.load_later = ctx.enter_context(nc.semaphore("load_later"))
    n.load_experts = ctx.enter_context(nc.semaphore("load_experts"))
    n.load_linear = ctx.enter_context(nc.semaphore("load_linear"))
    rows_done = ctx.enter_context(nc.semaphore("rows_done"))
    ident_base = ctx.enter_context(nc.semaphore("ident_base"))
    ident_done = ctx.enter_context(nc.semaphore("ident_done"))
    x_turned = ctx.enter_context(nc.semaphore("x_turned"))
    x_kept = ctx.enter_context(nc.semaphore("x_kept"))

    small = [("bq", a["L0_cond_WQ_b"]), ("bk", a["L0_cond_WK_b"]), ("bv", a["L0_cond_WV_b"]),
             ("bo", a["L0_cond_WO_b"]), ("bout", a["L0_attn_bout"]), ("b_l1", a["L1_cond_b"]),
             ("alpha", a["L1_cond_alpha"]), ("lq1", a["L1_attn_lambda_q1"]), ("lk1", a["L1_attn_lambda_k1"]),
             ("lq2", a["L1_attn_lambda_q2"]), ("lk2", a["L1_attn_lambda_k2"])]
    with ExitStack() as local:
        rows = local.enter_context(nc.sbuf_tensor("rows", [NROWS, P], F32))
        xtok = local.enter_context(nc.sbuf_tensor("xtok", [P, NBLK, D], F32))
        turn = [local.enter_context(nc.psum_tensor(f"turn{i}", [P, 4, P], F32)) for i in range(2)]
        turn_rows = local.enter_context(nc.psum_tensor("turn_rows", [P, NROWS], F32))
        with nc.Block() as block:

            @block.sync
            def _(sp):
                for name, src in small:
                    r0, k = ROWS[name]
                    sp.dma_start(rows[r0:r0 + k, :], src.rearrange("(r d) -> r d", d=P)).then_inc(load_small, 16)
                r0, k = ROWS["b1"]
                sp.dma_start(rows[r0:r0 + k, :], a["L0_ffn_b1"].rearrange("e (c f) -> (e c) f", f=P)).then_inc(load_small, 16)
                for name, src in (("cond", "cond_1024"), ("router", "L0_ffn_router_w"), ("gate", "L1_ffn_gate_w")):
                    r0, k = ROWS[name]
                    sp.dma_start(rows[r0:r0 + k, :], a[src]).then_inc(load_small, 16)
                for i, key in enumerate(("L0_cond2_W_ir", "L0_cond2_W_iz", "L0_cond2_W_in",
                                         "L0_cond2_W_hr", "L0_cond2_W_hz", "L0_cond2_W_hn")):
                    sp.dma_start(n.gru_w[:, i, :], a[key]).then_inc(n.load_later, 16)
                for i, key in enumerate(("L0_cond2_b_ir", "L0_cond2_b_iz", "L0_cond2_b_in", "L0_cond2_b_hn")):
                    sp.dma_start(n.gru_b[:, i, :], a[key].rearrange("(r d) -> r d", r=1)).then_inc(n.load_later, 16)
                for dst, key in ((n.l1w, "L1_cond_W"), (n.wq12, "L1_attn_w_q12"), (n.wk12, "L1_attn_w_k12"),
                                 (n.wv1, "L1_attn_w_v"), (n.wmod, "L1_cond2_weight"), (n.b2, "L0_ffn_b2")):
                    sp.dma_start(dst[:, :], a[key]).then_inc(n.load_later, 16)
                n.later_loads = 16 * 16

            @block.scalar
            def _(act):
                act.dma_start(xtok[:, :, :], a["x"].rearrange("b (i p) d -> p (b i) d", p=P)).then_inc(load_x, 16)
                act.wait_ge(rows_done, 1)
                nc.scalar.activation(n.cols[:, :], turn_rows[:, :], ACT.Copy)
                for g in range(NBLK // 4):
                    act.wait_ge(x_turned, g + 1)
                    out = n.xT[:, :].rearrange("p (i t b) -> p b i t", i=2, b=B)[:, 2 * g:2 * g + 2]
                    nc.scalar.activation(out, turn[g % 2][:, :, :].rearrange("p (b i) t -> p b i t", i=2),
                                         ACT.Copy).then_inc(x_kept, 1)

            @block.gpsimd
            def _(pool):
                pool.memset(n.ident[:, :], 0.0).then_inc(ident_base, 1)
                pool.wait_ge(ident_base, 1)
                pool.affine_select(out=n.ident[:, :], in_=n.ident[:, :], compare_op=ALU.not_equal, fill=1.0,
                                   base=0, pattern=[[-1, P]], channel_multiplier=1).then_inc(ident_done, 1)
                pool.wait_ge(ident_done, 1)
                pool.tensor_copy(n.identb[:, :], n.ident[:, :])
                for e in range(E):
                    pool.memset(n.iota8[:, e:e + 1], float(e))
                pool.memset(n.ones_row[:, :], 1.0)

            @block.tensor
            def _(pe):
                pe.wait_ge(ident_done, 1)
                pe.wait_ge(load_small, 16 * (len(small) + 4))
                nc.tensor.transpose(turn_rows[:, :], rows[:, :], n.ident[0:NROWS, 0:NROWS]).then_inc(rows_done, 1)
                pe.wait_ge(load_x, 16)
                for g in range(NBLK // 4):
                    if g >= 2:
                        pe.wait_ge(x_kept, g - 1)
                    for i in range(4):
                        mm = nc.tensor.transpose(turn[g % 2][:, i, :], xtok[:, 4 * g + i, :], n.ident[:, :])
                    mm.then_inc(x_turned, 1)
    return n


def local_attention(nc, n, a, yB, wqkv, wout):
    HALF = TOK // 2
    HB = HALF // P
    SH = B
    KW = HALF + 2 * SH
    UNITS = 2 * NC
    J = 4
    with ExitStack() as local:
        def sb(name, shape, dt=F32):
            return local.enter_context(nc.sbuf_tensor(name, shape, dt))

        def sem(name):
            return local.enter_context(nc.semaphore(name))

        wq, wk, wv = (sb(k, [P, INNER]) for k in ("wq", "wk", "wv"))
        wo = sb("wo", [P, NC, D])
        bq8 = sb("bq8", [P, NC])
        headsel = sb("headsel", [P, 2])
        pick = sb("pick", [24, J, 2, HD], BF16)
        akT, avT = sb("akT", [P, NC, B]), sb("avT", [P, NC, B])
        qb = [sb(f"qb{i}", [P, HALF]) for i in range(3)]
        kb = [sb(f"kb{i}", [P, KW + SH]) for i in range(3)]
        prod = [sb(f"prod{i}", [P, J, HALF]) for i in range(2)]
        s_max, s_sum, s_rec = (sb(k, [P, HB * 2]) for k in ("s_max", "s_sum", "s_rec"))
        s_sh, s_exp, prob, rest1, rest2 = (sb(k, [P, HB * 2, J]) for k in ("s_sh", "s_exp", "prob", "rest1", "rest2"))
        parts = [sb(f"parts{i}", [P, HB, 3, 2 * J], BF16) for i in range(2)]
        probT = [sb(f"probT{i}", [24, HALF], BF16) for i in range(2)]
        term = [sb(f"term{i}", [P, J, 512]) for i in range(2)]
        pair = [sb(f"pair{i}", [P, 2, 512]) for i in range(2)]
        att = [sb(f"att{i}", [P, 512]) for i in range(2)]
        y_ps = [local.enter_context(nc.psum_tensor(f"y_ps{i}", [P, 512], F32)) for i in range(2)]
        pj = [local.enter_context(nc.psum_tensor(f"pj{i}", [P, 512], F32)) for i in range(2)]
        bc = [local.enter_context(nc.psum_tensor(f"bc{i}", [P, 512], F32)) for i in range(2)]
        sc = local.enter_context(nc.psum_tensor("sc", [P, HB, 2, J], F32))
        tr = local.enter_context(nc.psum_tensor("tr", [24, HALF], BF16))

        loaded = sem("wload"); const_a = sem("const_a"); const_done = sem("const_done")
        cond_proj = sem("cond_proj"); cond_kept = sem("cond_kept")
        proj_done = sem("proj_done"); proj_kept = sem("proj_kept")
        prod_v = sem("prod_v"); prod_g = sem("prod_g")
        score_done = sem("score_done"); soft = sem("soft"); exp_done = sem("exp_done")
        parts_done = sem("parts_done"); turned = sem("turned"); turned_kept = sem("turned_kept")
        spread = sem("spread"); term_done = sem("term_done"); pair_done = sem("pair_done"); att_done = sem("att_done")
        y_part = sem("y_part"); y_kept = sem("y_kept")

        def pieces(u):
            h, c = divmod(u, NC)
            t0 = h * HALF
            k0 = 0 if h == 0 else t0 - SH
            return ([("q", t0, 0, 512), ("q", t0 + 512, 512, 512)]
                    + [("k", k0, SH, 512), ("k", k0 + 512, SH + 512, 512), ("k", k0 + 1024, SH + 1024, SH)])

        def key(u, j, at, width):
            base = (u // NC) * SH + (j - 1) * SH + at
            return kb[u % 3][:, base:base + width]

        with nc.Block() as block:

            @block.sync
            def _(sp):
                for dst, key in ((wk, "L0_cond_WK_w"), (wv, "L0_cond_WV_w"), (wq, "L0_cond_WQ_w")):
                    sp.dma_start(dst[:, :], a[key]).then_inc(loaded, 16)
                sp.dma_start(wo[:, :, :], a["L0_cond_WO_w"].rearrange("(c p) d -> p c d", p=P)).then_inc(loaded, 16)
                sp.dma_start(wqkv[:, :], a["L0_attn_Wqkv"]).then_inc(n.load_linear, 16)
                sp.dma_start(wout[:, :, :], a["L0_attn_Wout"].rearrange("(c p) d -> p c d", p=P)).then_inc(n.load_linear, 16)

            @block.gpsimd
            def _(pool):
                pool.memset(pick[:, :, :, :], 0.0).then_inc(const_a, 1)
                for part in range(3):
                    pool.wait_ge(const_a, part + 1)
                    pool.affine_select(out=pick[:, :, :, :], in_=pick[:, :, :, :], compare_op=ALU.not_equal, fill=1.0,
                                       base=-8 * part, pattern=[[-1, J], [-J, 2], [0, HD]],
                                       channel_multiplier=1).then_inc(const_a, 1)

                def product(u, j):
                    pool.wait_ge(proj_kept, 5 * (u + 1))
                    if u >= 2:
                        pool.wait_ge(score_done, u - 1)
                    pool.tensor_tensor(prod[u % 2][:, j, :], qb[u % 3][:, :], key(u, j, 0, HALF),
                                       ALU.mult).then_inc(prod_g, 1)

                def pair_sum(u, m):
                    s = 2 * u + m
                    pool.wait_ge(term_done, J * (s + 1))
                    if s >= 2:
                        pool.wait_ge(att_done, s - 1)
                    t = term[s % 2]
                    pool.tensor_tensor(pair[s % 2][:, :, :], t[:, 0:2, :], t[:, 2:4, :], ALU.add).then_inc(pair_done, 1)

                for u in range(2):
                    product(u, 1)
                    product(u, 3)
                for u in range(UNITS):
                    pair_sum(u, 0)
                    if u + 2 < UNITS:
                        product(u + 2, 1)
                        product(u + 2, 3)
                    pair_sum(u, 1)

            @block.tensor
            def _(pe):
                pe.wait_ge(loaded, 64)
                for i, w in enumerate((wk, wv)):
                    for c in range(NC):
                        mm = nc.tensor.matmul(pj[i][:, B * c:B * c + B], w[:, P * c:P * c + P], n.condT,
                                              start=True, stop=True)
                    mm.then_inc(cond_proj, 1)
                pe.wait_ge(cond_kept, 2)
                pe.wait_ge(const_done, 1)
                pe.wait_ge(const_a, 4)

                def project(u):
                    c = u % NC
                    for i, (kind, src, _, width) in enumerate(pieces(u)):
                        w = wq if kind == "q" else wk
                        g = 5 * u + i
                        if g >= 2:
                            pe.wait_ge(proj_kept, g - 1)
                        nc.tensor.matmul(pj[g % 2][:, 0:width], w[:, P * c:P * c + P], n.xT[:, src:src + width],
                                         start=True, stop=True).then_inc(proj_done, 1)

                def scores(u, i):
                    if u >= 1 and i == 0:
                        pe.wait_ge(soft, 9 * u - 7)
                    if i == 0:
                        pe.wait_ge(prod_v, 2 * (u + 1))
                        pe.wait_ge(prod_g, 2 * (u + 1))
                    for j in range(J):
                        mm = nc.tensor.matmul(sc[:, i, :, j], prod[u % 2][:, j, P * i:P * i + P], headsel[:, :],
                                              start=True, stop=True)
                    if i == HB - 1:
                        mm.then_inc(score_done, 1)

                def turn_probs(u):
                    pe.wait_ge(parts_done, u + 1)
                    if u >= 1:
                        pe.wait_ge(turned_kept, u)
                    for i in range(HB):
                        mm = nc.tensor.transpose(tr[:, P * i:P * i + P],
                                                 parts[u % 2][:, i, :, :].rearrange("p k r -> p (k r)"), n.identb[:, :])
                    mm.then_inc(turned, 1)

                def spread_probs(u, i):
                    if i == 0:
                        pe.wait_ge(turned_kept, u + 1)
                    m, j = divmod(i, J)
                    g = 2 * J * u + i
                    if g >= 2:
                        pe.wait_ge(term_done, g - 1)
                    nc.tensor.matmul(bc[g % 2][:, :], pick[:, j, :, :].rearrange("r h d -> r (h d)"),
                                     probT[u % 2][:, 512 * m:512 * m + 512], start=True, stop=True).then_inc(spread, 1)

                def project_out(u, m):
                    h, c = divmod(u, NC)
                    if c == 0 and h == 1:
                        pe.wait_ge(y_kept, m + 1)
                    pe.wait_ge(att_done, 2 * u + m + 1)
                    nc.tensor.matmul(y_ps[m][:, :], wo[:, c, :], att[m][:, :], start=(c == 0),
                                     stop=(c == NC - 1)).then_inc(y_part, 1)

                project(0)
                project(1)
                for i in range(HB):
                    scores(0, i)
                turn_probs(0)
                for u in range(UNITS):
                    for i in range(HB):
                        if u + 1 < UNITS:
                            scores(u + 1, i)
                        spread_probs(u, i)
                    if u >= 1:
                        project_out(u - 1, 1)
                    if u + 2 < UNITS:
                        project(u + 2)
                    if u + 1 < UNITS:
                        turn_probs(u + 1)
                    project_out(u, 0)
                project_out(UNITS - 1, 1)

            @block.scalar
            def _(act):
                act.wait_ge(cond_proj, 2)
                act.wait_ge(const_done, 1)

                def keep_projections(u):
                    c = u % NC
                    bk0 = ROWS["bk"][0]
                    if u >= 3:
                        act.wait_ge(prod_v, 2 * (u - 2))
                        act.wait_ge(prod_g, 2 * (u - 2))
                        act.wait_ge(term_done, 2 * J * (u - 2))
                    for i, (kind, _, dst, width) in enumerate(pieces(u)):
                        g = 5 * u + i
                        act.wait_ge(proj_done, g + 1)
                        if kind == "q":
                            nc.scalar.activation(qb[u % 3][:, dst:dst + width], pj[g % 2][:, 0:width], ACT.Identity,
                                                 bias=bq8[:, c:c + 1], scale=float(HD) ** -0.5).then_inc(proj_kept, 1)
                        else:
                            nc.scalar.activation(kb[u % 3][:, dst:dst + width], pj[g % 2][:, 0:width], ACT.Identity,
                                                 bias=n.cols[:, bk0 + c:bk0 + c + 1]).then_inc(proj_kept, 1)

                def exps(u):
                    act.wait_ge(soft, 9 * u + 2)
                    nc.scalar.activation(s_exp[:, :, :], s_sh[:, :, :], ACT.Exp).then_inc(exp_done, 1)

                def keep_turned(u):
                    act.wait_ge(turned, u + 1)
                    if u >= 2:
                        act.wait_ge(spread, 2 * J * (u - 1))
                    nc.scalar.activation(probT[u % 2][:, :], tr[:, :], ACT.Copy).then_inc(turned_kept, 1)

                def keep_y(h):
                    bo = ROWS["bo"][0]
                    for m in range(2):
                        act.wait_ge(y_part, 2 * NC * (h + 1) - 1 + m)
                        at = h * HALF + 512 * m
                        out = yB[:, :].rearrange("p (b t) -> p t b", b=B)[:, at // B:(at + 512) // B]
                        nc.scalar.activation(out, y_ps[m][:, :].rearrange("p (t b) -> p t b", b=B), ACT.Identity,
                                             bias=n.cols[:, bo:bo + 1]).then_inc(y_kept, 1)

                keep_projections(0)
                keep_projections(1)
                exps(0)
                keep_turned(0)
                for u in range(UNITS):
                    if u + 1 < UNITS:
                        exps(u + 1)
                    if u + 2 < UNITS:
                        keep_projections(u + 2)
                    if u + 1 < UNITS:
                        keep_turned(u + 1)
                    if u % NC == NC - 1:
                        keep_y(u // NC)

            @block.vector
            def _(dve):
                bq0, bk0, bv0 = ROWS["bq"][0], ROWS["bk"][0], ROWS["bv"][0]
                nc.vector.tensor_scalar(bq8[:, :], n.cols[:, bq0:bq0 + NC], float(HD) ** -0.5, None, ALU.mult)
                for h in range(2):
                    for other in range(2):
                        nc.vector.memset(headsel[HD * h:HD * h + HD, other:other + 1], float(h == other))
                for i in range(3):
                    nc.vector.memset(kb[i][:, 0:SH], 0.0)
                    last = nc.vector.memset(kb[i][:, KW:KW + SH], 0.0)
                last.then_inc(const_done, 1)
                dve.wait_ge(cond_proj, 2)
                for i, (dst, b0) in enumerate(((akT, bk0), (avT, bv0))):
                    src = pj[i][:, 0:NC * B].rearrange("p (c b) -> p c b", b=B)
                    bias = n.cols[:, b0:b0 + NC].unsqueeze(2).broadcast_to([P, NC, B])
                    nc.vector.tensor_tensor(dst[:, :, :], src, bias, ALU.add).then_inc(cond_kept, 1)
                dve.wait_ge(cond_kept, 2)

                def products(u):
                    c = u % NC
                    dve.wait_ge(proj_kept, 5 * (u + 1))
                    if u >= 2:
                        dve.wait_ge(score_done, u - 1)
                    q3 = qb[u % 3][:, :].rearrange("p (t b) -> p t b", b=B)
                    ak = akT[:, c, :].unsqueeze(1).broadcast_to([P, HALF // B, B])
                    nc.vector.tensor_tensor(prod[u % 2][:, 0, :].rearrange("p (t b) -> p t b", b=B), q3, ak,
                                            ALU.mult).then_inc(prod_v, 1)
                    nc.vector.tensor_tensor(prod[u % 2][:, 2, :], qb[u % 3][:, :], key(u, 2, 0, HALF),
                                            ALU.mult).then_inc(prod_v, 1)

                def softmax(u):
                    at = 9 * u
                    flat = sc[:, :, :, :].rearrange("p i h j -> p (i h) j")
                    wide = [P, HB * 2, J]
                    dve.wait_ge(score_done, u + 1)
                    nc.vector.tensor_reduce(s_max[:, :], flat, AX.X, ALU.max).then_inc(soft, 1)
                    dve.wait_ge(soft, at + 1)
                    nc.vector.tensor_tensor(s_sh[:, :, :], flat, s_max[:, :].unsqueeze(2).broadcast_to(wide),
                                            ALU.subtract).then_inc(soft, 1)
                    dve.wait_ge(exp_done, u + 1)
                    nc.vector.tensor_reduce(s_sum[:, :], s_exp[:, :, :], AX.X, ALU.add).then_inc(soft, 1)
                    dve.wait_ge(soft, at + 3)
                    nc.vector.reciprocal(s_rec[:, :], s_sum[:, :]).then_inc(soft, 1)
                    dve.wait_ge(soft, at + 4)
                    nc.vector.tensor_tensor(prob[:, :, :], s_exp[:, :, :], s_rec[:, :].unsqueeze(2).broadcast_to(wide),
                                            ALU.mult).then_inc(soft, 1)
                    pt = parts[u % 2]
                    if u >= 2:
                        dve.wait_ge(turned, u - 1)
                    pr, r1, r2 = (t[:, :, :].rearrange("p (i h) j -> p i (h j)", h=2) for t in (prob, rest1, rest2))
                    dve.wait_ge(soft, at + 5)
                    nc.vector.tensor_copy(pt[:, :, 0, :], pr).then_inc(soft, 1)
                    dve.wait_ge(soft, at + 6)
                    nc.vector.tensor_tensor(r1, pr, pt[:, :, 0, :], ALU.subtract).then_inc(soft, 1)
                    dve.wait_ge(soft, at + 7)
                    nc.vector.tensor_copy(pt[:, :, 1, :], r1).then_inc(soft, 1)
                    dve.wait_ge(soft, at + 8)
                    nc.vector.tensor_tensor(r2, r1, pt[:, :, 1, :], ALU.subtract).then_inc(soft, 1)
                    dve.wait_ge(soft, at + 9)
                    nc.vector.tensor_copy(pt[:, :, 2, :], r2).then_inc(parts_done, 1)

                def terms(u, m):
                    c = u % NC
                    s = 2 * u + m
                    if s >= 2:
                        dve.wait_ge(pair_done, s - 1)
                    for j in range(J):
                        g = s * J + j
                        dve.wait_ge(spread, g + 1)
                        if j == 0:
                            av = avT[:, c, :].unsqueeze(1).broadcast_to([P, 512 // B, B])
                            nc.vector.tensor_tensor(term[s % 2][:, 0, :].rearrange("p (t b) -> p t b", b=B),
                                                    bc[g % 2][:, :].rearrange("p (t b) -> p t b", b=B), av,
                                                    ALU.mult).then_inc(term_done, 1)
                        else:
                            nc.vector.tensor_tensor(term[s % 2][:, j, :], bc[g % 2][:, :], key(u, j, 512 * m, 512),
                                                    ALU.mult).then_inc(term_done, 1)

                def attended(u, m):
                    s = 2 * u + m
                    dve.wait_ge(pair_done, s + 1)
                    if s >= 2:
                        dve.wait_ge(y_part, s - 1)
                    nc.vector.tensor_tensor(att[s % 2][:, :], pair[s % 2][:, 0, :], pair[s % 2][:, 1, :],
                                            ALU.add).then_inc(att_done, 1)

                products(0)
                products(1)
                softmax(0)
                for u in range(UNITS):
                    terms(u, 0)
                    attended(u, 0)
                    terms(u, 1)
                    if u + 1 < UNITS:
                        softmax(u + 1)
                    if u + 2 < UNITS:
                        products(u + 2)
                    attended(u, 1)


def linear_attention(nc, n, yB, wqkv, wout):
    SEG = T // P
    EPS = 1e-6
    PIECES = 12
    ELU = 8
    with ExitStack() as local:
        def sb(name, shape, dt=F32):
            return local.enter_context(nc.sbuf_tensor(name, shape, dt))

        def ps(name, shape):
            return local.enter_context(nc.psum_tensor(name, shape, F32))

        def sem(name):
            return local.enter_context(nc.semaphore(name))

        kk = [sb(f"kk{i}", [P, SEG, INNER]) for i in range(2)]
        vv = [sb(f"vv{i}", [P, SEG, INNER]) for i in range(2)]
        qq = [sb(f"qq{i}", [P, NC, T]) for i in range(2)]
        ex = [sb(f"ex{i}", [P, 512]) for i in range(2)]
        rl = [sb(f"rl{i}", [P, 512]) for i in range(2)]
        kvT = sb("kvT", [P, NC, P])
        ksm = sb("ksm", [P, NC, P])
        kvw = sb("kvw", [P, NC, D])
        den = [sb(f"den{i}", [P, 512]) for i in range(2)]
        rec = [sb(f"rec{i}", [P, 512]) for i in range(2)]
        qn = sb("qn", [P, NC, T])
        mask = sb("mask", [P, P])
        ones = sb("ones", [P, 1])
        eps = sb("eps", [P, 1])
        pj = [ps(f"lpj{i}", [P, 512]) for i in range(2)]
        kvt_ps = [ps(f"kvt{i}", [P, 4, P]) for i in range(2)]
        kvw_ps = ps("kvw_ps", [P, 4, D])
        den_ps = [ps(f"den_ps{i}", [P, 512]) for i in range(2)]
        out_ps = ps("out_ps", [P, T + NC])
        ks_ps = out_ps[:, T:T + NC]

        const = sem("l_const"); proj_done = sem("l_proj"); piece_kept = sem("l_kept"); elu_in = sem("l_elu_in")
        elu_done = sem("l_elu"); v_kept = sem("l_v"); kvt_done = sem("l_kvt"); kvt_kept = sem("l_kvt_kept")
        ks_done = sem("l_ks"); ks_kept = sem("l_ks_kept"); kvw_done = sem("l_kvw"); kvw_kept = sem("l_kvw_kept")
        den_done = sem("l_den"); eps_done = sem("l_eps"); rec_done = sem("l_rec"); qn_done = sem("l_qn")
        out_done = sem("l_out"); added = sem("l_added")

        def kind(i):
            return "q" if i >= 8 else ("k" if i % 4 < 2 else "v")

        def elu_target(b, e):
            if e < 4:
                return kk[b % 2][:, e // 2, 512 * (e % 2):512 * (e % 2) + 512]
            return qq[b % 2][:, 2 * (e - 4):2 * (e - 4) + 2, :].rearrange("p c t -> p (c t)")

        with nc.Block() as block:

            @block.tensor
            def _(pe):
                pe.wait_ge(n.load_linear, 32)

                def project(b, i):
                    if b >= B:
                        return
                    g = PIECES * b + i
                    if g >= 2:
                        pe.wait_ge(piece_kept, g - 1)
                    if kind(i) == "q":
                        for c in range(2):
                            c0 = (2 * (i - 8) + c) * P
                            mm = nc.tensor.matmul(pj[g % 2][:, T * c:T * c + T], wqkv[:, c0:c0 + P],
                                                  yB[:, T * b:T * b + T], start=True, stop=True)
                    else:
                        at = T * b + P * (i // 4)
                        c0 = INNER + 512 * (i % 4)
                        mm = nc.tensor.matmul(pj[g % 2][:, :], yB[:, at:at + P], wqkv[:, c0:c0 + 512],
                                              start=True, stop=True)
                    mm.then_inc(proj_done, 1)

                def kv_products(b, h):
                    if b >= 1:
                        pe.wait_ge(kvt_kept, 2 * (b - 1) + h + 1)
                    for c in range(4 * h, 4 * h + 4):
                        for i in range(SEG):
                            mm = nc.tensor.matmul(kvt_ps[h][:, c % 4, :], vv[b % 2][:, i, P * c:P * c + P],
                                                  kk[b % 2][:, i, P * c:P * c + P], start=(i == 0), stop=(i == SEG - 1))
                    mm.then_inc(kvt_done, 1)

                def key_sums(b):
                    if b >= 1:
                        pe.wait_ge(added, b)
                    for c in range(NC):
                        for i in range(SEG):
                            mm = nc.tensor.matmul(ks_ps[:, c:c + 1], kk[b % 2][:, i, P * c:P * c + P], ones[:, :],
                                                  start=(i == 0), stop=(i == SEG - 1))
                    mm.then_inc(ks_done, 1)

                def kv_out(b, h):
                    pe.wait_ge(kvt_kept, 2 * b + h + 1)
                    if 2 * b + h >= 1:
                        pe.wait_ge(kvw_kept, 2 * b + h)
                    for c in range(4 * h, 4 * h + 4):
                        mm = nc.tensor.matmul(kvw_ps[:, c % 4, :], kvT[:, c, :], wout[:, c, :], start=True, stop=True)
                    mm.then_inc(kvw_done, 1)

                def denominators(b, m):
                    g = 4 * b + m
                    pe.wait_ge(ks_kept, b + 1)
                    if g >= 2:
                        pe.wait_ge(eps_done, g - 1)
                    for c in range(2):
                        mm = nc.tensor.matmul(den_ps[g % 2][:, T * c:T * c + T], ksm[:, 2 * m + c, :],
                                              qq[b % 2][:, 2 * m + c, :], start=True, stop=True)
                    mm.then_inc(den_done, 1)

                def outputs(b):
                    pe.wait_ge(kvw_kept, 2 * (b + 1))
                    if b >= 1:
                        pe.wait_ge(added, b)
                    for c in range(NC):
                        if c % 2 == 0:
                            pe.wait_ge(qn_done, 4 * b + c // 2 + 1)
                        mm = nc.tensor.matmul(out_ps[:, 0:T], kvw[:, c, :], qn[:, c, :], start=(c == 0), stop=(c == NC - 1))
                    mm.then_inc(out_done, 1)

                pe.wait_ge(const, 1)
                for i in range(PIECES):
                    project(0, i)
                for b in range(B):
                    pe.wait_ge(elu_done, ELU * b + 4)
                    pe.wait_ge(v_kept, 4 * (b + 1))
                    kv_products(b, 0)
                    kv_products(b, 1)
                    project(b + 1, 0)
                    project(b + 1, 1)
                    key_sums(b)
                    project(b + 1, 2)
                    project(b + 1, 3)
                    kv_out(b, 0)
                    project(b + 1, 4)
                    project(b + 1, 5)
                    kv_out(b, 1)
                    project(b + 1, 6)
                    project(b + 1, 7)
                    pe.wait_ge(elu_done, ELU * (b + 1))
                    denominators(b, 0)
                    denominators(b, 1)
                    project(b + 1, 8)
                    denominators(b, 2)
                    project(b + 1, 9)
                    denominators(b, 3)
                    project(b + 1, 10)
                    project(b + 1, 11)
                    outputs(b)

            @block.scalar
            def _(act):
                act.wait_ge(const, 1)

                def keep(b, i):
                    if b >= B:
                        return
                    g = PIECES * b + i
                    act.wait_ge(proj_done, g + 1)
                    if kind(i) == "v":
                        if b >= 2:
                            act.wait_ge(kvt_done, 2 * (b - 1))
                        out = vv[b % 2][:, i // 4, 512 * (i % 2):512 * (i % 2) + 512]
                        nc.scalar.activation(out, pj[g % 2][:, :], ACT.Copy).then_inc(piece_kept, 1)
                        act.wait_ge(piece_kept, g + 1)
                        act.sem_inc(v_kept, 1)
                        return
                    e = ELU * b + (2 * (i // 4) + i % 4 if i < 8 else i - 4)
                    if e >= 2:
                        act.wait_ge(elu_done, e - 1)
                    nc.scalar.activation(ex[e % 2][:, :], pj[g % 2][:, :], ACT.Exp).then_inc(elu_in, 1)
                    nc.scalar.activation(rl[e % 2][:, :], pj[g % 2][:, :], ACT.Relu).then_inc(elu_in, 1)
                    act.wait_ge(elu_in, 2 * (e + 1))
                    act.sem_inc(piece_kept, 1)

                def keep_kv_out(b, h):
                    act.wait_ge(kvw_done, 2 * b + h + 1)
                    if b >= 1:
                        act.wait_ge(out_done, b)
                    nc.scalar.activation(kvw[:, 4 * h:4 * h + 4, :], kvw_ps[:, :, :], ACT.Copy).then_inc(kvw_kept, 1)

                def add_eps(b, m):
                    g = 4 * b + m
                    act.wait_ge(den_done, g + 1)
                    if g >= 2:
                        act.wait_ge(rec_done, g - 1)
                    nc.scalar.activation(den[g % 2][:, :], den_ps[g % 2][:, :], ACT.Identity,
                                         bias=eps[:, 0:1]).then_inc(eps_done, 1)

                for i in range(PIECES):
                    keep(0, i)
                for b in range(B):
                    for i in range(4):
                        keep(b + 1, i)
                    keep_kv_out(b, 0)
                    keep(b + 1, 4)
                    keep(b + 1, 5)
                    keep_kv_out(b, 1)
                    keep(b + 1, 6)
                    keep(b + 1, 7)
                    add_eps(b, 0)
                    add_eps(b, 1)
                    keep(b + 1, 8)
                    add_eps(b, 2)
                    keep(b + 1, 9)
                    add_eps(b, 3)
                    keep(b + 1, 10)
                    keep(b + 1, 11)

            @block.gpsimd
            def _(pool):
                for b in range(B):
                    for m in range(4):
                        pool.wait_ge(rec_done, 4 * b + m + 1)
                        if b >= 1 and m == 0:
                            pool.wait_ge(out_done, b)
                        q = qq[b % 2][:, 2 * m:2 * m + 2, :].rearrange("p c t -> p (c t)")
                        pool.tensor_tensor(qn[:, 2 * m:2 * m + 2, :].rearrange("p c t -> p (c t)"), q,
                                           rec[m % 2][:, :], ALU.mult).then_inc(qn_done, 1)

            @block.vector
            def _(dve):
                nc.vector.memset(ones[:, :], 1.0)
                nc.vector.memset(eps[:, :], EPS)
                for h in range(2):
                    for other in range(2):
                        m = nc.vector.memset(mask[HD * h:HD * h + HD, HD * other:HD * other + HD], float(h == other))
                m.then_inc(const, 1)
                dve.wait_ge(const, 1)

                def elu(b, e):
                    if b >= B:
                        return
                    g = ELU * b + e
                    dve.wait_ge(elu_in, 2 * (g + 1))
                    if b >= 2 and e == 0:
                        dve.wait_ge(kvt_done, 2 * (b - 1))
                        dve.wait_ge(ks_done, b - 1)
                    if b >= 2 and e == 4:
                        dve.wait_ge(qn_done, 4 * (b - 1))
                        dve.wait_ge(den_done, 4 * (b - 1))
                    nc.vector.scalar_tensor_tensor(elu_target(b, e), ex[g % 2][:, :], 1.0, rl[g % 2][:, :],
                                                   ALU.min, ALU.add).then_inc(elu_done, 1)

                def keep_kv(b, h):
                    dve.wait_ge(kvt_done, 2 * b + h + 1)
                    if b >= 1:
                        dve.wait_ge(kvw_done, 2 * (b - 1) + h + 1)
                    nc.vector.tensor_tensor(kvT[:, 4 * h:4 * h + 4, :], kvt_ps[h][:, :, :],
                                            mask[:, :].unsqueeze(1).broadcast_to([P, 4, P]), ALU.mult).then_inc(kvt_kept, 1)

                def keep_key_sums(b):
                    dve.wait_ge(ks_done, b + 1)
                    if b >= 1:
                        dve.wait_ge(den_done, 4 * b)
                    nc.vector.tensor_tensor(ksm[:, :, :], mask[:, :].unsqueeze(1).broadcast_to([P, NC, P]),
                                            ks_ps.unsqueeze(2).broadcast_to([P, NC, P]), ALU.mult).then_inc(ks_kept, 1)

                def invert(b, m):
                    g = 4 * b + m
                    dve.wait_ge(eps_done, g + 1)
                    if g >= 2:
                        dve.wait_ge(qn_done, g - 1)
                    nc.vector.reciprocal(rec[g % 2][:, :], den[g % 2][:, :]).then_inc(rec_done, 1)

                def add(b):
                    dve.wait_ge(out_done, b + 1)
                    bout = ROWS["bout"][0]
                    x = n.xT[:, :].rearrange("p (t b) -> p b t", b=B)[:, b]
                    nc.vector.scalar_tensor_tensor(x, out_ps[:, 0:T], n.cols[:, bout:bout + 1], x,
                                                   ALU.add, ALU.add).then_inc(added, 1)

                for e in range(ELU):
                    elu(0, e)
                for b in range(B):
                    keep_kv(b, 0)
                    keep_kv(b, 1)
                    elu(b + 1, 0)
                    elu(b + 1, 1)
                    keep_key_sums(b)
                    elu(b + 1, 2)
                    elu(b + 1, 3)
                    invert(b, 0)
                    invert(b, 1)
                    elu(b + 1, 4)
                    invert(b, 2)
                    elu(b + 1, 5)
                    invert(b, 3)
                    elu(b + 1, 6)
                    elu(b + 1, 7)
                    add(b)


def gru_scan(nc, n, hist):
    G = 16
    GROUPS = T // G
    with ExitStack() as local:
        def sb(name, shape, dt=F32):
            return local.enter_context(nc.sbuf_tensor(name, shape, dt))

        def sem(name):
            return local.enter_context(nc.semaphore(name))

        pre_rz = [local.enter_context(nc.psum_tensor(f"pre_rz{i}", [P, 512], F32)) for i in range(2)]
        pre_n = [local.enter_context(nc.psum_tensor(f"pre_n{i}", [P, 512], F32)) for i in range(2)]
        rz = [sb(f"rz{i}", [P, 32]) for i in range(2)]
        narg = [sb(f"narg{i}", [P, 16]) for i in range(2)]
        keepz = [sb(f"keepz{i}", [P, 16]) for i in range(2)]
        mix = [sb(f"mix{i}", [P, 16]) for i in range(2)]
        const = sem("g_const"); inputs_in = sem("inputs_in"); rz_pre = sem("rz_pre"); n_pre = sem("n_pre")
        rz_done = sem("rz_done"); narg_done = sem("narg_done"); n_done = sem("n_done"); z_used = sem("z_used")
        state = sem("state")

        def rz_slot(s):
            return pre_rz[s // G % 2][:, 0:256].rearrange("p (s g b) -> p s g b", s=G, g=2)[:, s % G]

        def n_slot(s):
            return pre_n[s // G % 2][:, 16 * (s % G):16 * (s % G) + 16]

        def second(ap):
            return ap.rearrange("p (b two) -> p two b", two=2)[:, 1]

        def first(ap):
            return ap.rearrange("p (b two) -> p two b", two=2)[:, 0]

        def at_step(s):
            return hist[:, 16 * s:16 * s + 16]

        with nc.Block() as block:

            @block.tensor
            def _(pe):
                pe.wait_ge(n.load_later, 16 * 16)
                pe.wait_ge(const, 1)

                def inputs(g, i):
                    if g >= 2 and i == 0:
                        pe.wait_ge(state, G * (g - 1) + 1)
                    rzv = pre_rz[g % 2][:, 0:256].rearrange("p (s g b) -> p g s b", s=G, g=2)
                    nv = pre_n[g % 2][:, 0:256].rearrange("p (x two) -> p two x", two=2)
                    out = (rzv[:, 0], rzv[:, 0], rzv[:, 1], rzv[:, 1], nv[:, 1], nv[:, 1], nv[:, 0])[i]
                    if i in (1, 3, 5):
                        lhsT, rhs = n.gru_w[:, i // 2, :], n.xT[:, P * g:P * g + P]
                    else:
                        lhsT, rhs = n.gru_b[:, i // 2, :], n.ones_row[:, :]
                    if i < 4:
                        rhs = rhs.rearrange("p (s b) -> p s b", b=B)
                    mm = nc.tensor.matmul(out, lhsT, rhs, start=(i in (0, 4)), stop=False, skip_group_check=True)
                    if i == 6:
                        mm.then_inc(inputs_in, 1)

                for i in range(7):
                    inputs(0, i)
                for s in range(T):
                    h = second(at_step(s))
                    pe.wait_ge(state, s + 1)
                    for i in range(2):
                        mm = nc.tensor.matmul(rz_slot(s)[:, i], n.gru_w[:, 3 + i, :], h, start=False, stop=True,
                                              skip_group_check=True)
                    mm.then_inc(rz_pre, 1)
                    nc.tensor.matmul(first(n_slot(s)), n.gru_w[:, 5, :], h, start=False, stop=True,
                                     skip_group_check=True).then_inc(n_pre, 1)
                    g, i = s // G + 1, s % G - 4
                    if g < GROUPS and 0 <= i < 7:
                        inputs(g, i)

            @block.scalar
            def _(act):
                act.preload_act_table(ACT.Sigmoid)
                act.wait_ge(const, 1)
                for s in range(T):
                    act.wait_ge(rz_pre, s + 1)
                    out = rz[s % 2][:, :].rearrange("p (g b two) -> p g two b", g=2, two=2)[:, :, 1]
                    nc.scalar.activation(out, rz_slot(s), ACT.Sigmoid).then_inc(rz_done, 1)
                    act.wait_ge(narg_done, s + 1)
                    nc.scalar.activation(first(mix[s % 2][:, :]), second(narg[s % 2][:, :]), ACT.Tanh).then_inc(n_done, 1)

            @block.vector
            def _(dve):
                for i in range(2):
                    nc.vector.memset(rz[i][:, :], 0.0)
                    nc.vector.memset(keepz[i][:, :], 0.0)
                    last = nc.vector.memset(mix[i][:, :], 0.0)
                last.then_inc(const, 1)
                nc.vector.tensor_copy(second(at_step(0)), n.condT).then_inc(state, 1)
                dve.wait_ge(const, 1)
                dve.wait_ge(state, 1)
                for s in range(T):
                    p = s % 2
                    dve.wait_ge(rz_done, s + 1)
                    dve.wait_ge(n_pre, s + 1)
                    nc.vector.tensor_tensor_scan(narg[p][:, :], rz[p][:, 0:16], n_slot(s), 0.0,
                                                 ALU.mult, ALU.add).then_inc(narg_done, 1)
                    z = second(rz[p][:, 16:32])
                    nc.vector.tensor_scalar(second(keepz[p][:, :]), z, -1.0, 1.0, ALU.mult, ALU.add).then_inc(z_used, 1)
                    nc.vector.tensor_tensor(second(mix[p][:, :]), z, second(at_step(s)), ALU.mult).then_inc(z_used, 1)
                    dve.wait_ge(z_used, 2 * s + 2)
                    dve.wait_ge(n_done, s + 1)
                    nc.vector.tensor_tensor_scan(at_step(s + 1), keepz[p][:, :], mix[p][:, :], 0.0,
                                                 ALU.mult, ALU.add).then_inc(state, 1)


def route_top1(nc, n, hist, hB, take):
    with ExitStack() as local:
        def sb(name, shape, dt=F32):
            return local.enter_context(nc.sbuf_tensor(name, shape, dt))

        def sem(name):
            return local.enter_context(nc.semaphore(name))

        wide = [P, NBLK, E]
        score, prob, mark, chosen = (sb(k, wide) for k in ("r_score", "r_prob", "r_mark", "r_chosen"))
        top, total, inv, best, first = (sb(k, [P, NBLK]) for k in ("r_top", "r_total", "r_inv", "r_best", "r_first"))
        mine, rest1, rest2 = (sb(k, wide) for k in ("r_mine", "r_rest1", "r_rest2"))
        parts = sb("r_parts", [P, NBLK, 3, E], BF16)
        picks = sb("r_picks", [P, NBLK, 3, E], BF16)
        partsT = sb("r_partsT", [3 * E, TOK], BF16)
        picksT = sb("r_picksT", [3 * E, TOK], BF16)
        iota_m8 = sb("iota_m8", [P, E])
        before = sb("before", [P, P])
        junks = [sb(f"junk{i}", [P, TOK], BF16) for i in range(2)]
        counts = sb("r_counts", [P, 3, NBLK])
        rank, kept = sb("r_rank", [P, NBLK]), sb("r_kept", [P, NBLK])
        copied = sem("copied"); const = sem("r_const"); logits_in = sem("logits_in"); step = sem("r_step")
        exp_done = sem("r_exp"); turned = sem("r_turned"); turned_kept = sem("r_turned_kept")
        row_in = sem("row_in"); counted = sem("counted"); final = sem("r_final")

        with ExitStack() as early:
            logits = early.enter_context(nc.psum_tensor("logits", wide, F32))
            tp = early.enter_context(nc.psum_tensor("tp", [3 * E, TOK], BF16))
            tq = early.enter_context(nc.psum_tensor("tq", [3 * E, TOK], BF16))
            with nc.Block() as block:

                @block.gpsimd
                def _(pool):
                    pool.memset(before[:, :], 1.0).then_inc(const, 1)
                    pool.tensor_scalar(iota_m8[:, :], n.iota8[:, :], -float(E), None, ALU.add).then_inc(const, 1)
                    pool.wait_ge(const, 2)
                    pool.affine_select(out=before[:, :], in_=before[:, :], compare_op=ALU.is_gt, fill=0.0,
                                       base=0, pattern=[[-1, P]], channel_multiplier=1).then_inc(const, 1)

                @block.scalar
                def _(act):
                    states = hist[:, 16:].rearrange("p (t b two) -> p two b t", b=B, two=2)[:, 1]
                    for b in range(B):
                        nc.scalar.activation(hB[:, T * b:T * b + T], states[:, b], ACT.Copy).then_inc(copied, 1)
                    act.wait_ge(step, 2)
                    nc.scalar.activation(prob[:, :, :], score[:, :, :], ACT.Exp).then_inc(exp_done, 1)
                    act.wait_ge(turned, 1)
                    nc.scalar.activation(partsT[:, :], tp[:, :], ACT.Copy).then_inc(turned_kept, 1)

                @block.tensor
                def _(pe):
                    r0 = ROWS["router"][0]
                    for i in range(NBLK):
                        pe.wait_ge(copied, i // 2 + 1)
                        mm = nc.tensor.matmul(logits[:, i, :], hB[:, P * i:P * i + P], n.cols[:, r0:r0 + E],
                                              start=True, stop=True)
                    mm.then_inc(logits_in, 1)
                    pe.wait_ge(step, 18)
                    for src, dst in ((parts, tp), (picks, tq)):
                        for i in range(NBLK):
                            mm = nc.tensor.transpose(dst[:, P * i:P * i + P],
                                                     src[:, i, :, :].rearrange("p k e -> p (k e)"), n.identb[:, :])
                        mm.then_inc(turned, 1)

                @block.vector
                def _(dve):
                    at = [0]

                    def done(ins):
                        at[0] += 1
                        ins.then_inc(step, 1)
                        dve.wait_ge(step, at[0])

                    def per_token(ap):
                        return ap[:, :].unsqueeze(2).broadcast_to(wide)

                    V = nc.vector
                    dve.wait_ge(logits_in, 1)
                    done(V.tensor_reduce(top[:, :], logits[:, :, :], AX.X, ALU.max))
                    done(V.tensor_tensor(score[:, :, :], logits[:, :, :], per_token(top), ALU.subtract))
                    dve.wait_ge(exp_done, 1)
                    done(V.tensor_reduce(total[:, :], prob[:, :, :], AX.X, ALU.add))
                    done(V.reciprocal(inv[:, :], total[:, :]))
                    done(V.tensor_tensor(score[:, :, :], prob[:, :, :], per_token(inv), ALU.mult))
                    done(V.tensor_reduce(best[:, :], score[:, :, :], AX.X, ALU.max))
                    done(V.tensor_tensor(mark[:, :, :], score[:, :, :], per_token(best), ALU.is_equal))
                    dve.wait_ge(const, 3)
                    done(V.tensor_tensor(mark[:, :, :], mark[:, :, :], iota_m8[:, :].unsqueeze(1).broadcast_to(wide), ALU.mult))
                    done(V.tensor_reduce(first[:, :], mark[:, :, :], AX.X, ALU.min))
                    done(V.tensor_tensor(chosen[:, :, :], iota_m8[:, :].unsqueeze(1).broadcast_to(wide), per_token(first), ALU.is_equal))
                    done(V.tensor_tensor(mine[:, :, :], chosen[:, :, :], per_token(best), ALU.mult))
                    done(V.tensor_copy(parts[:, :, 0, :], mine[:, :, :]))
                    done(V.tensor_tensor(rest1[:, :, :], mine[:, :, :], parts[:, :, 0, :], ALU.subtract))
                    done(V.tensor_copy(parts[:, :, 1, :], rest1[:, :, :]))
                    done(V.tensor_tensor(rest2[:, :, :], rest1[:, :, :], parts[:, :, 1, :], ALU.subtract))
                    V.tensor_copy(parts[:, :, 2, :], rest2[:, :, :])
                    for k in range(3):
                        last = V.tensor_copy(picks[:, :, k, :], chosen[:, :, :])
                        if k:
                            done(last)
                    done(V.memset(counts[:, :, :], 0.0))
                    dve.wait_ge(turned, 2)
                    V.tensor_copy(picksT[:, :], tq[:, :]).then_inc(turned_kept, 1)

        rows = [local.enter_context(nc.psum_tensor(f"rows{i}", [P, TOK], F32)) for i in range(2)]
        with nc.Block() as block:

            @block.tensor
            def _(pe):
                for i in range(NBLK):
                    if i >= 2:
                        pe.wait_ge(counted, i - 1)
                    for m in range(TOK // 512):
                        mm = nc.tensor.matmul(rows[i % 2][:, 512 * m:512 * m + 512], picksT[:, P * i:P * i + P],
                                              partsT[:, 512 * m:512 * m + 512], start=True, stop=True)
                    mm.then_inc(row_in, 1)

            @block.vector
            def _(dve):
                V = nc.vector
                for i in range(NBLK):
                    p = best[:, i:i + 1]
                    row = rows[i % 2]
                    junk = junks[i % 2]
                    dve.wait_ge(row_in, i + 1)
                    if i >= 2:
                        dve.wait_ge(counted, i - 1)
                    if i:
                        V.tensor_scalar(junk[:, 0:P * i], row[:, 0:P * i], p, None, ALU.is_ge, ALU.add,
                                        accum_out=counts[:, 0, i:i + 1])
                    V.scalar_tensor_tensor(junk[:, P * i:P * i + P], row[:, P * i:P * i + P], p, before[:, :],
                                           ALU.is_equal, ALU.mult, accum_out=counts[:, 1, i:i + 1]).then_inc(final, 1)
                    dve.wait_ge(final, i + 1)
                    V.tensor_scalar(junk[:, P * i:TOK], row[:, P * i:TOK], p, None, ALU.is_gt, ALU.add,
                                    accum_out=counts[:, 2, i:i + 1]).then_inc(counted, 1)
                dve.wait_ge(counted, NBLK)
                V.tensor_reduce(rank[:, :], counts[:, :, :].rearrange("p k i -> p i k"), AX.X, ALU.add).then_inc(final, 1)
                dve.wait_ge(final, NBLK + 1)
                V.tensor_scalar(kept[:, :], rank[:, :], float(CAPACITY), None, ALU.is_lt).then_inc(final, 1)
                dve.wait_ge(final, NBLK + 2)
                V.tensor_tensor(take[:, :, :], chosen[:, :, :], kept[:, :].unsqueeze(2).broadcast_to(wide), ALU.mult).then_inc(final, 1)
                V.tensor_scalar(rank[:, :], kept[:, :], -1.0, 1.0, ALU.mult, ALU.add).then_inc(final, 1)
                dve.wait_ge(final, NBLK + 4)
                V.tensor_tensor(take[:, :, 0], take[:, :, 0], rank[:, :], ALU.add).then_inc(final, 1)


def experts(nc, n, layer, inB, weight, w_in, w_out, out):
    TILE = 512
    TB = TILE // P
    TILES = TOK // TILE
    gated = layer == 1
    UP = 2 if gated else 1
    UNITS = TILES * E
    with ExitStack() as local:
        def sb(name, shape, dt=F32):
            return local.enter_context(nc.sbuf_tensor(f"{name}_{layer}", shape, dt))

        def ps(name, shape, dt=F32):
            return local.enter_context(nc.psum_tensor(f"{name}_{layer}", shape, dt))

        def sem(name):
            return local.enter_context(nc.semaphore(f"{name}_{layer}"))

        hid = [sb(f"hid{i}", [P, NF, TILE]) for i in range(2)]
        acc = [sb(f"acc{i}", [P, TB, D]) for i in range(2)]
        takeT = sb("takeT", [E, TILE])
        gate = [sb(f"gate{i}", [P, TILE]) for i in range(2)]
        h_ps = [ps(f"h_ps{i}", [P, TILE]) for i in range(4)]
        y_ps = [ps(f"y_ps{i}", [P, TB, D]) for i in range(2)]
        x_ps = ps("x_ps", [P, TILE])
        t_ps = ps("t_ps", [E, TILE])
        h_in = sem("h_in"); gate_done = sem("gate_done"); h_done = sem("h_done"); y_in = sem("y_in"); summed = sem("summed")
        take_in = sem("take_in"); take_kept = sem("take_kept"); bias_in = sem("bias_in"); acc_set = sem("acc_set")
        x_in = sem("x_in"); x_added = sem("x_added"); stored = sem("stored")

        with nc.Block() as block:

            @block.tensor
            def _(pe):
                def hidden(v):
                    t, e = divmod(v, E)
                    for f in range(NF):
                        for k in range(UP):
                            g = (v * NF + f) * UP + k
                            if g >= 4:
                                pe.wait_ge(h_done, (g - 4) // UP + 1)
                            mm = nc.tensor.matmul(h_ps[g % 4][:, :], w_in[k][:, e, P * f:P * f + P],
                                                  inB[:, TILE * t:TILE * t + TILE], start=True, stop=True)
                            mm.then_inc(h_in, 1)

                def output(v):
                    t, e = divmod(v, E)
                    if v >= 2:
                        pe.wait_ge(summed, TB * (v - 1))
                    pe.wait_ge(h_done, NF * (v + 1))
                    for i in range(TB):
                        for f in range(NF):
                            mm = nc.tensor.matmul(y_ps[v % 2][:, i, :], hid[v % 2][:, f, P * i:P * i + P],
                                                  w_out[:, e, f, :], start=(f == 0), stop=(f == NF - 1))
                    mm.then_inc(y_in, 1)

                def bias(t):
                    if t:
                        pe.wait_ge(take_kept, t)
                    for i in range(TB):
                        mm = nc.tensor.transpose(t_ps[:, P * i:P * i + P], weight[:, TB * t + i, :], n.ident[:, :])
                    mm.then_inc(take_in, 1)
                    pe.wait_ge(take_kept, t + 1)
                    if t:
                        pe.wait_ge(x_added, t)
                    for i in range(TB):
                        mm = nc.tensor.matmul(x_ps[:, P * i:P * i + P], takeT[:, P * i:P * i + P], n.b2[:, :],
                                              start=True, stop=True)
                    mm.then_inc(bias_in, 1)

                def turn(t):
                    if gated:
                        if t:
                            pe.wait_ge(x_added, t)
                        for i in range(TB):
                            b, s = divmod(TB * t + i, T // P)
                            x = n.xT[:, :].rearrange("p (t b) -> p b t", b=B)[:, b, P * s:P * s + P]
                            mm = nc.tensor.transpose(x_ps[:, P * i:P * i + P], x, n.ident[:, :])
                    else:
                        pe.wait_ge(summed, TB * E * (t + 1))
                        pe.wait_ge(acc_set, t + 1)
                        for i in range(TB):
                            mm = nc.tensor.transpose(x_ps[:, P * i:P * i + P], acc[t % 2][:, i, :], n.ident[:, :])
                    mm.then_inc(x_in, 1)

                if not gated:
                    pe.wait_ge(n.load_experts, 32)
                hidden(0)
                for v in range(UNITS):
                    t, e = divmod(v, E)
                    if e == 0 and gated:
                        turn(t)
                    if v + 1 < UNITS:
                        hidden(v + 1)
                    if e == 0 and not gated:
                        bias(t)
                    output(v)
                    if e == 7 and not gated:
                        turn(t)

            @block.scalar
            def _(act):
                b10 = ROWS["b1"][0]
                for v in range(UNITS):
                    t, e = divmod(v, E)
                    for f in range(NF):
                        g = v * NF + f
                        if gated:
                            act.wait_ge(h_in, 2 * g + 1)
                            if g >= 2:
                                act.wait_ge(h_done, g - 1)
                            nc.scalar.activation(gate[g % 2][:, :], h_ps[2 * g % 4][:, :], ACT.Silu).then_inc(gate_done, 1)
                        else:
                            act.wait_ge(h_in, g + 1)
                            if v >= 2:
                                act.wait_ge(y_in, v - 1)
                            nc.scalar.activation(hid[v % 2][:, f, :], h_ps[g % 4][:, :], ACT.Relu,
                                                 bias=n.cols[:, b10 + NF * e + f:b10 + NF * e + f + 1]).then_inc(h_done, 1)
                    if e == 0 and not gated:
                        act.wait_ge(take_in, t + 1)
                        nc.scalar.activation(takeT[:, :], t_ps[:, :], ACT.Copy).then_inc(take_kept, 1)
                        act.wait_ge(bias_in, t + 1)
                        if t >= 2:
                            act.wait_ge(x_in, t - 1)
                        nc.scalar.activation(acc[t % 2][:, :, :].rearrange("p i d -> p (i d)"), x_ps[:, :],
                                             ACT.Copy).then_inc(acc_set, 1)

            @block.vector
            def _(dve):
                for v in range(UNITS + 1):
                    if gated and v < UNITS:
                        t, e = divmod(v, E)
                        if v >= 2:
                            dve.wait_ge(y_in, v - 1)
                        for f in range(NF):
                            g = v * NF + f
                            dve.wait_ge(gate_done, g + 1)
                            dve.wait_ge(h_in, 2 * g + 2)
                            nc.vector.tensor_tensor(hid[v % 2][:, f, :], gate[g % 2][:, :], h_ps[(2 * g + 1) % 4][:, :],
                                                    ALU.mult).then_inc(h_done, 1)
                        if e == 0:
                            dve.wait_ge(x_in, t + 1)
                            if t >= 2:
                                dve.wait_ge(stored, 16 * (t - 1))
                            nc.vector.tensor_copy(acc[t % 2][:, :, :].rearrange("p i d -> p (i d)"),
                                                  x_ps[:, :]).then_inc(x_added, 1)
                    if v == 0:
                        continue
                    w = v - 1
                    t, e = divmod(w, E)
                    dve.wait_ge(y_in, w + 1)
                    dve.wait_ge(x_added if gated else acc_set, t + 1)
                    if e:
                        dve.wait_ge(summed, TB * w)
                    for i in range(TB):
                        nc.vector.scalar_tensor_tensor(acc[t % 2][:, i, :], y_ps[w % 2][:, i, :],
                                                       weight[:, TB * t + i, e:e + 1], acc[t % 2][:, i, :],
                                                       ALU.mult, ALU.add).then_inc(summed, 1)
                    if e == E - 1 and not gated:
                        dve.wait_ge(x_in, t + 1)
                        x = n.xT[:, :].rearrange("p (t b) -> p b t", b=B)[:, 2 * t:2 * t + 2]
                        nc.vector.tensor_tensor(x, x_ps[:, :].rearrange("p (b t) -> p b t", b=2), x, ALU.add).then_inc(x_added, 1)

            @block.sync
            def _(sp):
                if gated:
                    for t in range(TILES):
                        sp.wait_ge(summed, TB * E * (t + 1))
                        dst = out.rearrange("b (s p) d -> p (b s) d", p=P)[:, TB * t:TB * t + TB]
                        sp.dma_start(dst, acc[t % 2][:, :, :]).then_inc(stored, 16)
                    sp.wait_ge(stored, 16 * TILES)


def gate_scan(nc, n, s2):
    G = 64
    with ExitStack() as local:
        def sb(name, shape, dt=F32):
            return local.enter_context(nc.sbuf_tensor(name, shape, dt))

        def sem(name):
            return local.enter_context(nc.semaphore(name))

        wT = sb("wT", [P, 2, D])
        leak = sb("leak", [P, 1])
        pairs = sb("pairs", [P, 16 * T])
        gates = [sb(f"gates{i}", [P, 16]) for i in range(2)]
        targ = [sb(f"targ{i}", [P, 16]) for i in range(2)]
        pre = [local.enter_context(nc.psum_tensor(f"s_pre{i}", [P, 512], F32)) for i in range(2)]
        w_ps = local.enter_context(nc.psum_tensor("w_ps", [P, 2, D], F32))
        turned = sem("s_turned"); w_kept = sem("w_kept"); const = sem("s_const"); z_in = sem("z_in")
        inputs_in = sem("s_inputs"); pre_in = sem("s_pre_in"); gate_done = sem("s_gate"); leaked = sem("leaked")
        arg_done = sem("s_arg"); state = sem("s_state")

        def second(ap):
            return ap.rearrange("p (b two) -> p two b", two=2)[:, 1]

        with nc.Block() as block:

            @block.gpsimd
            def _(pool):
                for q in range(4):
                    w = TOK // 4
                    out = pairs[:, 2 * w * q:2 * w * (q + 1)].rearrange("p (x two) -> p two x", two=2)[:, 0]
                    pool.tensor_copy(out, n.xT[:, w * q:w * q + w]).then_inc(z_in, 1)

            @block.tensor
            def _(pe):
                for i in range(2):
                    mm = nc.tensor.transpose(w_ps[:, i, :], n.l1w[:, D * i:D * i + D], n.ident[:, :])
                mm.then_inc(turned, 1)
                pe.wait_ge(w_kept, 1)

                def inputs(g):
                    if g >= 2:
                        pe.wait_ge(state, G * (g - 1) + 1)
                    nc.tensor.matmul(pre[g % 2][:, :], wT[:, 1, :], n.xT[:, 512 * g:512 * g + 512], start=True, stop=False,
                                     skip_group_check=True)

                inputs(0)
                for s in range(T):
                    pe.wait_ge(state, s + 1)
                    nc.tensor.matmul(pre[s // G % 2][:, 8 * (s % G):8 * (s % G) + 8], wT[:, 0, :], s2[:, 8 * s:8 * s + 8],
                                     start=False, stop=True, skip_group_check=True).then_inc(pre_in, 1)
                    if s % G == 4 and s // G + 1 < T // G:
                        inputs(s // G + 1)

            @block.scalar
            def _(act):
                act.wait_ge(turned, 1)
                act.preload_act_table(ACT.Sigmoid)
                nc.scalar.activation(wT[:, :, :], w_ps[:, :, :], ACT.Copy).then_inc(w_kept, 1)
                act.wait_ge(const, 1)
                bl = ROWS["b_l1"][0]
                for s in range(T):
                    act.wait_ge(pre_in, s + 1)
                    nc.scalar.activation(second(gates[s % 2][:, :]), pre[s // G % 2][:, 8 * (s % G):8 * (s % G) + 8],
                                         ACT.Sigmoid, bias=n.cols[:, bl:bl + 1]).then_inc(gate_done, 1)
                    act.wait_ge(arg_done, s + 1)
                    nc.scalar.activation(s2[:, 8 * s + 8:8 * s + 16], second(targ[s % 2][:, :]), ACT.Tanh).then_inc(state, 1)

            @block.vector
            def _(dve):
                al = ROWS["alpha"][0]
                for i in range(2):
                    nc.vector.memset(gates[i][:, :], 0.0)
                nc.vector.tensor_scalar(leak[:, :], n.cols[:, al:al + 1], -1.0, 1.0, ALU.mult, ALU.add).then_inc(const, 1)
                nc.vector.tensor_copy(s2[:, 0:8], n.condT).then_inc(state, 1)
                dve.wait_ge(const, 1)
                for s in range(T):
                    if s % G == 0:
                        dve.wait_ge(z_in, s // G + 1)
                    dve.wait_ge(state, s + 1)
                    pair = pairs[:, 16 * s:16 * s + 16]
                    nc.vector.tensor_scalar(second(pair), s2[:, 8 * s:8 * s + 8], leak[:, 0:1], None, ALU.mult).then_inc(leaked, 1)
                    dve.wait_ge(leaked, s + 1)
                    dve.wait_ge(gate_done, s + 1)
                    nc.vector.tensor_tensor_scan(targ[s % 2][:, :], gates[s % 2][:, :], pair, 0.0,
                                                 ALU.mult, ALU.add).then_inc(arg_done, 1)


def diff_attention(nc, n, s2):
    SCALE = float(D) ** -0.25
    EPS, LAMBDA_INIT = 1e-5, 0.8
    SEG = T // P
    UNITS = B * SEG
    with ExitStack() as local:
        def sb(name, shape, dt=F32):
            return local.enter_context(nc.sbuf_tensor(name, shape, dt))

        def ps(name, shape):
            return local.enter_context(nc.psum_tensor(name, shape, F32))

        def sem(name):
            return local.enter_context(nc.semaphore(name))

        sB = sb("sB", [P, TOK])
        qk = sb("qk", [P, 4, TOK])
        vt = sb("vt", [P, UNITS, D])
        lam2 = sb("lam2", [P, 2]); lam = sb("lam", [P, 1]); lq = sb("lq", [P, 2, P])
        negmax = [sb(f"negmax{i}", [P, 2]) for i in range(2)]
        sums = [sb(f"sums{i}", [P, 2]) for i in range(2)]
        inv = [sb(f"inv{i}", [P, 2]) for i in range(2)]
        probs = [sb(f"probs{i}", [P, 2, T]) for i in range(2)]
        diff = [sb(f"diff{i}", [P, T]) for i in range(2)]
        diffT = [sb(f"diffT{i}", [P, SEG, P]) for i in range(2)]
        heads = sb("heads", [P, UNITS, D])
        junk = sb("d_junk", [P, D])
        squares = sb("squares", [P, UNITS])
        rms = sb("rms", [P, UNITS]); unit = sb("unit", [P, UNITS]); eps = sb("d_eps", [P, 1])
        pj = [ps(f"dpj{i}", [P, 512]) for i in range(2)]
        s_ps = [ps(f"s_ps{i}", [P, 2, T]) for i in range(2)]
        t_ps = [ps(f"dt_ps{i}", [P, SEG, P]) for i in range(2)]
        o_ps = [ps(f"o_ps{i}", [P, D]) for i in range(2)]
        copied = sem("d_copied"); pj_in = sem("d_pj_in"); pj_kept = sem("d_pj_kept"); pre = sem("d_pre")
        lam_in = sem("lam_in"); lam_exp = sem("lam_exp"); lam_done = sem("lam_done")
        s_in = sem("d_s"); max_done = sem("d_max"); exp_done = sem("d_exp"); link = sem("d_link"); diff_done = sem("d_diff")
        t_in = sem("d_t"); t_kept = sem("d_t_kept"); o_in = sem("d_o"); o_kept = sem("d_o_kept"); sq_done = sem("d_sq")
        rms_done = sem("d_rms"); unit_done = sem("d_unit"); normed = sem("d_normed"); back_in = sem("d_back"); added = sem("d_added")

        with nc.Block() as block:

            @block.tensor
            def _(pe):
                pe.wait_ge(pre, 1)
                for i, row in enumerate(("lk1", "lk2")):
                    r0 = ROWS[row][0]
                    mm = nc.tensor.matmul(o_ps[0][:, i:i + 1], lq[:, i, :], n.cols[:, r0:r0 + 1], start=True, stop=True)
                mm.then_inc(lam_in, 1)
                g = 0
                pe.wait_ge(copied, B)
                for m in range(TOK // 512):
                    for i, w in enumerate((n.wq12, n.wq12, n.wk12, n.wk12)):
                        if g >= 2:
                            pe.wait_ge(pj_kept, g - 1)
                        nc.tensor.matmul(pj[g % 2][:, :], w[:, D * (i % 2):D * (i % 2) + D], sB[:, 512 * m:512 * m + 512],
                                         start=True, stop=True).then_inc(pj_in, 1)
                        g += 1
                for m in range(4):
                    pe.wait_ge(pj_kept, g - 1)
                    for i in range(4):
                        at = P * (4 * m + i)
                        mm = nc.tensor.matmul(pj[g % 2][:, P * i:P * i + P], sB[:, at:at + P], n.wv1[:, :], start=True, stop=True)
                    mm.then_inc(pj_in, 1)
                    g += 1
                pe.wait_ge(pj_kept, g)

                def scores(u):
                    b, i = divmod(u, SEG)
                    if u >= 2:
                        pe.wait_ge(exp_done, 2 * (u - 1))
                    for m in range(2):
                        mm = nc.tensor.matmul(s_ps[u % 2][:, m, :], qk[:, m, P * u:P * u + P],
                                              qk[:, 2 + m, T * b:T * b + T], start=True, stop=True)
                    mm.then_inc(s_in, 1)

                def turn(u):
                    pe.wait_ge(diff_done, u + 1)
                    if u >= 2:
                        pe.wait_ge(t_kept, u - 1)
                    for i in range(SEG):
                        mm = nc.tensor.transpose(t_ps[u % 2][:, i, :], diff[u % 2][:, P * i:P * i + P], n.ident[:, :])
                    mm.then_inc(t_in, 1)

                def attend(u):
                    pe.wait_ge(t_kept, u + 1)
                    if u >= 2:
                        pe.wait_ge(o_kept, u - 1)
                        pe.wait_ge(sq_done, u - 1)
                    for i in range(SEG):
                        mm = nc.tensor.matmul(o_ps[u % 2][:, :], diffT[u % 2][:, i, :], vt[:, u // SEG * SEG + i, :],
                                              start=(i == 0), stop=(i == SEG - 1))
                    mm.then_inc(o_in, 1)

                pe.wait_ge(lam_exp, 1)
                scores(0)
                scores(1)
                for u in range(UNITS + 1):
                    if u >= 1:
                        attend(u - 1)
                    if u < UNITS:
                        if u + 2 < UNITS and u >= 0:
                            pass
                        turn(u)
                        if u + 2 < UNITS:
                            scores(u + 2)
                for g in range(4):
                    pe.wait_ge(normed, 4 * (g + 1))
                    if g >= 2:
                        pe.wait_ge(added, g - 1)
                    for i in range(4):
                        mm = nc.tensor.transpose(pj[g % 2][:, P * i:P * i + P], heads[:, 4 * g + i, :], n.ident[:, :])
                    mm.then_inc(back_in, 1)

            @block.scalar
            def _(act):
                src = s2[:, 8:].rearrange("p (t b) -> p b t", b=B)
                for b in range(B):
                    nc.scalar.activation(sB[:, T * b:T * b + T], src[:, b], ACT.Copy).then_inc(copied, 1)
                act.wait_ge(lam_in, 1)
                nc.scalar.activation(lam2[:, :], o_ps[0][:, 0:2], ACT.Exp).then_inc(lam_exp, 1)
                for g in range(20):
                    act.wait_ge(pj_in, g + 1)
                    if g < 16:
                        out = qk[:, g % 4, 512 * (g // 4):512 * (g // 4) + 512]
                    else:
                        out = vt[:, 4 * (g - 16):4 * (g - 16) + 4, :].rearrange("p i d -> p (i d)")
                    nc.scalar.activation(out, pj[g % 2][:, :], ACT.Copy).then_inc(pj_kept, 1)

                def exps(u):
                    act.wait_ge(max_done, u + 1)
                    if u >= 2:
                        act.wait_ge(diff_done, u - 1)
                    for m in range(2):
                        nc.scalar.activation(probs[u % 2][:, m, :], s_ps[u % 2][:, m, :], ACT.Exp,
                                             bias=negmax[u % 2][:, m:m + 1], scale=SCALE,
                                             accum_out=sums[u % 2][:, m:m + 1]).then_inc(exp_done, 1)

                def keep(u):
                    act.wait_ge(t_in, u + 1)
                    if u >= 2:
                        act.wait_ge(o_in, u - 1)
                    nc.scalar.activation(diffT[u % 2][:, :, :], t_ps[u % 2][:, :, :], ACT.Copy).then_inc(t_kept, 1)

                exps(0)
                for u in range(UNITS):
                    if u + 1 < UNITS:
                        exps(u + 1)
                    keep(u)
                    if u >= 1:
                        act.wait_ge(o_kept, u)
                        if u >= 2:
                            act.wait_ge(sq_done, u - 1)
                        nc.scalar.activation(junk[:, :], heads[:, u - 1, :], ACT.Square,
                                             accum_out=squares[:, u - 1:u]).then_inc(sq_done, 1)
                act.wait_ge(o_kept, UNITS)
                act.wait_ge(sq_done, UNITS - 1)
                nc.scalar.activation(junk[:, :], heads[:, UNITS - 1, :], ACT.Square,
                                     accum_out=squares[:, UNITS - 1:UNITS]).then_inc(sq_done, 1)
                act.wait_ge(sq_done, UNITS)
                nc.scalar.activation(rms[:, :], squares[:, :], ACT.Sqrt, bias=eps[:, 0:1], scale=1.0 / D).then_inc(rms_done, 1)

            @block.vector
            def _(dve):
                V = nc.vector
                for i, row in enumerate(("lq1", "lq2")):
                    r0 = ROWS[row][0]
                    last = V.tensor_copy(lq[:, i, :], n.cols[:, r0:r0 + 1].broadcast_to([P, P]))
                last.then_inc(pre, 1)
                V.memset(eps[:, :], EPS)
                dve.wait_ge(lam_exp, 1)
                V.tensor_tensor(lam[:, :], lam2[:, 1:2], lam2[:, 0:1], ALU.subtract).then_inc(lam_done, 1)
                dve.wait_ge(lam_done, 1)
                V.tensor_scalar(lam[:, :], lam[:, :], -LAMBDA_INIT, None, ALU.add).then_inc(lam_done, 1)
                dve.wait_ge(lam_done, 2)

                def maxima(u):
                    dve.wait_ge(s_in, u + 1)
                    if u >= 2:
                        dve.wait_ge(exp_done, 2 * (u - 1))
                    V.tensor_reduce(negmax[u % 2][:, :], s_ps[u % 2][:, :, :], AX.X, ALU.max).then_inc(link, 1)
                    dve.wait_ge(link, u + 1)
                    V.tensor_scalar(negmax[u % 2][:, :], negmax[u % 2][:, :], -SCALE, None, ALU.mult).then_inc(max_done, 1)

                def difference(u):
                    p = u % 2
                    dve.wait_ge(exp_done, 2 * (u + 1))
                    V.reciprocal(inv[p][:, :], sums[p][:, :]).then_inc(unit_done, 1)
                    dve.wait_ge(unit_done, 3 * u + 1)
                    V.tensor_tensor(inv[p][:, 1:2], inv[p][:, 1:2], lam[:, :], ALU.mult).then_inc(unit_done, 1)
                    if u >= 2:
                        dve.wait_ge(t_in, u - 1)
                    dve.wait_ge(unit_done, 3 * u + 2)
                    V.tensor_scalar(diff[p][:, :], probs[p][:, 0, :], inv[p][:, 0:1], None, ALU.mult).then_inc(unit_done, 1)
                    dve.wait_ge(unit_done, 3 * u + 3)
                    V.scalar_tensor_tensor(diff[p][:, :], probs[p][:, 1, :], inv[p][:, 1:2], diff[p][:, :],
                                           ALU.mult, ALU.add).then_inc(diff_done, 1)

                def keep(u):
                    dve.wait_ge(o_in, u + 1)
                    V.tensor_copy(heads[:, u, :], o_ps[u % 2][:, :]).then_inc(o_kept, 1)

                maxima(0)
                for u in range(UNITS):
                    if u + 1 < UNITS:
                        maxima(u + 1)
                    difference(u)
                    if u >= 1:
                        keep(u - 1)
                keep(UNITS - 1)
                dve.wait_ge(rms_done, 1)
                V.reciprocal(unit[:, :], rms[:, :]).then_inc(link, 1)
                dve.wait_ge(link, UNITS + 1)
                for u in range(UNITS):
                    V.tensor_scalar(heads[:, u, :], heads[:, u, :], unit[:, u:u + 1], 1.0 - LAMBDA_INIT,
                                    ALU.mult, ALU.mult).then_inc(normed, 1)
                for g in range(4):
                    dve.wait_ge(back_in, g + 1)
                    x = n.xT[:, :].rearrange("p (t b) -> p b t", b=B)[:, 2 * g:2 * g + 2]
                    V.tensor_tensor(x, pj[g % 2][:, :].rearrange("p (b t) -> p b t", b=2), x, ALU.add).then_inc(added, 1)


def modulated_linear(nc, n, mB, comb):
    EPS = 1e-8
    SCALE = float(D) ** -0.5
    wide = [P, NBLK, E]
    with ExitStack() as local:
        def sb(name, shape, dt=F32):
            return local.enter_context(nc.sbuf_tensor(name, shape, dt))

        def sem(name):
            return local.enter_context(nc.semaphore(name))

        ys, ys2 = sb("ys", [P, B]), sb("ys2", [P, B])
        w2, eps, dd, dr = sb("w2", [P, D]), sb("m_eps", [P, 1]), sb("dd", [P, B]), sb("dr", [P, B])
        xs = sb("xs", [P, TOK])
        val, mark, one, two = (sb(k, wide) for k in ("m_val", "m_mark", "m_one", "m_two"))
        v1, v2, first, pa, pb = (sb(k, [P, NBLK]) for k in ("m_v1", "m_v2", "m_first", "m_pa", "m_pb"))
        iota_m8 = sb("m_iota", [P, E])
        d_ps = local.enter_context(nc.psum_tensor("d_ps", [P, B], F32))
        m_ps = [local.enter_context(nc.psum_tensor(f"m_ps{i}", [P, 512], F32)) for i in range(2)]
        g_ps = local.enter_context(nc.psum_tensor("g_ps", wide, F32))
        step = sem("m_step"); d_in = sem("m_d"); sq = sem("m_sq"); lin = sem("m_lin"); kept = sem("m_kept"); gates_in = sem("m_gates")
        exp_in = sem("m_exp")

        with nc.Block() as block:

            @block.tensor
            def _(pe):
                pe.wait_ge(step, 5)
                nc.tensor.matmul(d_ps[:, :], w2[:, :], ys2[:, :], start=True, stop=True).then_inc(d_in, 1)
                pe.wait_ge(step, 6)
                for g in range(4):
                    if g >= 2:
                        pe.wait_ge(kept, g - 1)
                    nc.tensor.matmul(m_ps[g % 2][:, :], n.wmod[:, :], xs[:, 512 * g:512 * g + 512], start=True, stop=True).then_inc(lin, 1)
                g0 = ROWS["gate"][0]
                pe.wait_ge(kept, 4)
                for i in range(NBLK):
                    mm = nc.tensor.matmul(g_ps[:, i, :], mB[:, P * i:P * i + P], n.cols[:, g0:g0 + E], start=True, stop=True)
                mm.then_inc(gates_in, 1)

            @block.scalar
            def _(act):
                act.wait_ge(d_in, 1)
                nc.scalar.activation(dd[:, :], d_ps[:, :], ACT.Sqrt, bias=eps[:, 0:1]).then_inc(sq, 1)
                act.wait_ge(exp_in, 1)
                nc.scalar.activation(pb[:, :], pa[:, :], ACT.Exp).then_inc(sq, 1)

            @block.vector
            def _(dve):
                V = nc.vector
                at = [0]

                def done(ins):
                    at[0] += 1
                    ins.then_inc(step, 1)
                    dve.wait_ge(step, at[0])

                def per_token(ap):
                    return ap[:, :].unsqueeze(2).broadcast_to(wide)

                done(V.memset(eps[:, :], EPS))
                done(V.tensor_scalar(iota_m8[:, :], n.iota8[:, :], -float(E), None, ALU.add))
                done(V.tensor_scalar(ys[:, :], n.condT, SCALE, None, ALU.mult))
                done(V.tensor_tensor(ys2[:, :], ys[:, :], ys[:, :], ALU.mult))
                done(V.tensor_tensor(w2[:, :], n.wmod[:, :], n.wmod[:, :], ALU.mult))
                steps = [P, T, B]
                done(V.tensor_tensor(xs[:, :].rearrange("p (t b) -> p t b", b=B), n.xT[:, :].rearrange("p (t b) -> p t b", b=B),
                                     ys[:, :].unsqueeze(1).broadcast_to(steps), ALU.mult))
                dve.wait_ge(sq, 1)
                done(V.reciprocal(dr[:, :], dd[:, :]))
                for g in range(4):
                    dve.wait_ge(lin, g + 1)
                    w = 512 // B
                    out = mB[:, :].rearrange("p (b t) -> p t b", b=B)[:, w * g:w * g + w]
                    V.tensor_tensor(out, m_ps[g % 2][:, :].rearrange("p (t b) -> p t b", b=B),
                                    dr[:, :].unsqueeze(1).broadcast_to([P, w, B]), ALU.mult).then_inc(kept, 1)
                dve.wait_ge(gates_in, 1)
                ramp = iota_m8[:, :].unsqueeze(1).broadcast_to(wide)
                done(V.tensor_copy(val[:, :, :], g_ps[:, :, :]))

                def take_largest(top, onehot):
                    done(V.tensor_reduce(top[:, :], val[:, :, :], AX.X, ALU.max))
                    done(V.tensor_tensor(mark[:, :, :], val[:, :, :], per_token(top), ALU.is_equal))
                    done(V.tensor_tensor(mark[:, :, :], mark[:, :, :], ramp, ALU.mult))
                    done(V.tensor_reduce(first[:, :], mark[:, :, :], AX.X, ALU.min))
                    done(V.tensor_tensor(onehot[:, :, :], ramp, per_token(first), ALU.is_equal))

                take_largest(v1, one)
                done(V.scalar_tensor_tensor(val[:, :, :].rearrange("p i e -> p (i e)"),
                                            one[:, :, :].rearrange("p i e -> p (i e)"), -3.0e38,
                                            val[:, :, :].rearrange("p i e -> p (i e)"), ALU.mult, ALU.add))
                take_largest(v2, two)
                V.tensor_tensor(pa[:, :], v2[:, :], v1[:, :], ALU.subtract).then_inc(exp_in, 1)
                dve.wait_ge(sq, 2)
                done(V.tensor_scalar(v1[:, :], pb[:, :], 1.0, None, ALU.add))
                done(V.reciprocal(pa[:, :], v1[:, :]))
                done(V.tensor_tensor(pb[:, :], pb[:, :], pa[:, :], ALU.mult))
                done(V.tensor_tensor(one[:, :, :], one[:, :, :], per_token(pa), ALU.mult))
                done(V.tensor_tensor(two[:, :, :], two[:, :, :], per_token(pb), ALU.mult))
                done(V.tensor_tensor(comb[:, :, :], one[:, :, :], two[:, :, :], ALU.add))


def turn_weights(nc, n, a, wgT, wuT, wdT):
    KINDS = (("L1_ffn_wg", wgT), ("L1_ffn_wu", wuT), ("L1_ffn_wd", wdT))
    with ExitStack() as local:
        def sem(name):
            return local.enter_context(nc.semaphore(name))

        raw = [local.enter_context(nc.sbuf_tensor(f"raw{i}", [P, NF, P], F32)) for i in range(4)]
        tps = [local.enter_context(nc.psum_tensor(f"tps{i}", [P, NF, P], F32)) for i in range(4)]
        ld = [sem(f"raw_in{i}") for i in range(4)]
        turned = sem("w_turned"); kept = sem("wt_kept")
        jobs = [(key, dst, e) for key, dst in KINDS for e in range(E)]

        with nc.Block() as block:

            @block.sync
            def _(sp):
                for j, (key, dst, e) in enumerate(jobs):
                    if j >= 4:
                        sp.wait_ge(turned, j - 3)
                    src = a[key][e]
                    src = src.rearrange("(f p) h -> p f h", p=P) if dst is not wdT else src.rearrange("h (f i) -> h f i", i=P)
                    sp.dma_start(raw[j % 4][:, :, :], src).then_inc(ld[j % 4], 16)

            @block.tensor
            def _(pe):
                for j in range(len(jobs)):
                    pe.wait_ge(ld[j % 4], 16 * (j // 4 + 1))
                    if j >= 4:
                        pe.wait_ge(kept, j - 3)
                    for f in range(NF):
                        mm = nc.tensor.transpose(tps[j % 4][:, f, :], raw[j % 4][:, f, :], n.ident[:, :])
                    mm.then_inc(turned, 1)

            @block.scalar
            def _(act):
                for j, (key, dst, e) in enumerate(jobs):
                    act.wait_ge(turned, j + 1)
                    if dst is wdT:
                        out = wdT[:, e, :, :]
                        nc.scalar.activation(out, tps[j % 4][:, :, :], ACT.Copy).then_inc(kept, 1)
                    else:
                        nc.scalar.activation(dst[:, e, :], tps[j % 4][:, :, :].rearrange("p f h -> p (f h)"),
                                             ACT.Copy).then_inc(kept, 1)


def program(nc, a, out):
    with ExitStack() as ctx:
        n = setup(nc, ctx, a)
        with ExitStack() as mid:
            yB = mid.enter_context(nc.sbuf_tensor("yB", [P, TOK], F32))
            wqkv = mid.enter_context(nc.sbuf_tensor("wqkv", [P, 3 * INNER], F32))
            wout = mid.enter_context(nc.sbuf_tensor("wout", [P, NC, D], F32))
            local_attention(nc, n, a, yB, wqkv, wout)
            linear_attention(nc, n, yB, wqkv, wout)
        with ExitStack() as mid:
            w1 = mid.enter_context(nc.sbuf_tensor("w1", [P, E, FF], F32))
            w2 = mid.enter_context(nc.sbuf_tensor("w2e", [P, E, NF, D], F32))
            load_experts(nc, n, a, w1, w2)
            hist = mid.enter_context(nc.sbuf_tensor("hist", [P, 16 * (T + 1)], F32))
            hB = mid.enter_context(nc.sbuf_tensor("hB", [P, TOK], F32))
            take = mid.enter_context(nc.sbuf_tensor("take", [P, NBLK, E], F32))
            gru_scan(nc, n, hist)
            route_top1(nc, n, hist, hB, take)
            experts(nc, n, 0, hB, take, (w1,), w2, None)
        with ExitStack() as mid:
            s2 = mid.enter_context(nc.sbuf_tensor("s2", [P, TOK + B], F32))
            gate_scan(nc, n, s2)
            diff_attention(nc, n, s2)
        mB = ctx.enter_context(nc.sbuf_tensor("mB", [P, TOK], F32))
        comb = ctx.enter_context(nc.sbuf_tensor("comb", [P, NBLK, E], F32))
        wgT = ctx.enter_context(nc.sbuf_tensor("wgT", [P, E, FF], F32))
        wuT = ctx.enter_context(nc.sbuf_tensor("wuT", [P, E, FF], F32))
        wdT = ctx.enter_context(nc.sbuf_tensor("wdT", [P, E, NF, D], F32))
        turn_weights(nc, n, a, wgT, wuT, wdT)
        modulated_linear(nc, n, mB, comb)
        experts(nc, n, 1, mB, comb, (wgT, wuT), wdT, out)


def load_experts(nc, n, a, w1, w2):
    done = n.load_experts
    with nc.Block() as block:
        @block.sync
        def _(sp):
            sp.dma_start(w1[:, :, :], a["L0_ffn_W1"].rearrange("e d f -> d e f")).then_inc(done, 16)
            sp.dma_start(w2[:, :, :, :], a["L0_ffn_W2"].rearrange("e (f p) d -> p e f d", p=P)).then_inc(done, 16)


def kernel(**inputs):
    import numpy as np
    import concourse.bacc as bacc
    from concourse.bass_utils import run_bass_kernel_spmd

    nc = bacc.Bacc("TRN2", target_bir_lowering=False, num_devices=1)
    arrays, aps = {}, {}
    for name, value in inputs.items():
        arrays[f"in_{name}"] = np.ascontiguousarray(value)
        aps[name] = nc.dram_tensor(f"in_{name}", arrays[f"in_{name}"].shape, F32, kind="ExternalInput").ap()
    out = nc.dram_tensor("out", (B, T, D), F32, kind="ExternalOutput").ap()
    program(nc, aps, out)
    result = run_bass_kernel_spmd(nc, [arrays], core_ids=[0])
    return result.results[0]["out"]
```

```python
from contextlib import ExitStack

import concourse.bass as bass
from concourse import mybir

F32 = mybir.dt.float32
BF16 = mybir.dt.bfloat16
I32 = mybir.dt.int32
ACT = mybir.ActivationFunctionType
ALU = mybir.AluOpType
AX = mybir.AxisListType

P = 128
B, T, D = 8, 256, 128
TOK = B * T
NBLK = TOK // P
HEADS, HD = 16, 64
INNER = HEADS * HD
NC = INNER // P
E = 8
FF = 512
NF = FF // P
CAPACITY = -(-TOK * 5 // (E * 4))

ROWS = {}
_at = 0
for _name, _count in (("bq", NC), ("bk", NC), ("bv", NC), ("bo", 1), ("bout", 1), ("alpha", 1),
                      ("lq1", 1), ("lk1", 1), ("lq2", 1), ("lk2", 1), ("b1", E * NF), ("cond", B),
                      ("router", E), ("gate", E), ("b2_0", 1)):
    ROWS[_name] = (_at, _count)
    _at += _count
NROWS = _at


class Net:
    pass


def allocate(nc, ctx):
    n = Net()

    def sb(name, shape, dt=F32):
        return ctx.enter_context(nc.sbuf_tensor(name, shape, dt))

    n.sb = sb
    n.xT = sb("xT", [P, TOK])
    n.cols = sb("cols", [P, P])
    n.ident = sb("ident", [P, P])
    n.identb = sb("identb", [P, P], BF16)
    n.gru_w = sb("gru_w", [P, 6, P])
    n.gru_b = sb("gru_b", [1, 4, P])
    n.ones_row = sb("ones_row", [1, P])
    n.b_l1 = sb("b_l1", [1, P])
    n.l1w = sb("l1w", [P, 2 * D])
    n.wq12 = sb("wq12", [P, 2 * D])
    n.wk12 = sb("wk12", [P, 2 * D])
    n.wv1 = sb("wv1", [P, D])
    n.wmod = sb("wmod", [P, D])
    n.b2 = sb("b2", [E, D])
    n.iota8 = sb("iota8", [P, E])
    n.condT = n.cols[:, ROWS["cond"][0]:ROWS["cond"][0] + B]

    n.load_small = ctx.enter_context(nc.semaphore("load_small"))
    n.load_x = ctx.enter_context(nc.semaphore("load_x"))
    n.load_local = ctx.enter_context(nc.semaphore("load_local"))
    n.load_later = ctx.enter_context(nc.semaphore("load_later"))
    n.load_experts = ctx.enter_context(nc.semaphore("load_experts"))
    n.load_linear = ctx.enter_context(nc.semaphore("load_linear"))
    n.later_loads = 16 * 17
    return n


def setup(nc, n, a, wq, wk, wv, wo):
    small = [("bq", a["L0_cond_WQ_b"]), ("bk", a["L0_cond_WK_b"]), ("bv", a["L0_cond_WV_b"]),
             ("bo", a["L0_cond_WO_b"]), ("bout", a["L0_attn_bout"]), 
             ("alpha", a["L1_cond_alpha"]), ("lq1", a["L1_attn_lambda_q1"]), ("lk1", a["L1_attn_lambda_k1"]),
             ("lq2", a["L1_attn_lambda_q2"]), ("lk2", a["L1_attn_lambda_k2"])]
    with ExitStack() as local:
        def sem(name):
            return local.enter_context(nc.semaphore(name))

        rows_done = sem("rows_done"); ident_base = sem("ident_base"); ident_done = sem("ident_done")
        x_turned = sem("x_turned"); x_kept = sem("x_kept")
        rows = local.enter_context(nc.sbuf_tensor("rows", [NROWS, P], F32))
        xtok = local.enter_context(nc.sbuf_tensor("xtok", [P, NBLK, D], F32))
        turn = [local.enter_context(nc.psum_tensor(f"turn{i}", [P, 4, P], F32)) for i in range(2)]
        turn_rows = local.enter_context(nc.psum_tensor("turn_rows", [P, NROWS], F32))
        with nc.Block() as block:

            @block.sync
            def _(sp):
                for name, src in small:
                    r0, k = ROWS[name]
                    sp.dma_start(rows[r0:r0 + k, :], src.rearrange("(r d) -> r d", d=P)).then_inc(n.load_small, 16)
                r0, k = ROWS["b1"]
                sp.dma_start(rows[r0:r0 + k, :], a["L0_ffn_b1"].rearrange("e (c f) -> (e c) f", f=P)).then_inc(n.load_small, 16)
                for name, src in (("cond", "cond_1024"), ("router", "L0_ffn_router_w"), ("gate", "L1_ffn_gate_w")):
                    r0, k = ROWS[name]
                    sp.dma_start(rows[r0:r0 + k, :], a[src]).then_inc(n.load_small, 16)
                r0 = ROWS["b2_0"][0]
                sp.dma_start(rows[r0:r0 + 1, :], a["L0_ffn_b2"][0:1, :]).then_inc(n.load_small, 16)

            @block.scalar
            def _(act):
                act.dma_start(xtok[:, :, :], a["x"].rearrange("b (i p) d -> p (b i) d", p=P)).then_inc(n.load_x, 16)
                for dst, key in ((wk, "L0_cond_WK_w"), (wv, "L0_cond_WV_w"), (wq, "L0_cond_WQ_w")):
                    act.dma_start(dst[:, :], a[key]).then_inc(n.load_local, 16)
                act.dma_start(wo[:, :, :], a["L0_cond_WO_w"].rearrange("(c p) d -> p c d", p=P)).then_inc(n.load_local, 16)
                for g in range(NBLK // 4):
                    act.wait_ge(x_turned, g + 1)
                    out = n.xT[:, :].rearrange("p (i t b) -> p b i t", i=2, b=B)[:, 2 * g:2 * g + 2]
                    nc.scalar.activation(out, turn[g % 2][:, :, :].rearrange("p (b i) t -> p b i t", i=2),
                                         ACT.Copy).then_inc(x_kept, 1)
                act.wait_ge(rows_done, 1)
                nc.scalar.activation(n.cols[:, 0:NROWS], turn_rows[:, :], ACT.Copy)

            @block.gpsimd
            def _(pool):
                pool.memset(n.ident[:, :], 0.0).then_inc(ident_base, 1)
                pool.wait_ge(ident_base, 1)
                pool.affine_select(out=n.ident[:, :], in_=n.ident[:, :], compare_op=ALU.not_equal, fill=1.0,
                                   base=0, pattern=[[-1, P]], channel_multiplier=1).then_inc(ident_done, 1)
                pool.wait_ge(ident_done, 1)
                pool.tensor_copy(n.identb[:, :], n.ident[:, :])
                for e in range(E):
                    pool.memset(n.iota8[:, e:e + 1], float(e))
                pool.memset(n.ones_row[:, :], 1.0)
                pool.memset(n.cols[:, NROWS:P], 0.0)

            @block.tensor
            def _(pe):
                pe.wait_ge(ident_done, 1)
                pe.wait_ge(n.load_x, 16)
                for g in range(NBLK // 4):
                    if g >= 2:
                        pe.wait_ge(x_kept, g - 1)
                    for i in range(4):
                        mm = nc.tensor.transpose(turn[g % 2][:, i, :], xtok[:, 4 * g + i, :], n.ident[:, :])
                    mm.then_inc(x_turned, 1)
                pe.wait_ge(n.load_small, 16 * (len(small) + 5))
                nc.tensor.transpose(turn_rows[:, :], rows[:, :], n.ident[0:NROWS, 0:NROWS]).then_inc(rows_done, 1)


def local_attention(nc, n, a, yB, wq, wk, wv, wo, wqkv, wout):
    HALF = TOK // 2
    HB = HALF // P
    SH = B
    KW = HALF + 2 * SH
    UNITS = 2 * NC
    J = 4
    with ExitStack() as local:
        def sb(name, shape, dt=F32):
            return local.enter_context(nc.sbuf_tensor(name, shape, dt))

        def sem(name):
            return local.enter_context(nc.semaphore(name))

        bq8 = sb("bq8", [P, NC])
        headsel = sb("headsel", [P, 2 * P])
        pick = sb("pick", [24, J, 2, HD], BF16)
        akT, avT = sb("akT", [P, NC, B]), sb("avT", [P, NC, B])
        qb = [sb(f"qb{i}", [P, HALF]) for i in range(4)]
        kb = [sb(f"kb{i}", [P, KW + SH]) for i in range(4)]
        prod = [sb(f"prod{i}", [P, J, HALF]) for i in range(2)]
        s_max, s_sum, s_rec = (sb(k, [P, HB * 2]) for k in ("s_max", "s_sum", "s_rec"))
        s_sh, s_exp, prob, rest1, rest2 = (sb(k, [P, HB * 2, J]) for k in ("s_sh", "s_exp", "prob", "rest1", "rest2"))
        parts = [sb(f"parts{i}", [P, HB, 3, 2 * J], BF16) for i in range(2)]
        probT = [sb(f"probT{i}", [24, HALF], BF16) for i in range(2)]
        term = [sb(f"term{i}", [P, J, 512]) for i in range(2)]
        pair = [sb(f"pair{i}", [P, 2, 512]) for i in range(2)]
        att = [sb(f"att{i}", [P, 512]) for i in range(2)]
        y_ps = [local.enter_context(nc.psum_tensor(f"y_ps{i}", [P, 512], F32)) for i in range(2)]
        pj = [local.enter_context(nc.psum_tensor(f"pj{i}", [P, 512], F32)) for i in range(2)]
        bc = [local.enter_context(nc.psum_tensor(f"bc{i}", [P, 512], F32)) for i in range(2)]
        sc = local.enter_context(nc.psum_tensor("sc", [P, P // (2 * J), J, 2], F32))
        tr = local.enter_context(nc.psum_tensor("tr", [24, HALF], BF16))

        const_a = sem("const_a"); const_done = sem("const_done")
        cond_proj = sem("cond_proj"); cond_kept = sem("cond_kept")
        proj_done = sem("proj_done"); proj_kept = sem("proj_kept")
        prod_v = sem("prod_v"); prod_g = sem("prod_g")
        score_done = sem("score_done"); soft = sem("soft"); exp_done = sem("exp_done")
        parts_done = sem("parts_done"); turned = sem("turned"); turned_kept = sem("turned_kept")
        spread = sem("spread"); term_done = sem("term_done"); pair_done = sem("pair_done"); att_done = sem("att_done")
        y_part = sem("y_part"); y_kept = sem("y_kept")

        def pieces(u):
            h, c = divmod(u, NC)
            t0 = h * HALF
            k0 = 0 if h == 0 else t0 - SH
            return ([("q", t0, 0, 512), ("q", t0 + 512, 512, 512)]
                    + [("k", k0, SH, 512), ("k", k0 + 512, SH + 512, 512), ("k", k0 + 1024, SH + 1024, SH)])

        def key(u, j, at, width):
            base = (u // NC) * SH + (j - 1) * SH + at
            return kb[u % 4][:, base:base + width]

        with nc.Block() as block:

            @block.sync
            def _(sp):
                sp.dma_start(wqkv[:, :], a["L0_attn_Wqkv"]).then_inc(n.load_linear, 16)
                sp.dma_start(wout[:, :, :], a["L0_attn_Wout"].rearrange("(c p) d -> p c d", p=P)).then_inc(n.load_linear, 16)
                for i, key in enumerate(("L0_cond2_W_ir", "L0_cond2_W_iz", "L0_cond2_W_in",
                                         "L0_cond2_W_hr", "L0_cond2_W_hz", "L0_cond2_W_hn")):
                    sp.dma_start(n.gru_w[:, i, :], a[key]).then_inc(n.load_later, 16)
                for i, key in enumerate(("L0_cond2_b_hn", "L0_cond2_b_ir", "L0_cond2_b_iz", "L0_cond2_b_in")):
                    sp.dma_start(n.gru_b[:, i, :], a[key].rearrange("(r d) -> r d", r=1)).then_inc(n.load_later, 16)
                sp.dma_start(n.b_l1[:, :], a["L1_cond_b"].rearrange("(r d) -> r d", r=1)).then_inc(n.load_later, 16)
                for dst, key in ((n.l1w, "L1_cond_W"), (n.wq12, "L1_attn_w_q12"), (n.wk12, "L1_attn_w_k12"),
                                 (n.wv1, "L1_attn_w_v"), (n.wmod, "L1_cond2_weight"), (n.b2, "L0_ffn_b2")):
                    sp.dma_start(dst[:, :], a[key]).then_inc(n.load_later, 16)

            @block.gpsimd
            def _(pool):
                pool.memset(pick[:, :, :, :], 0.0).then_inc(const_a, 1)
                for part in range(3):
                    pool.wait_ge(const_a, part + 1)
                    pool.affine_select(out=pick[:, :, :, :], in_=pick[:, :, :, :], compare_op=ALU.not_equal, fill=1.0,
                                       base=-8 * part, pattern=[[-1, J], [-J, 2], [0, HD]],
                                       channel_multiplier=1).then_inc(const_a, 1)

                def product(u, j):
                    pool.wait_ge(proj_kept, 5 * (u + 1))
                    if u >= 2:
                        pool.wait_ge(score_done, u - 1)
                    pool.tensor_tensor(prod[u % 2][:, j, :], qb[u % 4][:, :], key(u, j, 0, HALF),
                                       ALU.mult).then_inc(prod_g, 1)

                def pair_sum(u, m):
                    s = 2 * u + m
                    pool.wait_ge(term_done, J * (s + 1))
                    if s >= 2:
                        pool.wait_ge(att_done, s - 1)
                    t = term[s % 2]
                    pool.tensor_tensor(pair[s % 2][:, :, :], t[:, 0:2, :], t[:, 2:4, :], ALU.add).then_inc(pair_done, 1)

                for u in range(2):
                    product(u, 1)
                    product(u, 3)
                for u in range(UNITS):
                    if u >= 1:
                        pair_sum(u - 1, 1)
                    if u + 2 < UNITS:
                        product(u + 2, 1)
                        product(u + 2, 3)
                    pair_sum(u, 0)
                pair_sum(UNITS - 1, 1)

            @block.tensor
            def _(pe):
                pe.wait_ge(n.load_local, 64)
                for i, w in enumerate((wk, wv)):
                    for c in range(NC):
                        mm = nc.tensor.matmul(pj[i][:, B * c:B * c + B], w[:, P * c:P * c + P], n.condT,
                                              start=True, stop=True)
                    mm.then_inc(cond_proj, 1)
                pe.wait_ge(cond_kept, 2)
                pe.wait_ge(const_done, 2)
                pe.wait_ge(const_a, 4)

                def project(u, i):
                    if u >= UNITS:
                        return
                    c = u % NC
                    kind, src, _, width = pieces(u)[i]
                    w = wq if kind == "q" else wk
                    g = 5 * u + i
                    if g >= 2:
                        pe.wait_ge(proj_kept, g - 1)
                    nc.tensor.matmul(pj[g % 2][:, 0:width], w[:, P * c:P * c + P], n.xT[:, src:src + width],
                                     start=True, stop=True).then_inc(proj_done, 1)

                def scores(u, i):
                    if u >= UNITS:
                        return
                    if u >= 1 and i == 0:
                        pe.wait_ge(soft, 9 * u - 7)
                    if i == 0:
                        pe.wait_ge(prod_v, 2 * (u + 1))
                        pe.wait_ge(prod_g, 2 * (u + 1))
                    for j in range(J):
                        k = J * i + j
                        mm = nc.tensor.matmul(sc[:, :, :, :].rearrange("p i j h -> p (i j h)"),
                                              prod[u % 2][:, j, P * i:P * i + P], headsel[:, P - 2 * k:2 * P - 2 * k],
                                              start=(k == 0), stop=(k == HB * J - 1))
                    if i == HB - 1:
                        mm.then_inc(score_done, 1)

                def turn_probs(u):
                    pe.wait_ge(parts_done, u + 1)
                    if u >= 1:
                        pe.wait_ge(turned_kept, u)
                    for i in range(HB):
                        mm = nc.tensor.transpose(tr[:, P * i:P * i + P],
                                                 parts[u % 2][:, i, :, :].rearrange("p k r -> p (k r)"), n.identb[:, :])
                    mm.then_inc(turned, 1)

                def spread_probs(u, i):
                    if i == 0:
                        pe.wait_ge(turned_kept, u + 1)
                    m, j = divmod(i, J)
                    g = 2 * J * u + i
                    if g >= 2:
                        pe.wait_ge(term_done, g - 1)
                    nc.tensor.matmul(bc[g % 2][:, :], pick[:, j, :, :].rearrange("r h d -> r (h d)"),
                                     probT[u % 2][:, 512 * m:512 * m + 512], start=True, stop=True).then_inc(spread, 1)

                def project_out(u, m):
                    h, c = divmod(u, NC)
                    if c == 0 and h == 1:
                        pe.wait_ge(y_kept, m + 1)
                    pe.wait_ge(att_done, 2 * u + m + 1)
                    nc.tensor.matmul(y_ps[m][:, :], wo[:, c, :], att[m][:, :], start=(c == 0),
                                     stop=(c == NC - 1)).then_inc(y_part, 1)

                for u in range(2):
                    for i in range(5):
                        project(u, i)
                for i in range(HB):
                    scores(0, i)
                for i in range(5):
                    project(2, i)
                turn_probs(0)
                for u in range(UNITS):
                    scores(u + 1, 0)
                    for i in range(HB - 1):
                        scores(u + 1, i + 1)
                        spread_probs(u, i)
                    project(u + 3, 0)
                    spread_probs(u, HB - 1)
                    project(u + 3, 1)
                    if u >= 1:
                        project_out(u - 1, 1)
                    for i in range(2, 5):
                        project(u + 3, i)
                    project_out(u, 0)
                    if u + 1 < UNITS:
                        turn_probs(u + 1)
                project_out(UNITS - 1, 1)

            @block.scalar
            def _(act):
                act.wait_ge(cond_proj, 2)
                act.wait_ge(const_done, 2)

                def keep_projections(u):
                    c = u % NC
                    bk0 = ROWS["bk"][0]
                    if u >= 4:
                        act.wait_ge(prod_v, 2 * (u - 3))
                        act.wait_ge(prod_g, 2 * (u - 3))
                        act.wait_ge(term_done, 2 * J * (u - 3))
                    for i, (kind, _, dst, width) in enumerate(pieces(u)):
                        g = 5 * u + i
                        act.wait_ge(proj_done, g + 1)
                        if kind == "q":
                            nc.scalar.activation(qb[u % 4][:, dst:dst + width], pj[g % 2][:, 0:width], ACT.Identity,
                                                 bias=bq8[:, c:c + 1], scale=float(HD) ** -0.5).then_inc(proj_kept, 1)
                        else:
                            nc.scalar.activation(kb[u % 4][:, dst:dst + width], pj[g % 2][:, 0:width], ACT.Identity,
                                                 bias=n.cols[:, bk0 + c:bk0 + c + 1]).then_inc(proj_kept, 1)

                def exps(u):
                    act.wait_ge(soft, 9 * u + 2)
                    nc.scalar.activation(s_exp[:, :, :], s_sh[:, :, :], ACT.Exp).then_inc(exp_done, 1)

                def keep_turned(u):
                    act.wait_ge(turned, u + 1)
                    if u >= 2:
                        act.wait_ge(spread, 2 * J * (u - 1))
                    nc.scalar.activation(probT[u % 2][:, :], tr[:, :], ACT.Copy).then_inc(turned_kept, 1)

                def keep_y(h):
                    bo = ROWS["bo"][0]
                    for m in range(2):
                        act.wait_ge(y_part, 2 * NC * (h + 1) - 1 + m)
                        at = h * HALF + 512 * m
                        out = yB[:, :].rearrange("p (b t) -> p t b", b=B)[:, at // B:(at + 512) // B]
                        nc.scalar.activation(out, y_ps[m][:, :].rearrange("p (t b) -> p t b", b=B), ACT.Identity,
                                             bias=n.cols[:, bo:bo + 1]).then_inc(y_kept, 1)

                keep_projections(0)
                keep_projections(1)
                exps(0)
                keep_projections(2)
                keep_turned(0)
                for u in range(UNITS):
                    if u + 1 < UNITS:
                        exps(u + 1)
                    if u + 3 < UNITS:
                        keep_projections(u + 3)
                    if u + 1 < UNITS:
                        keep_turned(u + 1)
                    if u % NC == NC - 1:
                        keep_y(u // NC)

            @block.vector
            def _(dve):
                bq0, bk0, bv0 = ROWS["bq"][0], ROWS["bk"][0], ROWS["bv"][0]
                nc.vector.tensor_scalar(bq8[:, :], n.cols[:, bq0:bq0 + NC], float(HD) ** -0.5, None, ALU.mult)
                nc.vector.memset(headsel[:, :], 0.0).then_inc(const_done, 1)
                dve.wait_ge(const_done, 1)
                for h in range(2):
                    nc.vector.memset(headsel[HD * h:HD * h + HD, P + h:P + h + 1], 1.0)
                for i in range(4):
                    nc.vector.memset(kb[i][:, 0:SH], 0.0)
                    last = nc.vector.memset(kb[i][:, KW:KW + SH], 0.0)
                last.then_inc(const_done, 1)
                dve.wait_ge(cond_proj, 2)
                for i, (dst, b0) in enumerate(((akT, bk0), (avT, bv0))):
                    src = pj[i][:, 0:NC * B].rearrange("p (c b) -> p c b", b=B)
                    bias = n.cols[:, b0:b0 + NC].unsqueeze(2).broadcast_to([P, NC, B])
                    nc.vector.tensor_tensor(dst[:, :, :], src, bias, ALU.add).then_inc(cond_kept, 1)
                dve.wait_ge(cond_kept, 2)

                def products(u):
                    c = u % NC
                    dve.wait_ge(proj_kept, 5 * (u + 1))
                    if u >= 2:
                        dve.wait_ge(score_done, u - 1)
                    q3 = qb[u % 4][:, :].rearrange("p (t b) -> p t b", b=B)
                    ak = akT[:, c, :].unsqueeze(1).broadcast_to([P, HALF // B, B])
                    nc.vector.tensor_tensor(prod[u % 2][:, 0, :].rearrange("p (t b) -> p t b", b=B), q3, ak,
                                            ALU.mult).then_inc(prod_v, 1)
                    nc.vector.tensor_tensor(prod[u % 2][:, 2, :], qb[u % 4][:, :], key(u, 2, 0, HALF),
                                            ALU.mult).then_inc(prod_v, 1)

                def softmax(u):
                    at = 9 * u
                    flat = sc[:, 0:HB, :, :].rearrange("p i j h -> p i h j")
                    wide = [P, HB * 2, J]
                    heads = [P, HB, 2, J]
                    dve.wait_ge(score_done, u + 1)
                    top = s_max[:, :].rearrange("p (i h) -> p i h", h=2)
                    nc.vector.tensor_reduce(top, flat, AX.X, ALU.max).then_inc(soft, 1)
                    dve.wait_ge(soft, at + 1)
                    nc.vector.tensor_tensor(s_sh[:, :, :].rearrange("p (i h) j -> p i h j", h=2), flat,
                                            top.unsqueeze(3).broadcast_to(heads), ALU.subtract).then_inc(soft, 1)
                    dve.wait_ge(exp_done, u + 1)
                    nc.vector.tensor_reduce(s_sum[:, :], s_exp[:, :, :], AX.X, ALU.add).then_inc(soft, 1)
                    dve.wait_ge(soft, at + 3)
                    nc.vector.reciprocal(s_rec[:, :], s_sum[:, :]).then_inc(soft, 1)
                    dve.wait_ge(soft, at + 4)
                    nc.vector.tensor_tensor(prob[:, :, :], s_exp[:, :, :], s_rec[:, :].unsqueeze(2).broadcast_to(wide),
                                            ALU.mult).then_inc(soft, 1)
                    pt = parts[u % 2]
                    if u >= 2:
                        dve.wait_ge(turned, u - 1)
                    pr, r1, r2 = (t[:, :, :].rearrange("p (i h) j -> p i (h j)", h=2) for t in (prob, rest1, rest2))
                    dve.wait_ge(soft, at + 5)
                    nc.vector.tensor_copy(pt[:, :, 0, :], pr).then_inc(soft, 1)
                    dve.wait_ge(soft, at + 6)
                    nc.vector.tensor_tensor(r1, pr, pt[:, :, 0, :], ALU.subtract).then_inc(soft, 1)
                    dve.wait_ge(soft, at + 7)
                    nc.vector.tensor_copy(pt[:, :, 1, :], r1).then_inc(soft, 1)
                    dve.wait_ge(soft, at + 8)
                    nc.vector.tensor_tensor(r2, r1, pt[:, :, 1, :], ALU.subtract).then_inc(soft, 1)
                    dve.wait_ge(soft, at + 9)
                    nc.vector.tensor_copy(pt[:, :, 2, :], r2).then_inc(parts_done, 1)

                def terms(u, m, steps):
                    c = u % NC
                    s = 2 * u + m
                    if s >= 2:
                        dve.wait_ge(pair_done, s - 1)
                    for j in steps:
                        g = s * J + j
                        dve.wait_ge(spread, g + 1)
                        if j == 0:
                            av = avT[:, c, :].unsqueeze(1).broadcast_to([P, 512 // B, B])
                            nc.vector.tensor_tensor(term[s % 2][:, 0, :].rearrange("p (t b) -> p t b", b=B),
                                                    bc[g % 2][:, :].rearrange("p (t b) -> p t b", b=B), av,
                                                    ALU.mult).then_inc(term_done, 1)
                        else:
                            nc.vector.tensor_tensor(term[s % 2][:, j, :], bc[g % 2][:, :], key(u, j, 512 * m, 512),
                                                    ALU.mult).then_inc(term_done, 1)

                def attended(u, m):
                    s = 2 * u + m
                    dve.wait_ge(pair_done, s + 1)
                    if s >= 2:
                        dve.wait_ge(y_part, s - 1)
                    nc.vector.tensor_tensor(att[s % 2][:, :], pair[s % 2][:, 0, :], pair[s % 2][:, 1, :],
                                            ALU.add).then_inc(att_done, 1)

                products(0)
                products(1)
                softmax(0)
                for u in range(UNITS):
                    if u + 2 < UNITS:
                        products(u + 2)
                    if u >= 1:
                        attended(u - 1, 1)
                    terms(u, 0, range(J))
                    terms(u, 1, range(2))
                    if u + 1 < UNITS:
                        softmax(u + 1)
                    attended(u, 0)
                    terms(u, 1, range(2, J))
                attended(UNITS - 1, 1)
def linear_attention(nc, n, yB, wqkv, wout):
    SEG = T // P
    EPS = 1e-6
    PIECES = 12
    ELU = 8
    W = P + 2
    GROUPS = ((0, 1, 2), (3, 4, 5), (6, 7))
    NG = len(GROUPS)
    with ExitStack() as local:
        def sb(name, shape, dt=F32):
            return local.enter_context(nc.sbuf_tensor(name, shape, dt))

        def ps(name, shape):
            return local.enter_context(nc.psum_tensor(name, shape, F32))

        def sem(name):
            return local.enter_context(nc.semaphore(name))

        kk = [sb(f"kk{i}", [P, SEG, INNER]) for i in range(2)]
        vv = [sb(f"vv{i}", [P, SEG, NC, W]) for i in range(2)]
        qq = [sb(f"qq{i}", [P, NC, T]) for i in range(2)]
        ex = [sb(f"ex{i}", [P, 512]) for i in range(2)]
        rl = [sb(f"rl{i}", [P, 512]) for i in range(2)]
        kv = sb("kv", [P, NC, W])
        den = [sb(f"den{i}", [P, 3, 2]) for i in range(2)]
        rec = [sb(f"rec{i}", [P, 3, 2]) for i in range(2)]
        heads = sb("l_heads", [P, SEG, INNER])
        headsT = sb("l_headsT", [P, NC, T])
        mask = sb("mask", [P, W])
        pj = [ps(f"lpj{i}", [P, 512]) for i in range(2)]
        kv_ps = [ps(f"kv_ps{i}", [P, 3, W]) for i in range(2)]
        att_ps = [ps(f"att_ps{i}", [P, 3, W]) for i in range(2)]
        t_ps = ps("lt_ps", [P, 4, P])
        out_ps = ps("out_ps", [P, T])

        const = sem("l_const"); proj_done = sem("l_proj"); piece_kept = sem("l_kept"); elu_in = sem("l_elu_in")
        elu_done = sem("l_elu"); v_kept = sem("l_v"); kv_done = sem("l_kv"); kv_kept = sem("l_kv_kept")
        att_done = sem("l_att"); rec_step = sem("l_rec"); normed = sem("l_normed")
        turned = sem("l_turned"); turned_kept = sem("l_turned_kept"); out_done = sem("l_out"); added = sem("l_added")

        def kind(i):
            return "q" if i >= 8 else ("k" if i % 4 < 2 else "v")

        def elu_target(b, e):
            if e < 4:
                return kk[b % 2][:, e // 2, 512 * (e % 2):512 * (e % 2) + 512]
            return qq[b % 2][:, 2 * (e - 4):2 * (e - 4) + 2, :].rearrange("p c t -> p (c t)")

        with nc.Block() as block:

            @block.tensor
            def _(pe):
                pe.wait_ge(n.load_linear, 32)

                def project(b, i):
                    if b >= B:
                        return
                    g = PIECES * b + i
                    if g >= 2:
                        pe.wait_ge(piece_kept, g - 1)
                    if kind(i) == "q":
                        for c in range(2):
                            c0 = (2 * (i - 8) + c) * P
                            mm = nc.tensor.matmul(pj[g % 2][:, T * c:T * c + T], wqkv[:, c0:c0 + P],
                                                  yB[:, T * b:T * b + T], start=True, stop=True)
                    else:
                        at = T * b + P * (i // 4)
                        c0 = INNER + 512 * (i % 4)
                        mm = nc.tensor.matmul(pj[g % 2][:, :], yB[:, at:at + P], wqkv[:, c0:c0 + 512],
                                              start=True, stop=True)
                    mm.then_inc(proj_done, 1)

                def key_values(b, j):
                    g = NG * b + j
                    if g >= 2:
                        pe.wait_ge(kv_kept, g - 1)
                    for k, c in enumerate(GROUPS[j]):
                        for i in range(SEG):
                            mm = nc.tensor.matmul(kv_ps[g % 2][:, k, :], kk[b % 2][:, i, P * c:P * c + P],
                                                  vv[b % 2][:, i, c, :], start=(i == 0), stop=(i == SEG - 1))
                    mm.then_inc(kv_done, 1)

                def attend(b, j):
                    i, grp = divmod(j, NG)
                    g = 2 * NG * b + j
                    pe.wait_ge(kv_kept, NG * b + grp + 1)
                    if g >= 2:
                        pe.wait_ge(normed, g - 1)
                    for k, c in enumerate(GROUPS[grp]):
                        mm = nc.tensor.matmul(att_ps[g % 2][:, k, :], qq[b % 2][:, c, P * i:P * i + P], kv[:, c, :],
                                              start=True, stop=True)
                    mm.then_inc(att_done, 1)

                def turn(b, j):
                    i, half = divmod(j, 2)
                    pe.wait_ge(normed, 2 * NG * b + NG * i + (2, 3)[half])
                    if 4 * b + j >= 1:
                        pe.wait_ge(turned_kept, 4 * b + j)
                    for k in range(4):
                        c = 4 * half + k
                        mm = nc.tensor.transpose(t_ps[:, k, :], heads[:, i, P * c:P * c + P], n.ident[:, :])
                    mm.then_inc(turned, 1)

                def outputs(b):
                    pe.wait_ge(turned_kept, 4 * (b + 1))
                    if b >= 1:
                        pe.wait_ge(added, b)
                    for c in range(NC):
                        mm = nc.tensor.matmul(out_ps[:, :], wout[:, c, :], headsT[:, c, :], start=(c == 0), stop=(c == NC - 1))
                    mm.then_inc(out_done, 1)

                pe.wait_ge(const, 1)
                for i in range(PIECES):
                    project(0, i)
                for b in range(B):
                    pe.wait_ge(elu_done, ELU * (b + 1))
                    pe.wait_ge(v_kept, 4 * (b + 1))
                    for i in range(NG):
                        key_values(b, i)
                        project(b + 1, i)
                    for i in range(NG):
                        attend(b, i)
                        project(b + 1, NG + i)
                    attend(b, 3)
                    turn(b, 0)
                    project(b + 1, 6)
                    attend(b, 4)
                    turn(b, 1)
                    project(b + 1, 7)
                    attend(b, 5)
                    project(b + 1, 8)
                    turn(b, 2)
                    project(b + 1, 9)
                    project(b + 1, 10)
                    turn(b, 3)
                    project(b + 1, 11)
                    outputs(b)

            @block.scalar
            def _(act):
                act.wait_ge(const, 1)

                def keep(b, i):
                    if b >= B:
                        return
                    g = PIECES * b + i
                    act.wait_ge(proj_done, g + 1)
                    if kind(i) == "v":
                        if b >= 2:
                            act.wait_ge(kv_done, NG * (b - 1))
                        out = vv[b % 2][:, i // 4, 4 * (i % 2):4 * (i % 2) + 4, 0:P]
                        nc.scalar.activation(out, pj[g % 2][:, :].rearrange("p (c f) -> p c f", f=P), ACT.Copy).then_inc(piece_kept, 1)
                        act.wait_ge(piece_kept, g + 1)
                        act.sem_inc(v_kept, 1)
                        return
                    e = ELU * b + (2 * (i // 4) + i % 4 if i < 8 else i - 4)
                    if e >= 2:
                        act.wait_ge(elu_done, e - 1)
                    nc.scalar.activation(ex[e % 2][:, :], pj[g % 2][:, :], ACT.Exp).then_inc(elu_in, 1)
                    nc.scalar.activation(rl[e % 2][:, :], pj[g % 2][:, :], ACT.Relu).then_inc(elu_in, 1)
                    act.wait_ge(elu_in, 2 * (e + 1))
                    act.sem_inc(piece_kept, 1)

                def keep_turned(b, j):
                    i, half = divmod(j, 2)
                    act.wait_ge(turned, 4 * b + j + 1)
                    if b >= 1 and j == 0:
                        act.wait_ge(out_done, b)
                    nc.scalar.activation(headsT[:, 4 * half:4 * half + 4, P * i:P * i + P], t_ps[:, :, :],
                                         ACT.Copy).then_inc(turned_kept, 1)

                for i in range(PIECES):
                    keep(0, i)
                for b in range(B):
                    for i in range(6):
                        keep(b + 1, i)
                    keep_turned(b, 0)
                    keep(b + 1, 6)
                    keep_turned(b, 1)
                    keep(b + 1, 7)
                    keep(b + 1, 8)
                    keep_turned(b, 2)
                    keep(b + 1, 9)
                    keep(b + 1, 10)
                    keep_turned(b, 3)
                    keep(b + 1, 11)

            @block.vector
            def _(dve):
                for i in range(2):
                    nc.vector.memset(vv[i][:, :, :, P:W], 1.0)
                for h in range(2):
                    for other in range(2):
                        nc.vector.memset(mask[HD * h:HD * h + HD, HD * other:HD * other + HD], float(h == other))
                        m = nc.vector.memset(mask[HD * h:HD * h + HD, P + other:P + other + 1], float(h == other))
                m.then_inc(const, 1)
                dve.wait_ge(const, 1)

                def elu(b, e):
                    if b >= B:
                        return
                    g = ELU * b + e
                    dve.wait_ge(elu_in, 2 * (g + 1))
                    if b >= 2 and e == 0:
                        dve.wait_ge(kv_done, NG * (b - 1))
                    if b >= 2 and e == 4:
                        dve.wait_ge(att_done, 2 * NG * (b - 1))
                    nc.vector.scalar_tensor_tensor(elu_target(b, e), ex[g % 2][:, :], 1.0, rl[g % 2][:, :],
                                                   ALU.min, ALU.add).then_inc(elu_done, 1)

                def keep_key_values(b, j):
                    g, k = NG * b + j, len(GROUPS[j])
                    c = GROUPS[j][0]
                    dve.wait_ge(kv_done, g + 1)
                    if b >= 1 and j == 0:
                        dve.wait_ge(att_done, 2 * NG * b)
                    nc.vector.tensor_tensor(kv[:, c:c + k, :], kv_ps[g % 2][:, 0:k, :],
                                            mask[:, :].unsqueeze(1).broadcast_to([P, k, W]), ALU.mult).then_inc(kv_kept, 1)

                def normalise(b, j):
                    i, grp = divmod(j, NG)
                    g, k, c = 2 * NG * b + j, len(GROUPS[grp]), GROUPS[grp][0]
                    dve.wait_ge(att_done, g + 1)
                    if b >= 1 and j == 0:
                        dve.wait_ge(turned, 4 * b)
                    nc.vector.tensor_scalar(den[g % 2][:, 0:k, :], att_ps[g % 2][:, 0:k, P:W], EPS, None, ALU.add).then_inc(rec_step, 1)
                    dve.wait_ge(rec_step, 2 * g + 1)
                    nc.vector.reciprocal(rec[g % 2][:, 0:k, :], den[g % 2][:, 0:k, :]).then_inc(rec_step, 1)
                    dve.wait_ge(rec_step, 2 * g + 2)
                    out = heads[:, i, P * c:P * (c + k)].rearrange("p (c h d) -> p c h d", h=2, d=HD)
                    nc.vector.tensor_tensor(out, att_ps[g % 2][:, 0:k, 0:P].rearrange("p c (h d) -> p c h d", h=2),
                                            rec[g % 2][:, 0:k, :].unsqueeze(3).broadcast_to([P, k, 2, HD]),
                                            ALU.mult).then_inc(normed, 1)

                def add(b):
                    dve.wait_ge(out_done, b + 1)
                    bout = ROWS["bout"][0]
                    x = n.xT[:, :].rearrange("p (t b) -> p b t", b=B)[:, b]
                    nc.vector.scalar_tensor_tensor(x, out_ps[:, :], n.cols[:, bout:bout + 1], x,
                                                   ALU.add, ALU.add).then_inc(added, 1)

                for e in range(ELU):
                    elu(0, e)
                for b in range(B):
                    keep_key_values(b, 0)
                    elu(b + 1, 0)
                    keep_key_values(b, 1)
                    elu(b + 1, 1)
                    keep_key_values(b, 2)
                    normalise(b, 0)
                    normalise(b, 1)
                    elu(b + 1, 2)
                    normalise(b, 2)
                    elu(b + 1, 3)
                    normalise(b, 3)
                    normalise(b, 4)
                    normalise(b, 5)
                    for e in range(4, ELU):
                        elu(b + 1, e)
                    add(b)


def gru_scan(nc, n, hist, w1, w2, diffT):
    G = P // B
    GROUPS = T // G
    JOBS = GROUPS * E
    FILL = 16
    b10, b20, r0 = ROWS["b1"][0], ROWS["b2_0"][0], ROWS["router"][0]
    with ExitStack() as local:
        def sb(name, shape, dt=F32):
            return local.enter_context(nc.sbuf_tensor(name, shape, dt))

        def sem(name):
            return local.enter_context(nc.semaphore(name))

        def ps(name, shape):
            return local.enter_context(nc.psum_tensor(name, shape, F32))

        pre_r = [ps(f"pre_r{i}", [P, 512]) for i in range(2)]
        pre_z = [ps(f"pre_z{i}", [P, 512]) for i in range(2)]
        pre_n = [ps(f"pre_n{i}", [P, 512]) for i in range(2)]
        h_ps = ps("gh_ps", [P, NF, P])
        y_bank = ps("gy_ps", [P, 4, P])
        y_ps, turn_ps, diff_ps, logits_ps = (y_bank[:, i, :] for i in range(4))
        rz = [sb(f"rz{i}", [P, 32]) for i in range(2)]
        narg = [sb(f"narg{i}", [P, 16]) for i in range(2)]
        keepz = [sb(f"keepz{i}", [P, 16]) for i in range(2)]
        mix = [sb(f"mix{i}", [P, 16]) for i in range(2)]
        hid = [sb(f"ghid{i}", [P, NF, P]) for i in range(2)]
        diff, y0 = sb("g_diff", [P, D]), sb("g_y0", [P, D])
        top, mark, first_e, choice = sb("g_top", [P, 1]), sb("g_mark", [P, E]), sb("g_first", [P, 1]), sb("g_choice", [P, E])
        choiceT = sb("g_choiceT", [E, P])
        iota_m8, zero_hot = sb("g_iota", [P, E]), sb("g_zero_hot", [P, E])
        const = sem("g_const"); r_pre = sem("r_pre"); z_pre = sem("z_pre"); n_pre = sem("n_pre")
        r_done = sem("r_done"); z_done = sem("z_done"); narg_done = sem("narg_done"); n_done = sem("n_done"); z_used = sem("z_used")
        state = sem("state"); hist_zero = sem("hist_zero")
        h_in = sem("g_h_in"); h_done = sem("g_h_done"); y_in = sem("g_y_in"); summed = sem("g_summed")
        logits_in = sem("g_logits"); choosing = sem("g_choosing"); choice_in = sem("g_choice_in")
        choice_kept = sem("g_choice_kept"); bias_in = sem("g_bias_in"); bias_kept = sem("g_bias_kept"); back_in = sem("g_back_in"); kept = sem("g_kept")

        def gate_slot(pre, s):
            return pre[s // G % 2][:, B * (s % G):B * (s % G) + B]

        def n_slot(s):
            return pre_n[s // G % 2][:, 16 * (s % G):16 * (s % G) + 16]

        def second(ap):
            return ap.rearrange("p (b two) -> p two b", two=2)[:, 1]

        def first(ap):
            return ap.rearrange("p (b two) -> p two b", two=2)[:, 0]

        def at_step(s):
            return hist[:, 16 * s:16 * s + 16]

        def tokens(g):
            return second(hist[:, 16 * (G * g + 1):16 * (G * (g + 1) + 1)])

        def jobs_at(s):
            return divmod(s - G, G)

        STEPS = T + G + 5

        with nc.Block() as block:

            @block.gpsimd
            def _(pool):
                pool.memset(hist[:, 16 * 40:], 0.0).then_inc(hist_zero, 1)

            @block.tensor
            def _(pe):
                pe.wait_ge(n.load_later, n.later_loads)
                pe.wait_ge(const, 4)

                def inputs(g, i):
                    if g >= 2 and i == 0:
                        pe.wait_ge(state, G * (g - 1) + 1)
                    nv = pre_n[g % 2][:, 0:256].rearrange("p (x two) -> p two x", two=2)
                    rv, zv = pre_r[g % 2][:, 0:P], pre_z[g % 2][:, 0:P]
                    out = (rv, zv, nv[:, 1], nv[:, 0], rv, zv, nv[:, 1])[i]
                    if i < 3:
                        lhsT, rhs = n.gru_w[:, i, :], n.xT[:, P * g:P * g + P]
                    else:
                        lhsT, rhs = n.gru_b[:, i - 3, :], n.ones_row[:, :]
                    nc.tensor.matmul(out, lhsT, rhs, start=(i < 3), stop=False, skip_group_check=True)

                def hidden(v):
                    g, e = divmod(v, E)
                    if v:
                        pe.wait_ge(h_done, NF * v)
                    for f in range(NF):
                        mm = nc.tensor.matmul(h_ps[:, f, :], w1[:, e, P * f:P * f + P], tokens(g), start=True, stop=True)
                    mm.then_inc(h_in, 1)

                def output(v):
                    g, e = divmod(v, E)
                    pe.wait_ge(h_done, NF * (v + 1))
                    if v:
                        pe.wait_ge(summed, v)
                    for f in range(NF):
                        mm = nc.tensor.matmul(y_ps, hid[v % 2][:, f, :], w2[:, e, f, :], start=(f == 0), stop=(f == NF - 1))
                    mm.then_inc(y_in, 1)

                def work(s):
                    g, k = jobs_at(s)
                    if g < 0:
                        for _ in range(FILL):
                            nc.tensor.matmul(y_ps, n.identb[:, :], n.identb[:, :], start=True, stop=True)
                        return
                    v = (s - G) // 2
                    if k % 2 == 0 and v < JOBS:
                        if v == 0:
                            pe.wait_ge(n.load_experts, 32)
                        hidden(v)
                    if s == G + 3:
                        pe.wait_ge(choosing, 2)
                    if k % 2 == 1 and 0 <= v - 1 < JOBS:
                        output(v - 1)
                    if k == 1 and g < GROUPS:
                        if g:
                            pe.wait_ge(bias_kept, g)
                        nc.tensor.matmul(logits_ps, tokens(g), n.cols[:, :], start=True, stop=True).then_inc(logits_in, 1)
                    if k == 3 and g:
                        pe.wait_ge(summed, E * g)
                        if g < GROUPS:
                            pe.wait_ge(choosing, 4 * g + 2)
                        nc.tensor.transpose(diff_ps, diff[:, :], n.ident[:, :])
                        nc.tensor.transpose(turn_ps, y0[:, :], n.ident[:, :]).then_inc(back_in, 1)
                    if k == 5 and g < GROUPS:
                        pe.wait_ge(choosing, 4 * (g + 1))
                        if g:
                            pe.wait_ge(kept, 2 * g)
                        nc.tensor.transpose(turn_ps[0:E, :], choice[:, :], n.ident[:, :]).then_inc(choice_in, 1)
                    if k == 7 and g < GROUPS:
                        pe.wait_ge(choice_kept, g + 1)
                        nc.tensor.matmul(turn_ps, n.b2[:, :], choiceT[:, :], start=True, stop=True).then_inc(bias_in, 1)

                for i in range(7):
                    inputs(0, i)
                for s in range(STEPS):
                    if s < T:
                        h = second(hist[:, 16 * s:16 * (s + G)]).rearrange("p (s b) -> p s b", b=B)
                        at = 16 * (s % G)
                        at8 = B * (s % G)
                        r_out, z_out = (pre[s // G % 2][:, at8:at8 + P].rearrange("p (s b) -> p s b", b=B) for pre in (pre_r, pre_z))
                        n_out = first(pre_n[s // G % 2][:, at:at + 16 * G]).rearrange("p (s b) -> p s b", b=B)
                        if s == 24:
                            pe.wait_ge(hist_zero, 1)
                        pe.wait_ge(state, s + 1)
                        for out, i, ready in ((r_out, 3, r_pre), (n_out, 5, n_pre), (z_out, 4, z_pre)):
                            nc.tensor.matmul(out, n.gru_w[:, i, :], h, start=False, stop=True,
                                             skip_group_check=True).then_inc(ready, 1)
                    elif s == T:
                        pe.wait_ge(state, T + 1)
                    work(s)
                    g, i = s // G + 1, s % G - 9
                    if g < GROUPS and 0 <= i < 7:
                        inputs(g, i)

            @block.scalar
            def _(act):
                act.preload_act_table(ACT.Sigmoid)
                act.wait_ge(const, 4)
                for s in range(STEPS):
                    if s < T:
                        act.wait_ge(r_pre, s + 1)
                        nc.scalar.activation(second(rz[s % 2][:, 0:16]), gate_slot(pre_r, s), ACT.Sigmoid).then_inc(r_done, 1)
                        act.wait_ge(z_pre, s + 1)
                        nc.scalar.activation(second(rz[s % 2][:, 16:32]), gate_slot(pre_z, s), ACT.Sigmoid).then_inc(z_done, 1)
                        act.wait_ge(narg_done, s + 1)
                        nc.scalar.activation(first(mix[s % 2][:, :]), second(narg[s % 2][:, :]), ACT.Tanh).then_inc(n_done, 1)
                    v, odd = divmod(s - G, 2)
                    if odd and 0 <= v < JOBS:
                        e = v % E
                        act.wait_ge(h_in, v + 1)
                        if v >= 2:
                            act.wait_ge(y_in, v - 1)
                        for f in range(NF):
                            at = b10 + NF * e + f
                            nc.scalar.activation(hid[v % 2][:, f, :], h_ps[:, f, :], ACT.Relu,
                                                 bias=n.cols[:, at:at + 1]).then_inc(h_done, 1)

            @block.vector
            def _(dve):
                V = nc.vector
                for i in range(2):
                    V.memset(rz[i][:, :], 0.0)
                    V.memset(keepz[i][:, :], 0.0)
                    last = V.memset(mix[i][:, :], 0.0)
                last.then_inc(const, 1)
                V.tensor_scalar(iota_m8[:, :], n.iota8[:, :], -float(E), None, ALU.add).then_inc(const, 1)
                V.tensor_scalar(zero_hot[:, :], n.iota8[:, :], 0.0, None, ALU.is_equal).then_inc(const, 1)
                V.memset(hist[:, 0:16 * 40], 0.0).then_inc(const, 1)
                dve.wait_ge(const, 4)
                V.tensor_copy(second(at_step(0)), n.condT).then_inc(state, 1)
                dve.wait_ge(state, 1)

                def choose(g, k):
                    dve.wait_ge(logits_in, g + 1)
                    if g or k:
                        dve.wait_ge(choosing, 4 * g + k)
                    if k == 0:
                        ins = V.tensor_reduce(top[:, :], logits_ps[:, r0:r0 + E], AX.X, ALU.max)
                    elif k == 1:
                        ins = V.scalar_tensor_tensor(mark[:, :], logits_ps[:, r0:r0 + E], top[:, 0:1], iota_m8[:, :], ALU.is_equal, ALU.mult)
                    elif k == 2:
                        ins = V.tensor_reduce(first_e[:, :], mark[:, :], AX.X, ALU.min)
                    else:
                        if g:
                            dve.wait_ge(choice_in, g)
                            dve.wait_ge(summed, E * g)
                        ins = V.scalar_tensor_tensor(choice[:, :], iota_m8[:, :], first_e[:, 0:1], zero_hot[:, :],
                                                     ALU.is_equal, ALU.subtract)
                    ins.then_inc(choosing, 1)

                def add(v):
                    g, e = divmod(v, E)
                    dve.wait_ge(y_in, v + 1)
                    if e == 0:
                        if g:
                            dve.wait_ge(back_in, g)
                        V.tensor_copy(y0[:, :], y_ps)
                        dve.wait_ge(choosing, 4 * (g + 1))
                        V.tensor_scalar(diff[:, :], y_ps, choice[:, 0:1], None, ALU.mult).then_inc(summed, 1)
                    else:
                        dve.wait_ge(summed, v)
                        V.scalar_tensor_tensor(diff[:, :], y_ps, choice[:, e:e + 1], diff[:, :],
                                               ALU.mult, ALU.add).then_inc(summed, 1)

                def keep(g):
                    cols = slice(P * g, P * g + P)
                    dve.wait_ge(back_in, g + 1)
                    V.scalar_tensor_tensor(n.xT[:, cols], turn_ps, n.cols[:, b20:b20 + 1], n.xT[:, cols],
                                           ALU.add, ALU.add).then_inc(kept, 1)
                    dve.wait_ge(bias_kept, g + 1)
                    V.tensor_tensor(diffT[:, cols], diff_ps, diffT[:, cols], ALU.add).then_inc(kept, 1)

                for s in range(STEPS):
                    if s < T:
                        p = s % 2
                        dve.wait_ge(r_done, s + 1)
                        dve.wait_ge(n_pre, s + 1)
                        V.tensor_tensor_scan(narg[p][:, :], rz[p][:, 0:16], n_slot(s), 0.0,
                                             ALU.mult, ALU.add).then_inc(narg_done, 1)
                        z = second(rz[p][:, 16:32])
                        dve.wait_ge(z_done, s + 1)
                        V.tensor_scalar(second(keepz[p][:, :]), z, -1.0, 1.0, ALU.mult, ALU.add).then_inc(z_used, 1)
                        V.tensor_tensor(second(mix[p][:, :]), z, second(at_step(s)), ALU.mult).then_inc(z_used, 1)
                        dve.wait_ge(z_used, 2 * s + 2)
                        dve.wait_ge(n_done, s + 1)
                        V.tensor_tensor_scan(at_step(s + 1), keepz[p][:, :], mix[p][:, :], 0.0,
                                             ALU.mult, ALU.add).then_inc(state, 1)
                    g, k = jobs_at(s)
                    if g < 0:
                        continue
                    if k == 4 and g:
                        keep(g - 1)
                    if k == 2 and g < GROUPS:
                        choose(g, 0)
                        choose(g, 1)
                    if k == 3 and g < GROUPS:
                        choose(g, 2)
                        choose(g, 3)
                    if k == 6 and g < GROUPS:
                        dve.wait_ge(choice_in, g + 1)
                        V.tensor_copy(choiceT[:, :], turn_ps[0:E, :]).then_inc(choice_kept, 1)
                    if k == 8 and g < GROUPS:
                        dve.wait_ge(bias_in, g + 1)
                        V.tensor_copy(diffT[:, P * g:P * g + P], turn_ps).then_inc(bias_kept, 1)
                    v = (s - G) // 2 - 2
                    if k % 2 == 0 and 0 <= v < JOBS:
                        add(v)


def route_top1(nc, n, hist, diffT):
    with ExitStack() as local:
        def sb(name, shape, dt=F32):
            return local.enter_context(nc.sbuf_tensor(name, shape, dt))

        def sem(name):
            return local.enter_context(nc.semaphore(name))

        wide = [P, NBLK, E]
        hB = sb("hB", [P, TOK])
        score, prob, mark, chosen = (sb(k, wide) for k in ("r_score", "r_prob", "r_mark", "r_chosen"))
        top, total, best, first = (sb(k, [P, NBLK]) for k in ("r_top", "r_total", "r_best", "r_first"))
        mine, rest1, rest2 = (sb(k, wide) for k in ("r_mine", "r_rest1", "r_rest2"))
        parts = sb("r_parts", [P, NBLK, 3, E], BF16)
        picks = sb("r_picks", [P, NBLK, 3, E], BF16)
        partsT = sb("r_partsT", [3 * E, TOK], BF16)
        picksT = sb("r_picksT", [3 * E, TOK], BF16)
        iota_m8 = sb("iota_m8", [P, E])
        before = sb("before", [P, P])
        ones = sb("r_ones", [P, P], BF16)
        junks = [sb(f"junk{i}", [P, TOK], BF16) for i in range(2)]
        counts = sb("r_counts", [P, 3, NBLK])
        rank, kept = sb("r_rank", [P, NBLK]), sb("r_kept", [P, NBLK])
        diag = sb("r_diag", [P, NBLK, P], BF16)
        added = [sb(f"r_added{i}", [P, 2 * T]) for i in range(2)]
        copied = sem("copied"); copied_odd = sem("copied_odd"); const = sem("r_const"); logits_in = sem("logits_in"); step = sem("r_step")
        exp_done = sem("r_exp"); turned = sem("r_turned"); turned_kept = sem("r_turned_kept")
        row_in = sem("row_in"); counted = sem("counted"); final = sem("r_final")
        diag_done = sem("r_diag_done"); spread = sem("r_spread"); added_in = sem("r_added_in"); x_done = sem("r_x_done")

        with ExitStack() as early:
            logits = early.enter_context(nc.psum_tensor("logits", wide, F32))
            tp = early.enter_context(nc.psum_tensor("tp", [3 * E, TOK], BF16))
            tq = early.enter_context(nc.psum_tensor("tq", [3 * E, TOK], BF16))
            with nc.Block() as block:

                @block.gpsimd
                def _(pool):
                    pool.memset(before[:, :], 1.0).then_inc(const, 1)
                    pool.tensor_scalar(iota_m8[:, :], n.iota8[:, :], -float(E), None, ALU.add).then_inc(const, 1)
                    pool.wait_ge(const, 2)
                    pool.affine_select(out=before[:, :], in_=before[:, :], compare_op=ALU.is_gt, fill=0.0,
                                       base=0, pattern=[[-1, P]], channel_multiplier=1).then_inc(const, 1)
                    pool.memset(ones[:, :], 1.0)

                @block.scalar
                def _(act):
                    act.preload_act_table(ACT.Exp)
                    states = hist[:, 16:16 * (T + 1)].rearrange("p (t b two) -> p two b t", b=B, two=2)[:, 1]
                    for b in range(0, B, 2):
                        nc.scalar.activation(hB[:, T * b:T * b + T], states[:, b], ACT.Copy).then_inc(copied, 1)
                    act.wait_ge(step, 2)
                    nc.scalar.activation(prob[:, :, :], score[:, :, :], ACT.Exp).then_inc(exp_done, 1)
                    act.wait_ge(turned, 2)
                    nc.scalar.activation(partsT[:, :], tp[:, :], ACT.Copy).then_inc(turned_kept, 1)

                @block.tensor
                def _(pe):
                    r0 = ROWS["router"][0]
                    for i in range(NBLK):
                        pe.wait_ge((copied, copied_odd)[i // 2 % 2], i // 4 + 1)
                        mm = nc.tensor.matmul(logits[:, i, :], hB[:, P * i:P * i + P], n.cols[:, r0:r0 + E],
                                              start=True, stop=True)
                    mm.then_inc(logits_in, 1)
                    for src, dst, ready in ((picks, tq, 6), (parts, tp, 14)):
                        pe.wait_ge(step, ready)
                        for i in range(NBLK):
                            mm = nc.tensor.transpose(dst[:, P * i:P * i + P],
                                                     src[:, i, :, :].rearrange("p k e -> p (k e)"), n.identb[:, :])
                        mm.then_inc(turned, 1)

                @block.vector
                def _(dve):
                    at = [0]

                    def done(ins):
                        at[0] += 1
                        ins.then_inc(step, 1)
                        dve.wait_ge(step, at[0])

                    def per_token(ap):
                        return ap[:, :].unsqueeze(2).broadcast_to(wide)

                    V = nc.vector
                    states = hist[:, 16:16 * (T + 1)].rearrange("p (t b two) -> p two b t", b=B, two=2)[:, 1]
                    for b in range(1, B, 2):
                        V.tensor_copy(hB[:, T * b:T * b + T], states[:, b]).then_inc(copied_odd, 1)
                    V.memset(counts[:, :, :], 0.0)
                    dve.wait_ge(logits_in, 1)
                    done(V.tensor_reduce(top[:, :], logits[:, :, :], AX.X, ALU.max))
                    done(V.tensor_tensor(score[:, :, :], logits[:, :, :], per_token(top), ALU.subtract))
                    dve.wait_ge(const, 3)
                    ramp = iota_m8[:, :].unsqueeze(1).broadcast_to(wide)
                    done(V.scalar_tensor_tensor(mark[:, :, :], score[:, :, :], 0.0, ramp, ALU.is_equal, ALU.mult))
                    done(V.tensor_reduce(first[:, :], mark[:, :, :], AX.X, ALU.min))
                    done(V.tensor_tensor(chosen[:, :, :], ramp, per_token(first), ALU.is_equal))
                    done(V.tensor_copy(picks[:, :, :, :], chosen[:, :, :].unsqueeze(2).broadcast_to([P, NBLK, 3, E])))
                    dve.wait_ge(exp_done, 1)
                    done(V.tensor_reduce(total[:, :], prob[:, :, :], AX.X, ALU.add))
                    done(V.reciprocal(best[:, :], total[:, :]))
                    done(V.tensor_tensor(mine[:, :, :], chosen[:, :, :], per_token(best), ALU.mult))
                    done(V.tensor_copy(parts[:, :, 0, :], mine[:, :, :]))
                    done(V.tensor_tensor(rest1[:, :, :], mine[:, :, :], parts[:, :, 0, :], ALU.subtract))
                    done(V.tensor_copy(parts[:, :, 1, :], rest1[:, :, :]))
                    done(V.tensor_tensor(rest2[:, :, :], rest1[:, :, :], parts[:, :, 1, :], ALU.subtract))
                    done(V.tensor_copy(parts[:, :, 2, :], rest2[:, :, :]))
                    dve.wait_ge(turned, 1)
                    V.tensor_copy(picksT[:, :], tq[:, :]).then_inc(turned_kept, 1)

        with ExitStack() as middle:
            rows = [middle.enter_context(nc.psum_tensor(f"rows{i}", [P, TOK], F32)) for i in range(2)]
            with nc.Block() as block:

                @block.tensor
                def _(pe):
                    for i in range(NBLK):
                        if i >= 2:
                            pe.wait_ge(counted, i - 1)
                        for m in range(TOK // 512):
                            mm = nc.tensor.matmul(rows[i % 2][:, 512 * m:512 * m + 512], picksT[:, P * i:P * i + P],
                                                  partsT[:, 512 * m:512 * m + 512], start=True, stop=True)
                        mm.then_inc(row_in, 1)

                @block.vector
                def _(dve):
                    V = nc.vector
                    for i in range(NBLK):
                        p = best[:, i:i + 1]
                        row = rows[i % 2]
                        junk = junks[i % 2]
                        dve.wait_ge(row_in, i + 1)
                        if i >= 2:
                            dve.wait_ge(counted, i - 1)
                        if i:
                            V.tensor_scalar(junk[:, 0:P * i], row[:, 0:P * i], p, None, ALU.is_ge, ALU.add,
                                            accum_out=counts[:, 0, i:i + 1])
                        V.scalar_tensor_tensor(junk[:, P * i:P * i + P], row[:, P * i:P * i + P], p, before[:, :],
                                               ALU.is_equal, ALU.mult, accum_out=counts[:, 1, i:i + 1]).then_inc(final, 1)
                        dve.wait_ge(final, i + 1)
                        V.tensor_scalar(junk[:, P * i:TOK], row[:, P * i:TOK], p, None, ALU.is_gt, ALU.add,
                                        accum_out=counts[:, 2, i:i + 1]).then_inc(counted, 1)
                    dve.wait_ge(counted, NBLK)
                    V.tensor_reduce(rank[:, :], counts[:, :, :].rearrange("p k i -> p i k"), AX.X, ALU.add).then_inc(final, 1)
                    dve.wait_ge(final, NBLK + 1)
                    V.tensor_scalar(kept[:, :], rank[:, :], float(CAPACITY), None, ALU.is_lt).then_inc(final, 1)
                    dve.wait_ge(final, NBLK + 2)
                    for m in range(4):
                        blocks = slice(4 * m, 4 * m + 4)
                        V.tensor_tensor(diag[:, blocks, :], n.identb[:, :].unsqueeze(1).broadcast_to([P, 4, P]),
                                        kept[:, blocks].unsqueeze(2).broadcast_to([P, 4, P]), ALU.mult).then_inc(diag_done, 1)

        keptB = [local.enter_context(nc.psum_tensor(f"keptB{m}", [P, 2 * T], F32)) for m in range(4)]
        with nc.Block() as block:

            @block.tensor
            def _(pe):
                for m in range(4):
                    pe.wait_ge(diag_done, m + 1)
                    nc.tensor.matmul(keptB[m][:, :], ones[:, :], diag[:, 4 * m:4 * m + 4, :].rearrange("p i t -> p (i t)"),
                                     start=True, stop=True).then_inc(spread, 1)

            @block.vector
            def _(dve):
                V = nc.vector
                for m in range(4):
                    pair = slice(2 * m, 2 * m + 2)
                    dve.wait_ge(spread, m + 1)
                    if m >= 2:
                        dve.wait_ge(x_done, m - 1)
                    V.tensor_tensor(added[m % 2][:, :].rearrange("p (t b) -> p t b", b=2),
                                    diffT[:, :].rearrange("p (t b) -> p t b", b=B)[:, :, pair],
                                    keptB[m][:, :].rearrange("p (b t) -> p t b", b=2), ALU.mult).then_inc(added_in, 1)
                    dve.wait_ge(added_in, m + 1)
                    x = n.xT[:, :].rearrange("p (t b) -> p t b", b=B)[:, :, pair]
                    V.tensor_tensor(x, added[m % 2][:, :].rearrange("p (t b) -> p t b", b=2), x, ALU.add).then_inc(x_done, 1)


def experts(nc, n, layer, inB, weight, w_in, w_out, out):
    TILE = 512
    TB = TILE // P
    TILES = TOK // TILE
    gated = layer == 1
    UP = 2 if gated else 1
    UNITS = TILES * E
    with ExitStack() as local:
        def sb(name, shape, dt=F32):
            return local.enter_context(nc.sbuf_tensor(f"{name}_{layer}", shape, dt))

        def ps(name, shape, dt=F32):
            return local.enter_context(nc.psum_tensor(f"{name}_{layer}", shape, dt))

        def sem(name):
            return local.enter_context(nc.semaphore(f"{name}_{layer}"))

        hid = [sb(f"hid{i}", [P, NF, TILE]) for i in range(2)]
        acc = [sb(f"acc{i}", [P, TB, D]) for i in range(2)]
        takeT = sb("takeT", [E, TILE])
        gate = [sb(f"gate{i}", [P, TILE]) for i in range(2)]
        h_ps = [ps(f"h_ps{i}", [P, TILE]) for i in range(4)]
        y_ps = [ps(f"y_ps{i}", [P, TB, D]) for i in range(2)]
        x_ps = ps("x_ps", [P, TILE])
        t_ps = ps("t_ps", [E, TILE])
        h_in = sem("h_in"); gate_done = sem("gate_done"); h_done = sem("h_done"); y_in = sem("y_in"); summed = sem("summed")
        take_in = sem("take_in"); take_kept = sem("take_kept"); bias_in = sem("bias_in"); acc_set = sem("acc_set")
        x_in = sem("x_in"); x_added = sem("x_added"); stored = sem("stored")

        with nc.Block() as block:

            @block.tensor
            def _(pe):
                def hidden(v):
                    t, e = divmod(v, E)
                    for f in range(NF):
                        for k in range(UP):
                            g = (v * NF + f) * UP + k
                            if g >= 4:
                                pe.wait_ge(h_done, (g - 4) // UP + 1)
                            mm = nc.tensor.matmul(h_ps[g % 4][:, :], w_in[k][:, e, P * f:P * f + P],
                                                  inB[:, TILE * t:TILE * t + TILE], start=True, stop=True)
                            mm.then_inc(h_in, 1)

                def output(v):
                    t, e = divmod(v, E)
                    if v >= 2:
                        pe.wait_ge(summed, TB * (v - 1))
                    pe.wait_ge(h_done, NF * (v + 1))
                    for i in range(TB):
                        for f in range(NF):
                            mm = nc.tensor.matmul(y_ps[v % 2][:, i, :], hid[v % 2][:, f, P * i:P * i + P],
                                                  w_out[:, e, f, :], start=(f == 0), stop=(f == NF - 1))
                    mm.then_inc(y_in, 1)

                def bias(t):
                    if t:
                        pe.wait_ge(take_kept, t)
                    for i in range(TB):
                        mm = nc.tensor.transpose(t_ps[:, P * i:P * i + P], weight[:, TB * t + i, :], n.ident[:, :])
                    mm.then_inc(take_in, 1)
                    pe.wait_ge(take_kept, t + 1)
                    if t:
                        pe.wait_ge(x_added, t)
                    for i in range(TB):
                        mm = nc.tensor.matmul(x_ps[:, P * i:P * i + P], takeT[:, P * i:P * i + P], n.b2[:, :],
                                              start=True, stop=True)
                    mm.then_inc(bias_in, 1)

                def turn(t):
                    if gated:
                        if t:
                            pe.wait_ge(x_added, t)
                        for i in range(TB):
                            b, s = divmod(TB * t + i, T // P)
                            x = n.xT[:, :].rearrange("p (t b) -> p b t", b=B)[:, b, P * s:P * s + P]
                            mm = nc.tensor.transpose(x_ps[:, P * i:P * i + P], x, n.ident[:, :])
                    else:
                        pe.wait_ge(summed, TB * E * (t + 1))
                        pe.wait_ge(acc_set, t + 1)
                        for i in range(TB):
                            mm = nc.tensor.transpose(x_ps[:, P * i:P * i + P], acc[t % 2][:, i, :], n.ident[:, :])
                    mm.then_inc(x_in, 1)

                if not gated:
                    pe.wait_ge(n.load_experts, 32)
                hidden(0)
                for v in range(UNITS):
                    t, e = divmod(v, E)
                    if e == 0 and gated:
                        turn(t)
                    if v + 1 < UNITS:
                        hidden(v + 1)
                    if e == 0 and not gated:
                        bias(t)
                    output(v)
                    if e == 7 and not gated:
                        turn(t)

            @block.scalar
            def _(act):
                b10 = ROWS["b1"][0]
                for v in range(UNITS):
                    t, e = divmod(v, E)
                    for f in range(NF):
                        g = v * NF + f
                        if gated:
                            act.wait_ge(h_in, 2 * g + 1)
                            if g >= 2:
                                act.wait_ge(h_done, g - 1)
                            nc.scalar.activation(gate[g % 2][:, :], h_ps[2 * g % 4][:, :], ACT.Silu).then_inc(gate_done, 1)
                        else:
                            act.wait_ge(h_in, g + 1)
                            if v >= 2:
                                act.wait_ge(y_in, v - 1)
                            nc.scalar.activation(hid[v % 2][:, f, :], h_ps[g % 4][:, :], ACT.Relu,
                                                 bias=n.cols[:, b10 + NF * e + f:b10 + NF * e + f + 1]).then_inc(h_done, 1)
                    if e == 0 and not gated:
                        act.wait_ge(take_in, t + 1)
                        nc.scalar.activation(takeT[:, :], t_ps[:, :], ACT.Copy).then_inc(take_kept, 1)
                        act.wait_ge(bias_in, t + 1)
                        if t >= 2:
                            act.wait_ge(x_in, t - 1)
                        nc.scalar.activation(acc[t % 2][:, :, :].rearrange("p i d -> p (i d)"), x_ps[:, :],
                                             ACT.Copy).then_inc(acc_set, 1)

            @block.vector
            def _(dve):
                for v in range(UNITS + 1):
                    if gated and v < UNITS:
                        t, e = divmod(v, E)
                        if v >= 2:
                            dve.wait_ge(y_in, v - 1)
                        for f in range(NF):
                            g = v * NF + f
                            dve.wait_ge(gate_done, g + 1)
                            dve.wait_ge(h_in, 2 * g + 2)
                            nc.vector.tensor_tensor(hid[v % 2][:, f, :], gate[g % 2][:, :], h_ps[(2 * g + 1) % 4][:, :],
                                                    ALU.mult).then_inc(h_done, 1)
                        if e == 0:
                            dve.wait_ge(x_in, t + 1)
                            if t >= 2:
                                dve.wait_ge(stored, 16 * (t - 1))
                            nc.vector.tensor_copy(acc[t % 2][:, :, :].rearrange("p i d -> p (i d)"),
                                                  x_ps[:, :]).then_inc(x_added, 1)
                    if v == 0:
                        continue
                    w = v - 1
                    t, e = divmod(w, E)
                    dve.wait_ge(y_in, w + 1)
                    dve.wait_ge(x_added if gated else acc_set, t + 1)
                    if e:
                        dve.wait_ge(summed, TB * w)
                    for i in range(TB):
                        nc.vector.scalar_tensor_tensor(acc[t % 2][:, i, :], y_ps[w % 2][:, i, :],
                                                       weight[:, TB * t + i, e:e + 1], acc[t % 2][:, i, :],
                                                       ALU.mult, ALU.add).then_inc(summed, 1)
                    if e == E - 1 and not gated:
                        dve.wait_ge(x_in, t + 1)
                        x = n.xT[:, :].rearrange("p (t b) -> p b t", b=B)[:, 2 * t:2 * t + 2]
                        nc.vector.tensor_tensor(x, x_ps[:, :].rearrange("p (b t) -> p b t", b=2), x, ALU.add).then_inc(x_added, 1)

            @block.sync
            def _(sp):
                if gated:
                    for t in range(TILES):
                        sp.wait_ge(summed, TB * E * (t + 1))
                        dst = out.rearrange("b (s p) d -> p (b s) d", p=P)[:, TB * t:TB * t + TB]
                        sp.dma_start(dst, acc[t % 2][:, :, :]).then_inc(stored, 16)
                    sp.wait_ge(stored, 16 * TILES)


def gate_scan(nc, n, a, s2, qk, vt, wgT, wuT, wdT):
    KINDS = (("L1_ffn_wg", wgT), ("L1_ffn_wu", wuT), ("L1_ffn_wd", wdT))
    jobs = [(key, dst, e) for key, dst in KINDS for e in range(E)]
    EVERY = T // len(jobs)
    RAW = 4
    FILL = 12
    SPAN = 32
    plan, at = {}, 0
    for p in range(T // SPAN - 1):
        at = max(at, SPAN * (p + 1))
        for item in [("qk", p, k) for k in range(4)] + ([("v", p, k) for k in range(4)] if SPAN * (p + 1) == P else []):
            at += 1
            while (at - 4) % EVERY in (0, 1):
                at += 1
            plan[at] = (len(plan),) + item
    assert at < T
    G = 32
    with ExitStack() as local:
        def sb(name, shape, dt=F32):
            return local.enter_context(nc.sbuf_tensor(name, shape, dt))

        def sem(name):
            return local.enter_context(nc.semaphore(name))

        wT = sb("wT", [P, 2, D])
        leak = sb("leak", [P, 1])
        ones_w = sb("ones_w", [1, B * G])
        pairs = sb("pairs", [P, 16 * T])
        gates = [sb(f"gates{i}", [P, 16]) for i in range(2)]
        targ = [sb(f"targ{i}", [P, 16]) for i in range(2)]
        pre = [local.enter_context(nc.psum_tensor(f"s_pre{i}", [P, 512], F32)) for i in range(2)]
        w_ps = local.enter_context(nc.psum_tensor("w_ps", [P, 2, D], F32))
        raw = [sb(f"raw{i}", [P, NF, P]) for i in range(RAW)]
        tps = [local.enter_context(nc.psum_tensor(f"tps{i}", [P, NF, P], F32)) for i in range(2)]
        spare = local.enter_context(nc.psum_tensor("spare", [P, 512], F32))
        pj = [local.enter_context(nc.psum_tensor(f"s_pj{i}", [P, 256], F32)) for i in range(2)]
        pj_in = sem("s_pj_in"); pj_kept = sem("s_pj_kept")
        ld = [sem(f"raw_in{i}") for i in range(RAW)]
        jobs_turned = sem("w_turned"); jobs_kept = sem("wt_kept")
        turned = sem("s_turned"); w_kept = sem("w_kept"); const = sem("s_const"); z_in = sem("z_in")
        inputs_in = sem("s_inputs"); pre_in = sem("s_pre_in"); gate_done = sem("s_gate"); leaked = sem("leaked")
        arg_done = sem("s_arg"); state = sem("s_state")

        def second(ap):
            return ap.rearrange("p (b two) -> p two b", two=2)[:, 1]

        with nc.Block() as block:

            @block.sync
            def _(sp):
                for j, (key, dst, e) in enumerate(jobs):
                    if j >= RAW:
                        sp.wait_ge(jobs_turned, j - RAW + 1)
                    src = a[key][e]
                    src = src.rearrange("(f p) h -> p f h", p=P) if dst is not wdT else src.rearrange("h (f i) -> h f i", i=P)
                    sp.dma_start(raw[j % RAW][:, :, :], src).then_inc(ld[j % RAW], 16)

            @block.gpsimd
            def _(pool):
                for q in range(4):
                    w = TOK // 4
                    out = pairs[:, 2 * w * q:2 * w * (q + 1)].rearrange("p (x two) -> p two x", two=2)[:, 0]
                    pool.tensor_copy(out, n.xT[:, w * q:w * q + w]).then_inc(z_in, 1)

            @block.tensor
            def _(pe):
                for i in range(2):
                    mm = nc.tensor.transpose(w_ps[:, i, :], n.l1w[:, D * i:D * i + D], n.ident[:, :])
                mm.then_inc(turned, 1)
                pe.wait_ge(w_kept, 1)
                pe.wait_ge(const, 2)

                def inputs(g):
                    if g >= 2:
                        pe.wait_ge(state, G * (g - 1) + 1)
                    w = B * G
                    nc.tensor.matmul(pre[g % 2][:, 0:w], wT[:, 1, :], n.xT[:, w * g:w * g + w], start=True, stop=False,
                                     skip_group_check=True)
                    nc.tensor.matmul(pre[g % 2][:, 0:w], n.b_l1[:, :], ones_w[:, :], start=False, stop=False,
                                     skip_group_check=True)

                inputs(0)
                for s in range(T):
                    pe.wait_ge(state, s + 1)
                    at = 8 * (s % G)
                    nc.tensor.matmul(pre[s // G % 2][:, at:at + P], wT[:, 0, :], s2[:, 8 * s:8 * s + P],
                                     start=False, stop=True, skip_group_check=True).then_inc(pre_in, 1)
                    if s % G == 4 and s // G + 1 < T // G:
                        inputs(s // G + 1)
                    j, k = divmod(s - 4, EVERY)
                    if k == 0 and 0 <= j < len(jobs):
                        pe.wait_ge(ld[j % RAW], 16 * (j // RAW + 1))
                        if j >= 2:
                            pe.wait_ge(jobs_kept, 2 * (j - 1))
                        for f in range(NF):
                            mm = nc.tensor.transpose(tps[j % 2][:, f, :], raw[j % RAW][:, f, :], n.ident[:, :])
                        mm.then_inc(jobs_turned, 1)
                    if s in plan:
                        i, kind, p, k = plan[s]
                        if i >= 2:
                            pe.wait_ge(pj_kept, i - 1)
                        if kind == "qk":
                            w = (n.wq12, n.wq12, n.wk12, n.wk12)[k]
                            c0 = B * (SPAN * p + 1)
                            mm = nc.tensor.matmul(pj[i % 2][:, :], w[:, D * (k % 2):D * (k % 2) + D],
                                                  s2[:, c0:c0 + B * SPAN], start=True, stop=True)
                        else:
                            for j in range(2):
                                states = s2[:, B:B + B * P].rearrange("p (t b) -> p b t", b=B)[:, 2 * k + j]
                                mm = nc.tensor.matmul(pj[i % 2][:, D * j:D * j + D], states, n.wv1[:, :], start=True, stop=True)
                        mm.then_inc(pj_in, 1)
                    for _ in range(FILL if s not in plan else FILL // 3):
                        nc.tensor.matmul(spare[:, 0:P], n.identb[:, :], n.identb[:, :], start=True, stop=True)

            @block.scalar
            def _(act):
                act.wait_ge(turned, 1)
                act.preload_act_table(ACT.Sigmoid)
                nc.scalar.activation(wT[:, :, :], w_ps[:, :, :], ACT.Copy).then_inc(w_kept, 1)
                act.wait_ge(const, 2)
                for s in range(T):
                    act.wait_ge(pre_in, s + 1)
                    nc.scalar.activation(second(gates[s % 2][:, :]), pre[s // G % 2][:, 8 * (s % G):8 * (s % G) + 8],
                                         ACT.Sigmoid).then_inc(gate_done, 1)
                    act.wait_ge(arg_done, s + 1)
                    nc.scalar.activation(s2[:, 8 * s + 8:8 * s + 16], second(targ[s % 2][:, :]), ACT.Tanh).then_inc(state, 1)
                    j, k = divmod(s - 5, EVERY)
                    if k < 2 and 0 <= j < len(jobs):
                        dst, e = jobs[j][1:]
                        act.wait_ge(jobs_turned, j + 1)
                        out = wdT[:, e, :, :] if dst is wdT else dst[:, e, :].rearrange("p (f h) -> p f h", h=P)
                        nc.scalar.activation(out[:, 2 * k:2 * k + 2], tps[j % 2][:, 2 * k:2 * k + 2, :], ACT.Copy).then_inc(jobs_kept, 1)
                    if s - 1 in plan:
                        i, kind, p, k = plan[s - 1]
                        act.wait_ge(pj_in, i + 1)
                        if kind == "qk":
                            out = qk[:, k, :].rearrange("p (b t) -> p t b", b=B)[:, SPAN * p:SPAN * p + SPAN]
                            src = pj[i % 2][:, :].rearrange("p (t b) -> p t b", b=B)
                        else:
                            out = vt.rearrange("p (b s) d -> p s b d", s=T // P)[:, 0, 2 * k:2 * k + 2, :]
                            src = pj[i % 2][:, :].rearrange("p (b d) -> p b d", d=D)
                        nc.scalar.activation(out, src, ACT.Copy).then_inc(pj_kept, 1)

            @block.vector
            def _(dve):
                al = ROWS["alpha"][0]
                for i in range(2):
                    nc.vector.memset(gates[i][:, :], 0.0)
                nc.vector.tensor_scalar(leak[:, :], n.cols[:, al:al + 1], -1.0, 1.0, ALU.mult, ALU.add).then_inc(const, 1)
                nc.vector.memset(ones_w[:, :], 1.0)
                nc.vector.memset(s2[:, :], 0.0).then_inc(const, 1)
                dve.wait_ge(const, 2)
                nc.vector.tensor_copy(s2[:, 0:8], n.condT).then_inc(state, 1)
                for s in range(T):
                    if s % (T // 4) == 0:
                        dve.wait_ge(z_in, s // (T // 4) + 1)
                    dve.wait_ge(state, s + 1)
                    pair = pairs[:, 16 * s:16 * s + 16]
                    nc.vector.tensor_scalar(second(pair), s2[:, 8 * s:8 * s + 8], leak[:, 0:1], None, ALU.mult).then_inc(leaked, 1)
                    dve.wait_ge(leaked, s + 1)
                    dve.wait_ge(gate_done, s + 1)
                    nc.vector.tensor_tensor_scan(targ[s % 2][:, :], gates[s % 2][:, :], pair, 0.0,
                                                 ALU.mult, ALU.add).then_inc(arg_done, 1)


def diff_attention(nc, n, s2, qk, vt):
    SPAN = 32
    SCALE = float(D) ** -0.25
    EPS, LAMBDA_INIT = 1e-5, 0.8
    SEG = T // P
    UNITS = B * SEG
    with ExitStack() as local:
        def sb(name, shape, dt=F32):
            return local.enter_context(nc.sbuf_tensor(name, shape, dt))

        def ps(name, shape):
            return local.enter_context(nc.psum_tensor(name, shape, F32))

        def sem(name):
            return local.enter_context(nc.semaphore(name))

        lam2 = sb("lam2", [P, 2]); lam = sb("lam", [P, 1]); lq = sb("lq", [P, 2, P])
        negmax = [sb(f"negmax{i}", [P, 2]) for i in range(2)]
        sums = [sb(f"sums{i}", [P, 2]) for i in range(2)]
        inv = [sb(f"inv{i}", [P, 2]) for i in range(2)]
        probs = [sb(f"probs{i}", [P, 2, T]) for i in range(2)]
        diff = [sb(f"diff{i}", [P, T]) for i in range(2)]
        diffT = [sb(f"diffT{i}", [P, SEG, P]) for i in range(2)]
        heads = sb("heads", [P, UNITS, D])
        junk = sb("d_junk", [P, D])
        squares = sb("squares", [P, UNITS])
        rms = sb("rms", [P, UNITS]); unit = sb("unit", [P, UNITS]); eps = sb("d_eps", [P, 1])
        pj = [ps(f"dpj{i}", [P, 512]) for i in range(2)]
        s_ps = [ps(f"s_ps{i}", [P, 2, T]) for i in range(2)]
        t_ps = [ps(f"dt_ps{i}", [P, SEG, P]) for i in range(2)]
        o_ps = [ps(f"o_ps{i}", [P, D]) for i in range(2)]
        pj_in = sem("d_pj_in"); pj_kept = sem("d_pj_kept"); pre = sem("d_pre")
        lam_in = sem("lam_in"); lam_exp = sem("lam_exp"); lam_done = sem("lam_done")
        s_in = sem("d_s"); max_done = sem("d_max"); exp_done = sem("d_exp"); link = sem("d_link"); diff_done = sem("d_diff")
        t_in = sem("d_t"); t_kept = sem("d_t_kept"); o_in = sem("d_o"); o_kept = sem("d_o_kept"); sq_done = sem("d_sq")
        rms_done = sem("d_rms"); unit_done = sem("d_unit"); normed = sem("d_normed"); back_in = sem("d_back"); added = sem("d_added")

        with nc.Block() as block:

            @block.tensor
            def _(pe):
                pe.wait_ge(pre, 1)
                for i, row in enumerate(("lk1", "lk2")):
                    r0 = ROWS[row][0]
                    mm = nc.tensor.matmul(o_ps[0][:, i:i + 1], lq[:, i, :], n.cols[:, r0:r0 + 1], start=True, stop=True)
                mm.then_inc(lam_in, 1)
                for g in range(6):
                    if g >= 2:
                        pe.wait_ge(pj_kept, g - 1)
                    for i in range(2):
                        if g < 2:
                            w, c0 = (n.wq12, n.wk12)[g], B * (T - SPAN + 1)
                            mm = nc.tensor.matmul(pj[g % 2][:, 256 * i:256 * i + 256], w[:, D * i:D * i + D],
                                                  s2[:, c0:c0 + B * SPAN], start=True, stop=True)
                        else:
                            states = s2[:, B * (P + 1):B * (T + 1)].rearrange("p (t b) -> p b t", b=B)[:, 2 * (g - 2) + i]
                            mm = nc.tensor.matmul(pj[g % 2][:, D * i:D * i + D], states, n.wv1[:, :], start=True, stop=True)
                    mm.then_inc(pj_in, 1)
                pe.wait_ge(pj_kept, 6)

                def scores(u):
                    b, i = divmod(u, SEG)
                    if u >= 2:
                        pe.wait_ge(exp_done, 2 * (u - 1))
                    for m in range(2):
                        mm = nc.tensor.matmul(s_ps[u % 2][:, m, :], qk[:, m, P * u:P * u + P],
                                              qk[:, 2 + m, T * b:T * b + T], start=True, stop=True)
                    mm.then_inc(s_in, 1)

                def turn(u):
                    pe.wait_ge(diff_done, u + 1)
                    if u >= 2:
                        pe.wait_ge(t_kept, u - 1)
                    for i in range(SEG):
                        mm = nc.tensor.transpose(t_ps[u % 2][:, i, :], diff[u % 2][:, P * i:P * i + P], n.ident[:, :])
                    mm.then_inc(t_in, 1)

                def attend(u):
                    pe.wait_ge(t_kept, u + 1)
                    if u >= 2:
                        pe.wait_ge(o_kept, u - 1)
                        pe.wait_ge(sq_done, u - 1)
                    for i in range(SEG):
                        mm = nc.tensor.matmul(o_ps[u % 2][:, :], diffT[u % 2][:, i, :], vt[:, u // SEG * SEG + i, :],
                                              start=(i == 0), stop=(i == SEG - 1))
                    mm.then_inc(o_in, 1)

                pe.wait_ge(lam_exp, 1)
                scores(0)
                scores(1)
                for u in range(UNITS + 1):
                    if u + 2 < UNITS:
                        scores(u + 2)
                    if u >= 1:
                        attend(u - 1)
                    if u < UNITS:
                        turn(u)
                for g in range(4):
                    pe.wait_ge(normed, 4 * (g + 1))
                    if g >= 2:
                        pe.wait_ge(added, g - 1)
                    for i in range(4):
                        mm = nc.tensor.transpose(pj[g % 2][:, P * i:P * i + P], heads[:, 4 * g + i, :], n.ident[:, :])
                    mm.then_inc(back_in, 1)

            @block.scalar
            def _(act):
                act.wait_ge(lam_in, 1)
                nc.scalar.activation(lam2[:, :], o_ps[0][:, 0:2], ACT.Exp).then_inc(lam_exp, 1)
                for g in range(6):
                    act.wait_ge(pj_in, g + 1)
                    if g < 2:
                        out = qk[:, 2 * g:2 * g + 2, :].rearrange("p k (b t) -> p k t b", b=B)[:, :, T - SPAN:T]
                        for i in range(2):
                            last = nc.scalar.activation(out[:, i], pj[g % 2][:, 256 * i:256 * i + 256].rearrange("p (t b) -> p t b", b=B), ACT.Copy)
                    else:
                        out = vt.rearrange("p (b s) d -> p s b d", s=SEG)[:, 1, 2 * (g - 2):2 * (g - 2) + 2, :]
                        last = nc.scalar.activation(out, pj[g % 2][:, 0:256].rearrange("p (b d) -> p b d", d=D), ACT.Copy)
                    last.then_inc(pj_kept, 1)

                def exps(u):
                    act.wait_ge(max_done, u + 1)
                    if u >= 2:
                        act.wait_ge(diff_done, u - 1)
                    for m in range(2):
                        nc.scalar.activation(probs[u % 2][:, m, :], s_ps[u % 2][:, m, :], ACT.Exp,
                                             bias=negmax[u % 2][:, m:m + 1], scale=SCALE,
                                             accum_out=sums[u % 2][:, m:m + 1]).then_inc(exp_done, 1)

                def keep(u):
                    act.wait_ge(t_in, u + 1)
                    if u >= 2:
                        act.wait_ge(o_in, u - 1)
                    nc.scalar.activation(diffT[u % 2][:, :, :], t_ps[u % 2][:, :, :], ACT.Copy).then_inc(t_kept, 1)

                exps(0)
                for u in range(UNITS):
                    if u + 1 < UNITS:
                        exps(u + 1)
                    keep(u)
                    if u >= 1:
                        act.wait_ge(o_kept, u)
                        if u >= 2:
                            act.wait_ge(sq_done, u - 1)
                        nc.scalar.activation(junk[:, :], heads[:, u - 1, :], ACT.Square,
                                             accum_out=squares[:, u - 1:u]).then_inc(sq_done, 1)
                act.wait_ge(o_kept, UNITS)
                act.wait_ge(sq_done, UNITS - 1)
                nc.scalar.activation(junk[:, :], heads[:, UNITS - 1, :], ACT.Square,
                                     accum_out=squares[:, UNITS - 1:UNITS]).then_inc(sq_done, 1)
                act.wait_ge(sq_done, UNITS)
                nc.scalar.activation(rms[:, :], squares[:, :], ACT.Sqrt, bias=eps[:, 0:1], scale=1.0 / D).then_inc(rms_done, 1)

            @block.vector
            def _(dve):
                V = nc.vector
                for i, row in enumerate(("lq1", "lq2")):
                    r0 = ROWS[row][0]
                    last = V.tensor_copy(lq[:, i, :], n.cols[:, r0:r0 + 1].broadcast_to([P, P]))
                last.then_inc(pre, 1)
                V.memset(eps[:, :], EPS)
                dve.wait_ge(lam_exp, 1)
                V.tensor_tensor(lam[:, :], lam2[:, 1:2], lam2[:, 0:1], ALU.subtract).then_inc(lam_done, 1)
                dve.wait_ge(lam_done, 1)
                V.tensor_scalar(lam[:, :], lam[:, :], -LAMBDA_INIT, None, ALU.add).then_inc(lam_done, 1)
                dve.wait_ge(lam_done, 2)

                def maxima(u):
                    dve.wait_ge(s_in, u + 1)
                    if u >= 2:
                        dve.wait_ge(exp_done, 2 * (u - 1))
                    V.tensor_reduce(negmax[u % 2][:, :], s_ps[u % 2][:, :, :], AX.X, ALU.max).then_inc(link, 1)
                    dve.wait_ge(link, u + 1)
                    V.tensor_scalar(negmax[u % 2][:, :], negmax[u % 2][:, :], -SCALE, None, ALU.mult).then_inc(max_done, 1)

                def difference(u):
                    p = u % 2
                    dve.wait_ge(exp_done, 2 * (u + 1))
                    V.reciprocal(inv[p][:, :], sums[p][:, :]).then_inc(unit_done, 1)
                    dve.wait_ge(unit_done, 3 * u + 1)
                    V.tensor_tensor(inv[p][:, 1:2], inv[p][:, 1:2], lam[:, :], ALU.mult).then_inc(unit_done, 1)
                    if u >= 2:
                        dve.wait_ge(t_in, u - 1)
                    dve.wait_ge(unit_done, 3 * u + 2)
                    V.tensor_scalar(diff[p][:, :], probs[p][:, 0, :], inv[p][:, 0:1], None, ALU.mult).then_inc(unit_done, 1)
                    dve.wait_ge(unit_done, 3 * u + 3)
                    V.scalar_tensor_tensor(diff[p][:, :], probs[p][:, 1, :], inv[p][:, 1:2], diff[p][:, :],
                                           ALU.mult, ALU.add).then_inc(diff_done, 1)

                def keep(u):
                    dve.wait_ge(o_in, u + 1)
                    V.tensor_copy(heads[:, u, :], o_ps[u % 2][:, :]).then_inc(o_kept, 1)

                maxima(0)
                for u in range(UNITS):
                    if u + 1 < UNITS:
                        maxima(u + 1)
                    difference(u)
                    if u >= 1:
                        keep(u - 1)
                keep(UNITS - 1)
                dve.wait_ge(rms_done, 1)
                V.reciprocal(unit[:, :], rms[:, :]).then_inc(link, 1)
                dve.wait_ge(link, UNITS + 1)
                for u in range(UNITS):
                    V.tensor_scalar(heads[:, u, :], heads[:, u, :], unit[:, u:u + 1], 1.0 - LAMBDA_INIT,
                                    ALU.mult, ALU.mult).then_inc(normed, 1)
                for g in range(4):
                    dve.wait_ge(back_in, g + 1)
                    x = n.xT[:, :].rearrange("p (t b) -> p b t", b=B)[:, 2 * g:2 * g + 2]
                    V.tensor_tensor(x, pj[g % 2][:, :].rearrange("p (b t) -> p b t", b=2), x, ALU.add).then_inc(added, 1)


def modulated_linear(nc, n, mB, comb):
    EPS = 1e-8
    SCALE = float(D) ** -0.5
    wide = [P, NBLK, E]
    with ExitStack() as local:
        def sb(name, shape, dt=F32):
            return local.enter_context(nc.sbuf_tensor(name, shape, dt))

        def sem(name):
            return local.enter_context(nc.semaphore(name))

        ys, ys2 = sb("ys", [P, B]), sb("ys2", [P, B])
        w2, eps, dd, dr = sb("w2", [P, D]), sb("m_eps", [P, 1]), sb("dd", [P, B]), sb("dr", [P, B])
        xs = sb("xs", [P, TOK])
        val, mark, one, two = (sb(k, wide) for k in ("m_val", "m_mark", "m_one", "m_two"))
        v1, v2, first, pa, pb = (sb(k, [P, NBLK]) for k in ("m_v1", "m_v2", "m_first", "m_pa", "m_pb"))
        iota_m8 = sb("m_iota", [P, E])
        d_ps = local.enter_context(nc.psum_tensor("d_ps", [P, B], F32))
        m_ps = [local.enter_context(nc.psum_tensor(f"m_ps{i}", [P, 512], F32)) for i in range(2)]
        g_ps = local.enter_context(nc.psum_tensor("g_ps", wide, F32))
        step = sem("m_step"); d_in = sem("m_d"); sq = sem("m_sq"); lin = sem("m_lin"); kept = sem("m_kept"); gates_in = sem("m_gates")
        exp_in = sem("m_exp")

        with nc.Block() as block:

            @block.tensor
            def _(pe):
                pe.wait_ge(step, 5)
                nc.tensor.matmul(d_ps[:, :], w2[:, :], ys2[:, :], start=True, stop=True).then_inc(d_in, 1)
                pe.wait_ge(step, 6)
                for g in range(4):
                    if g >= 2:
                        pe.wait_ge(kept, g - 1)
                    nc.tensor.matmul(m_ps[g % 2][:, :], n.wmod[:, :], xs[:, 512 * g:512 * g + 512], start=True, stop=True).then_inc(lin, 1)
                g0 = ROWS["gate"][0]
                pe.wait_ge(kept, 4)
                for i in range(NBLK):
                    mm = nc.tensor.matmul(g_ps[:, i, :], mB[:, P * i:P * i + P], n.cols[:, g0:g0 + E], start=True, stop=True)
                mm.then_inc(gates_in, 1)

            @block.scalar
            def _(act):
                act.wait_ge(d_in, 1)
                nc.scalar.activation(dd[:, :], d_ps[:, :], ACT.Sqrt, bias=eps[:, 0:1]).then_inc(sq, 1)
                act.wait_ge(exp_in, 1)
                nc.scalar.activation(pb[:, :], pa[:, :], ACT.Exp).then_inc(sq, 1)

            @block.vector
            def _(dve):
                V = nc.vector
                at = [0]

                def done(ins):
                    at[0] += 1
                    ins.then_inc(step, 1)
                    dve.wait_ge(step, at[0])

                def per_token(ap):
                    return ap[:, :].unsqueeze(2).broadcast_to(wide)

                done(V.memset(eps[:, :], EPS))
                done(V.tensor_scalar(iota_m8[:, :], n.iota8[:, :], -float(E), None, ALU.add))
                done(V.tensor_scalar(ys[:, :], n.condT, SCALE, None, ALU.mult))
                done(V.tensor_tensor(ys2[:, :], ys[:, :], ys[:, :], ALU.mult))
                done(V.tensor_tensor(w2[:, :], n.wmod[:, :], n.wmod[:, :], ALU.mult))
                steps = [P, T, B]
                done(V.tensor_tensor(xs[:, :].rearrange("p (t b) -> p t b", b=B), n.xT[:, :].rearrange("p (t b) -> p t b", b=B),
                                     ys[:, :].unsqueeze(1).broadcast_to(steps), ALU.mult))
                dve.wait_ge(sq, 1)
                done(V.reciprocal(dr[:, :], dd[:, :]))
                for g in range(4):
                    dve.wait_ge(lin, g + 1)
                    w = 512 // B
                    out = mB[:, :].rearrange("p (b t) -> p t b", b=B)[:, w * g:w * g + w]
                    V.tensor_tensor(out, m_ps[g % 2][:, :].rearrange("p (t b) -> p t b", b=B),
                                    dr[:, :].unsqueeze(1).broadcast_to([P, w, B]), ALU.mult).then_inc(kept, 1)
                dve.wait_ge(gates_in, 1)
                ramp = iota_m8[:, :].unsqueeze(1).broadcast_to(wide)
                done(V.tensor_copy(val[:, :, :], g_ps[:, :, :]))

                def take_largest(top, onehot):
                    done(V.tensor_reduce(top[:, :], val[:, :, :], AX.X, ALU.max))
                    done(V.tensor_tensor(mark[:, :, :], val[:, :, :], per_token(top), ALU.is_equal))
                    done(V.tensor_tensor(mark[:, :, :], mark[:, :, :], ramp, ALU.mult))
                    done(V.tensor_reduce(first[:, :], mark[:, :, :], AX.X, ALU.min))
                    done(V.tensor_tensor(onehot[:, :, :], ramp, per_token(first), ALU.is_equal))

                take_largest(v1, one)
                done(V.scalar_tensor_tensor(val[:, :, :].rearrange("p i e -> p (i e)"),
                                            one[:, :, :].rearrange("p i e -> p (i e)"), -3.0e38,
                                            val[:, :, :].rearrange("p i e -> p (i e)"), ALU.mult, ALU.add))
                take_largest(v2, two)
                V.tensor_tensor(pa[:, :], v2[:, :], v1[:, :], ALU.subtract).then_inc(exp_in, 1)
                dve.wait_ge(sq, 2)
                done(V.tensor_scalar(v1[:, :], pb[:, :], 1.0, None, ALU.add))
                done(V.reciprocal(pa[:, :], v1[:, :]))
                done(V.tensor_tensor(pb[:, :], pb[:, :], pa[:, :], ALU.mult))
                done(V.tensor_tensor(one[:, :, :], one[:, :, :], per_token(pa), ALU.mult))
                done(V.tensor_tensor(two[:, :, :], two[:, :, :], per_token(pb), ALU.mult))
                done(V.tensor_tensor(comb[:, :, :], one[:, :, :], two[:, :, :], ALU.add))


def program(nc, a, out):
    with ExitStack() as ctx:
        n = allocate(nc, ctx)
        with ExitStack() as mid:
            yB = mid.enter_context(nc.sbuf_tensor("yB", [P, TOK], F32))
            wqkv = mid.enter_context(nc.sbuf_tensor("wqkv", [P, 3 * INNER], F32))
            wout = mid.enter_context(nc.sbuf_tensor("wout", [P, NC, D], F32))
            with ExitStack() as early:
                wq, wk, wv = (early.enter_context(nc.sbuf_tensor(k, [P, INNER], F32)) for k in ("wq", "wk", "wv"))
                wo = early.enter_context(nc.sbuf_tensor("wo", [P, NC, D], F32))
                setup(nc, n, a, wq, wk, wv, wo)
                local_attention(nc, n, a, yB, wq, wk, wv, wo, wqkv, wout)
            linear_attention(nc, n, yB, wqkv, wout)
        with ExitStack() as mid:
            w1 = mid.enter_context(nc.sbuf_tensor("w1", [P, E, FF], F32))
            w2 = mid.enter_context(nc.sbuf_tensor("w2e", [P, E, NF, D], F32))
            load_experts(nc, n, a, w1, w2)
            hist = mid.enter_context(nc.sbuf_tensor("hist", [P, 16 * (T + P // B)], F32))
            diffT = mid.enter_context(nc.sbuf_tensor("expert_diff", [P, TOK], F32))
            gru_scan(nc, n, hist, w1, w2, diffT)
            route_top1(nc, n, hist, diffT)
        wgT = ctx.enter_context(nc.sbuf_tensor("wgT", [P, E, FF], F32))
        wuT = ctx.enter_context(nc.sbuf_tensor("wuT", [P, E, FF], F32))
        wdT = ctx.enter_context(nc.sbuf_tensor("wdT", [P, E, NF, D], F32))
        with ExitStack() as mid:
            s2 = mid.enter_context(nc.sbuf_tensor("s2", [P, TOK + P], F32))
            qk = mid.enter_context(nc.sbuf_tensor("qk", [P, 4, TOK], F32))
            vt = mid.enter_context(nc.sbuf_tensor("vt", [P, NBLK, D], F32))
            gate_scan(nc, n, a, s2, qk, vt, wgT, wuT, wdT)
            diff_attention(nc, n, s2, qk, vt)
        mB = ctx.enter_context(nc.sbuf_tensor("mB", [P, TOK], F32))
        comb = ctx.enter_context(nc.sbuf_tensor("comb", [P, NBLK, E], F32))
        modulated_linear(nc, n, mB, comb)
        experts(nc, n, 1, mB, comb, (wgT, wuT), wdT, out)


def load_experts(nc, n, a, w1, w2):
    done = n.load_experts
    with nc.Block() as block:
        @block.sync
        def _(sp):
            sp.dma_start(w1[:, :, :], a["L0_ffn_W1"].rearrange("e d f -> d e f")).then_inc(done, 16)
            sp.dma_start(w2[:, :, :, :], a["L0_ffn_W2"].rearrange("e (f p) d -> p e f d", p=P)).then_inc(done, 16)


def kernel(**inputs):
    import numpy as np
    import concourse.bacc as bacc
    from concourse.bass_utils import run_bass_kernel_spmd

    nc = bacc.Bacc("TRN2", target_bir_lowering=False, num_devices=1)
    arrays, aps = {}, {}
    for name, value in inputs.items():
        arrays[f"in_{name}"] = np.ascontiguousarray(value)
        aps[name] = nc.dram_tensor(f"in_{name}", arrays[f"in_{name}"].shape, F32, kind="ExternalInput").ap()
    out = nc.dram_tensor("out", (B, T, D), F32, kind="ExternalOutput").ap()
    program(nc, aps, out)
    result = run_bass_kernel_spmd(nc, [arrays], core_ids=[0])
    return result.results[0]["out"]
```

```python
from contextlib import ExitStack

import concourse.bass as bass
from concourse import mybir

F32 = mybir.dt.float32
BF16 = mybir.dt.bfloat16
I32 = mybir.dt.int32
ACT = mybir.ActivationFunctionType
ALU = mybir.AluOpType
AX = mybir.AxisListType

P = 128
B, T, D = 8, 256, 128
TOK = B * T
NBLK = TOK // P
HEADS, HD = 16, 64
INNER = HEADS * HD
NC = INNER // P
E = 8
FF = 512
NF = FF // P
CAPACITY = -(-TOK * 5 // (E * 4))

ROWS = {}
_at = 0
for _name, _count in (("bq", NC), ("bk", NC), ("bv", NC), ("bo", 1), ("bout", 1), ("alpha", 1),
                      ("lq1", 1), ("lk1", 1), ("lq2", 1), ("lk2", 1), ("b1", E * NF), ("cond", B),
                      ("router", E), ("gate", E), ("b2_0", 1)):
    ROWS[_name] = (_at, _count)
    _at += _count
NROWS = _at


class Net:
    pass


def allocate(nc, ctx):
    n = Net()

    def sb(name, shape, dt=F32):
        return ctx.enter_context(nc.sbuf_tensor(name, shape, dt))

    n.sb = sb
    n.xT = sb("xT", [P, TOK])
    n.cols = sb("cols", [P, P])
    n.ident = sb("ident", [P, P])
    n.identb = sb("identb", [P, P], BF16)
    n.gru_w = sb("gru_w", [P, 6, P])
    n.gru_b = sb("gru_b", [1, 4, P])
    n.ones_row = sb("ones_row", [1, P])
    n.b_l1 = sb("b_l1", [1, P])
    n.l1w = sb("l1w", [P, 2 * D])
    n.wq12 = sb("wq12", [P, 2 * D])
    n.wk12 = sb("wk12", [P, 2 * D])
    n.wv1 = sb("wv1", [P, D])
    n.wmod = sb("wmod", [P, D])
    n.b2 = sb("b2", [E, D])
    n.iota8 = sb("iota8", [P, E])
    n.ys, n.dr = sb("ys", [P, B]), sb("dr", [P, B])
    n.condT = n.cols[:, ROWS["cond"][0]:ROWS["cond"][0] + B]

    n.load_small = ctx.enter_context(nc.semaphore("load_small"))
    n.load_x = ctx.enter_context(nc.semaphore("load_x"))
    n.load_local = ctx.enter_context(nc.semaphore("load_local"))
    n.load_later = ctx.enter_context(nc.semaphore("load_later"))
    n.load_experts = ctx.enter_context(nc.semaphore("load_experts"))
    n.load_linear = ctx.enter_context(nc.semaphore("load_linear"))
    n.later_loads = 16 * 17
    return n


def setup(nc, n, a, wq, wk, wv, wo):
    small = [("bq", a["L0_cond_WQ_b"]), ("bk", a["L0_cond_WK_b"]), ("bv", a["L0_cond_WV_b"]),
             ("bo", a["L0_cond_WO_b"]), ("bout", a["L0_attn_bout"]), 
             ("alpha", a["L1_cond_alpha"]), ("lq1", a["L1_attn_lambda_q1"]), ("lk1", a["L1_attn_lambda_k1"]),
             ("lq2", a["L1_attn_lambda_q2"]), ("lk2", a["L1_attn_lambda_k2"])]
    with ExitStack() as local:
        def sem(name):
            return local.enter_context(nc.semaphore(name))

        rows_done = sem("rows_done"); ident_base = sem("ident_base"); ident_done = sem("ident_done")
        x_turned = sem("x_turned"); x_kept = sem("x_kept")
        rows = local.enter_context(nc.sbuf_tensor("rows", [NROWS, P], F32))
        xtok = local.enter_context(nc.sbuf_tensor("xtok", [P, NBLK, D], F32))
        turn = [local.enter_context(nc.psum_tensor(f"turn{i}", [P, 4, P], F32)) for i in range(2)]
        turn_rows = local.enter_context(nc.psum_tensor("turn_rows", [P, NROWS], F32))
        with nc.Block() as block:

            @block.sync
            def _(sp):
                for name, src in small:
                    r0, k = ROWS[name]
                    sp.dma_start(rows[r0:r0 + k, :], src.rearrange("(r d) -> r d", d=P)).then_inc(n.load_small, 16)
                r0, k = ROWS["b1"]
                sp.dma_start(rows[r0:r0 + k, :], a["L0_ffn_b1"].rearrange("e (c f) -> (e c) f", f=P)).then_inc(n.load_small, 16)
                for name, src in (("cond", "cond_1024"), ("router", "L0_ffn_router_w"), ("gate", "L1_ffn_gate_w")):
                    r0, k = ROWS[name]
                    sp.dma_start(rows[r0:r0 + k, :], a[src]).then_inc(n.load_small, 16)
                r0 = ROWS["b2_0"][0]
                sp.dma_start(rows[r0:r0 + 1, :], a["L0_ffn_b2"][0:1, :]).then_inc(n.load_small, 16)

            @block.scalar
            def _(act):
                act.dma_start(xtok[:, :, :], a["x"].rearrange("b (i p) d -> p (b i) d", p=P)).then_inc(n.load_x, 16)
                for dst, key in ((wk, "L0_cond_WK_w"), (wv, "L0_cond_WV_w"), (wq, "L0_cond_WQ_w")):
                    act.dma_start(dst[:, :], a[key]).then_inc(n.load_local, 16)
                act.dma_start(wo[:, :, :], a["L0_cond_WO_w"].rearrange("(c p) d -> p c d", p=P)).then_inc(n.load_local, 16)
                for g in range(NBLK // 4):
                    act.wait_ge(x_turned, g + 1)
                    out = n.xT[:, :].rearrange("p (i t b) -> p b i t", i=2, b=B)[:, 2 * g:2 * g + 2]
                    nc.scalar.activation(out, turn[g % 2][:, :, :].rearrange("p (b i) t -> p b i t", i=2),
                                         ACT.Copy).then_inc(x_kept, 1)
                act.wait_ge(rows_done, 1)
                nc.scalar.activation(n.cols[:, 0:NROWS], turn_rows[:, :], ACT.Copy)

            @block.gpsimd
            def _(pool):
                pool.memset(n.ident[:, :], 0.0).then_inc(ident_base, 1)
                pool.wait_ge(ident_base, 1)
                pool.affine_select(out=n.ident[:, :], in_=n.ident[:, :], compare_op=ALU.not_equal, fill=1.0,
                                   base=0, pattern=[[-1, P]], channel_multiplier=1).then_inc(ident_done, 1)
                pool.wait_ge(ident_done, 1)
                pool.tensor_copy(n.identb[:, :], n.ident[:, :])
                for e in range(E):
                    pool.memset(n.iota8[:, e:e + 1], float(e))
                pool.memset(n.ones_row[:, :], 1.0)
                pool.memset(n.cols[:, NROWS:P], 0.0)

            @block.tensor
            def _(pe):
                pe.wait_ge(ident_done, 1)
                pe.wait_ge(n.load_x, 16)
                for g in range(NBLK // 4):
                    if g >= 2:
                        pe.wait_ge(x_kept, g - 1)
                    for i in range(4):
                        mm = nc.tensor.transpose(turn[g % 2][:, i, :], xtok[:, 4 * g + i, :], n.ident[:, :])
                    mm.then_inc(x_turned, 1)
                pe.wait_ge(n.load_small, 16 * (len(small) + 5))
                nc.tensor.transpose(turn_rows[:, :], rows[:, :], n.ident[0:NROWS, 0:NROWS]).then_inc(rows_done, 1)


def local_attention(nc, n, a, yB, wq, wk, wv, wo, wqkv, wout):
    HALF = TOK // 2
    HB = HALF // P
    SH = B
    KW = HALF + 2 * SH
    UNITS = 2 * NC
    J = 4
    with ExitStack() as local:
        def sb(name, shape, dt=F32):
            return local.enter_context(nc.sbuf_tensor(name, shape, dt))

        def sem(name):
            return local.enter_context(nc.semaphore(name))

        bq8 = sb("bq8", [P, NC])
        headsel = sb("headsel", [P, 2 * P])
        pick = sb("pick", [24, J, 2, HD], BF16)
        akT, avT = sb("akT", [P, NC, B]), sb("avT", [P, NC, B])
        qb = [sb(f"qb{i}", [P, HALF]) for i in range(4)]
        kb = [sb(f"kb{i}", [P, KW + SH]) for i in range(4)]
        prod = [sb(f"prod{i}", [P, J, HALF]) for i in range(2)]
        s_max, s_sum, s_rec = (sb(k, [P, HB * 2]) for k in ("s_max", "s_sum", "s_rec"))
        s_sh, s_exp, prob, rest1, rest2 = (sb(k, [P, HB * 2, J]) for k in ("s_sh", "s_exp", "prob", "rest1", "rest2"))
        parts = [sb(f"parts{i}", [P, HB, 3, 2 * J], BF16) for i in range(2)]
        probT = [sb(f"probT{i}", [24, HALF], BF16) for i in range(2)]
        term = [sb(f"term{i}", [P, J, 512]) for i in range(2)]
        pair = [sb(f"pair{i}", [P, 2, 512]) for i in range(2)]
        att = [sb(f"att{i}", [P, 512]) for i in range(2)]
        y_ps = [local.enter_context(nc.psum_tensor(f"y_ps{i}", [P, 512], F32)) for i in range(2)]
        pj = [local.enter_context(nc.psum_tensor(f"pj{i}", [P, 512], F32)) for i in range(2)]
        bc = [local.enter_context(nc.psum_tensor(f"bc{i}", [P, 512], F32)) for i in range(2)]
        sc = local.enter_context(nc.psum_tensor("sc", [P, P // (2 * J), J, 2], F32))
        tr = local.enter_context(nc.psum_tensor("tr", [24, HALF], BF16))

        const_a = sem("const_a"); const_done = sem("const_done")
        cond_proj = sem("cond_proj"); cond_kept = sem("cond_kept")
        proj_done = sem("proj_done"); proj_kept = sem("proj_kept")
        prod_v = sem("prod_v"); prod_g = sem("prod_g")
        score_done = sem("score_done"); soft = sem("soft"); exp_done = sem("exp_done")
        parts_done = sem("parts_done"); turned = sem("turned"); turned_kept = sem("turned_kept")
        spread = sem("spread"); term_done = sem("term_done"); pair_done = sem("pair_done"); att_done = sem("att_done")
        y_part = sem("y_part"); y_kept = sem("y_kept")

        def pieces(u):
            h, c = divmod(u, NC)
            t0 = h * HALF
            k0 = 0 if h == 0 else t0 - SH
            return ([("q", t0, 0, 512), ("q", t0 + 512, 512, 512)]
                    + [("k", k0, SH, 512), ("k", k0 + 512, SH + 512, 512), ("k", k0 + 1024, SH + 1024, SH)])

        def key(u, j, at, width):
            base = (u // NC) * SH + (j - 1) * SH + at
            return kb[u % 4][:, base:base + width]

        with nc.Block() as block:

            @block.sync
            def _(sp):
                sp.dma_start(wqkv[:, :], a["L0_attn_Wqkv"]).then_inc(n.load_linear, 16)
                sp.dma_start(wout[:, :, :], a["L0_attn_Wout"].rearrange("(c p) d -> p c d", p=P)).then_inc(n.load_linear, 16)
                for i, key in enumerate(("L0_cond2_W_ir", "L0_cond2_W_iz", "L0_cond2_W_in",
                                         "L0_cond2_W_hr", "L0_cond2_W_hz", "L0_cond2_W_hn")):
                    sp.dma_start(n.gru_w[:, i, :], a[key]).then_inc(n.load_later, 16)
                for i, key in enumerate(("L0_cond2_b_hn", "L0_cond2_b_ir", "L0_cond2_b_iz", "L0_cond2_b_in")):
                    sp.dma_start(n.gru_b[:, i, :], a[key].rearrange("(r d) -> r d", r=1)).then_inc(n.load_later, 16)
                sp.dma_start(n.b_l1[:, :], a["L1_cond_b"].rearrange("(r d) -> r d", r=1)).then_inc(n.load_later, 16)
                for dst, key in ((n.l1w, "L1_cond_W"), (n.wq12, "L1_attn_w_q12"), (n.wk12, "L1_attn_w_k12"),
                                 (n.wv1, "L1_attn_w_v"), (n.wmod, "L1_cond2_weight"), (n.b2, "L0_ffn_b2")):
                    sp.dma_start(dst[:, :], a[key]).then_inc(n.load_later, 16)

            @block.gpsimd
            def _(pool):
                pool.memset(pick[:, :, :, :], 0.0).then_inc(const_a, 1)
                for part in range(3):
                    pool.wait_ge(const_a, part + 1)
                    pool.affine_select(out=pick[:, :, :, :], in_=pick[:, :, :, :], compare_op=ALU.not_equal, fill=1.0,
                                       base=-8 * part, pattern=[[-1, J], [-J, 2], [0, HD]],
                                       channel_multiplier=1).then_inc(const_a, 1)

                def product(u, j):
                    pool.wait_ge(proj_kept, 5 * (u + 1))
                    if u >= 2:
                        pool.wait_ge(score_done, u - 1)
                    pool.tensor_tensor(prod[u % 2][:, j, :], qb[u % 4][:, :], key(u, j, 0, HALF),
                                       ALU.mult).then_inc(prod_g, 1)

                def pair_sum(u, m):
                    s = 2 * u + m
                    pool.wait_ge(term_done, J * (s + 1))
                    if s >= 2:
                        pool.wait_ge(att_done, s - 1)
                    t = term[s % 2]
                    pool.tensor_tensor(pair[s % 2][:, :, :], t[:, 0:2, :], t[:, 2:4, :], ALU.add).then_inc(pair_done, 1)

                for u in range(2):
                    product(u, 1)
                    product(u, 3)
                for u in range(UNITS):
                    if u >= 1:
                        pair_sum(u - 1, 1)
                    if u + 2 < UNITS:
                        product(u + 2, 1)
                        product(u + 2, 3)
                    pair_sum(u, 0)
                pair_sum(UNITS - 1, 1)

            @block.tensor
            def _(pe):
                pe.wait_ge(n.load_local, 64)
                for i, w in enumerate((wk, wv)):
                    for c in range(NC):
                        mm = nc.tensor.matmul(pj[i][:, B * c:B * c + B], w[:, P * c:P * c + P], n.condT,
                                              start=True, stop=True)
                    mm.then_inc(cond_proj, 1)
                pe.wait_ge(cond_kept, 2)
                pe.wait_ge(const_done, 2)
                pe.wait_ge(const_a, 4)

                def project(u, i):
                    if u >= UNITS:
                        return
                    c = u % NC
                    kind, src, _, width = pieces(u)[i]
                    w = wq if kind == "q" else wk
                    g = 5 * u + i
                    if g >= 2:
                        pe.wait_ge(proj_kept, g - 1)
                    nc.tensor.matmul(pj[g % 2][:, 0:width], w[:, P * c:P * c + P], n.xT[:, src:src + width],
                                     start=True, stop=True).then_inc(proj_done, 1)

                def scores(u, i):
                    if u >= UNITS:
                        return
                    if u >= 1 and i == 0:
                        pe.wait_ge(soft, 9 * u - 7)
                    if i == 0:
                        pe.wait_ge(prod_v, 2 * (u + 1))
                        pe.wait_ge(prod_g, 2 * (u + 1))
                    for j in range(J):
                        k = J * i + j
                        mm = nc.tensor.matmul(sc[:, :, :, :].rearrange("p i j h -> p (i j h)"),
                                              prod[u % 2][:, j, P * i:P * i + P], headsel[:, P - 2 * k:2 * P - 2 * k],
                                              start=(k == 0), stop=(k == HB * J - 1))
                    if i == HB - 1:
                        mm.then_inc(score_done, 1)

                def turn_probs(u):
                    pe.wait_ge(parts_done, u + 1)
                    if u >= 1:
                        pe.wait_ge(turned_kept, u)
                    for i in range(HB):
                        mm = nc.tensor.transpose(tr[:, P * i:P * i + P],
                                                 parts[u % 2][:, i, :, :].rearrange("p k r -> p (k r)"), n.identb[:, :])
                    mm.then_inc(turned, 1)

                def spread_probs(u, i):
                    if i == 0:
                        pe.wait_ge(turned_kept, u + 1)
                    m, j = divmod(i, J)
                    g = 2 * J * u + i
                    if g >= 2:
                        pe.wait_ge(term_done, g - 1)
                    nc.tensor.matmul(bc[g % 2][:, :], pick[:, j, :, :].rearrange("r h d -> r (h d)"),
                                     probT[u % 2][:, 512 * m:512 * m + 512], start=True, stop=True).then_inc(spread, 1)

                def project_out(u, m):
                    h, c = divmod(u, NC)
                    if c == 0 and h == 1:
                        pe.wait_ge(y_kept, m + 1)
                    pe.wait_ge(att_done, 2 * u + m + 1)
                    nc.tensor.matmul(y_ps[m][:, :], wo[:, c, :], att[m][:, :], start=(c == 0),
                                     stop=(c == NC - 1)).then_inc(y_part, 1)

                for u in range(2):
                    for i in range(5):
                        project(u, i)
                for i in range(HB):
                    scores(0, i)
                for i in range(5):
                    project(2, i)
                turn_probs(0)
                for u in range(UNITS):
                    scores(u + 1, 0)
                    for i in range(HB - 1):
                        scores(u + 1, i + 1)
                        spread_probs(u, i)
                    project(u + 3, 0)
                    spread_probs(u, HB - 1)
                    project(u + 3, 1)
                    if u >= 1:
                        project_out(u - 1, 1)
                    for i in range(2, 5):
                        project(u + 3, i)
                    project_out(u, 0)
                    if u + 1 < UNITS:
                        turn_probs(u + 1)
                project_out(UNITS - 1, 1)

            @block.scalar
            def _(act):
                act.wait_ge(cond_proj, 2)
                act.wait_ge(const_done, 2)

                def keep_projections(u):
                    c = u % NC
                    bk0 = ROWS["bk"][0]
                    if u >= 4:
                        act.wait_ge(prod_v, 2 * (u - 3))
                        act.wait_ge(prod_g, 2 * (u - 3))
                        act.wait_ge(term_done, 2 * J * (u - 3))
                    for i, (kind, _, dst, width) in enumerate(pieces(u)):
                        g = 5 * u + i
                        act.wait_ge(proj_done, g + 1)
                        if kind == "q":
                            nc.scalar.activation(qb[u % 4][:, dst:dst + width], pj[g % 2][:, 0:width], ACT.Identity,
                                                 bias=bq8[:, c:c + 1], scale=float(HD) ** -0.5).then_inc(proj_kept, 1)
                        else:
                            nc.scalar.activation(kb[u % 4][:, dst:dst + width], pj[g % 2][:, 0:width], ACT.Identity,
                                                 bias=n.cols[:, bk0 + c:bk0 + c + 1]).then_inc(proj_kept, 1)

                def exps(u):
                    act.wait_ge(soft, 9 * u + 2)
                    nc.scalar.activation(s_exp[:, :, :], s_sh[:, :, :], ACT.Exp).then_inc(exp_done, 1)

                def keep_turned(u):
                    act.wait_ge(turned, u + 1)
                    if u >= 2:
                        act.wait_ge(spread, 2 * J * (u - 1))
                    nc.scalar.activation(probT[u % 2][:, :], tr[:, :], ACT.Copy).then_inc(turned_kept, 1)

                def keep_y(h):
                    bo = ROWS["bo"][0]
                    for m in range(2):
                        act.wait_ge(y_part, 2 * NC * (h + 1) - 1 + m)
                        at = h * HALF + 512 * m
                        out = yB[:, :].rearrange("p (b t) -> p t b", b=B)[:, at // B:(at + 512) // B]
                        nc.scalar.activation(out, y_ps[m][:, :].rearrange("p (t b) -> p t b", b=B), ACT.Identity,
                                             bias=n.cols[:, bo:bo + 1]).then_inc(y_kept, 1)

                keep_projections(0)
                keep_projections(1)
                exps(0)
                keep_projections(2)
                keep_turned(0)
                for u in range(UNITS):
                    if u + 1 < UNITS:
                        exps(u + 1)
                    if u + 3 < UNITS:
                        keep_projections(u + 3)
                    if u + 1 < UNITS:
                        keep_turned(u + 1)
                    if u % NC == NC - 1:
                        keep_y(u // NC)

            @block.vector
            def _(dve):
                bq0, bk0, bv0 = ROWS["bq"][0], ROWS["bk"][0], ROWS["bv"][0]
                nc.vector.tensor_scalar(bq8[:, :], n.cols[:, bq0:bq0 + NC], float(HD) ** -0.5, None, ALU.mult)
                nc.vector.memset(headsel[:, :], 0.0).then_inc(const_done, 1)
                dve.wait_ge(const_done, 1)
                for h in range(2):
                    nc.vector.memset(headsel[HD * h:HD * h + HD, P + h:P + h + 1], 1.0)
                for i in range(4):
                    nc.vector.memset(kb[i][:, 0:SH], 0.0)
                    last = nc.vector.memset(kb[i][:, KW:KW + SH], 0.0)
                last.then_inc(const_done, 1)
                dve.wait_ge(cond_proj, 2)
                for i, (dst, b0) in enumerate(((akT, bk0), (avT, bv0))):
                    src = pj[i][:, 0:NC * B].rearrange("p (c b) -> p c b", b=B)
                    bias = n.cols[:, b0:b0 + NC].unsqueeze(2).broadcast_to([P, NC, B])
                    nc.vector.tensor_tensor(dst[:, :, :], src, bias, ALU.add).then_inc(cond_kept, 1)
                dve.wait_ge(cond_kept, 2)

                def products(u):
                    c = u % NC
                    dve.wait_ge(proj_kept, 5 * (u + 1))
                    if u >= 2:
                        dve.wait_ge(score_done, u - 1)
                    q3 = qb[u % 4][:, :].rearrange("p (t b) -> p t b", b=B)
                    ak = akT[:, c, :].unsqueeze(1).broadcast_to([P, HALF // B, B])
                    nc.vector.tensor_tensor(prod[u % 2][:, 0, :].rearrange("p (t b) -> p t b", b=B), q3, ak,
                                            ALU.mult).then_inc(prod_v, 1)
                    nc.vector.tensor_tensor(prod[u % 2][:, 2, :], qb[u % 4][:, :], key(u, 2, 0, HALF),
                                            ALU.mult).then_inc(prod_v, 1)

                def softmax(u):
                    at = 9 * u
                    flat = sc[:, 0:HB, :, :].rearrange("p i j h -> p i h j")
                    wide = [P, HB * 2, J]
                    heads = [P, HB, 2, J]
                    dve.wait_ge(score_done, u + 1)
                    top = s_max[:, :].rearrange("p (i h) -> p i h", h=2)
                    nc.vector.tensor_reduce(top, flat, AX.X, ALU.max).then_inc(soft, 1)
                    dve.wait_ge(soft, at + 1)
                    nc.vector.tensor_tensor(s_sh[:, :, :].rearrange("p (i h) j -> p i h j", h=2), flat,
                                            top.unsqueeze(3).broadcast_to(heads), ALU.subtract).then_inc(soft, 1)
                    dve.wait_ge(exp_done, u + 1)
                    nc.vector.tensor_reduce(s_sum[:, :], s_exp[:, :, :], AX.X, ALU.add).then_inc(soft, 1)
                    dve.wait_ge(soft, at + 3)
                    nc.vector.reciprocal(s_rec[:, :], s_sum[:, :]).then_inc(soft, 1)
                    dve.wait_ge(soft, at + 4)
                    nc.vector.tensor_tensor(prob[:, :, :], s_exp[:, :, :], s_rec[:, :].unsqueeze(2).broadcast_to(wide),
                                            ALU.mult).then_inc(soft, 1)
                    pt = parts[u % 2]
                    if u >= 2:
                        dve.wait_ge(turned, u - 1)
                    pr, r1, r2 = (t[:, :, :].rearrange("p (i h) j -> p i (h j)", h=2) for t in (prob, rest1, rest2))
                    dve.wait_ge(soft, at + 5)
                    nc.vector.tensor_copy(pt[:, :, 0, :], pr).then_inc(soft, 1)
                    dve.wait_ge(soft, at + 6)
                    nc.vector.tensor_tensor(r1, pr, pt[:, :, 0, :], ALU.subtract).then_inc(soft, 1)
                    dve.wait_ge(soft, at + 7)
                    nc.vector.tensor_copy(pt[:, :, 1, :], r1).then_inc(soft, 1)
                    dve.wait_ge(soft, at + 8)
                    nc.vector.tensor_tensor(r2, r1, pt[:, :, 1, :], ALU.subtract).then_inc(soft, 1)
                    dve.wait_ge(soft, at + 9)
                    nc.vector.tensor_copy(pt[:, :, 2, :], r2).then_inc(parts_done, 1)

                def terms(u, m, steps):
                    c = u % NC
                    s = 2 * u + m
                    if s >= 2:
                        dve.wait_ge(pair_done, s - 1)
                    for j in steps:
                        g = s * J + j
                        dve.wait_ge(spread, g + 1)
                        if j == 0:
                            av = avT[:, c, :].unsqueeze(1).broadcast_to([P, 512 // B, B])
                            nc.vector.tensor_tensor(term[s % 2][:, 0, :].rearrange("p (t b) -> p t b", b=B),
                                                    bc[g % 2][:, :].rearrange("p (t b) -> p t b", b=B), av,
                                                    ALU.mult).then_inc(term_done, 1)
                        else:
                            nc.vector.tensor_tensor(term[s % 2][:, j, :], bc[g % 2][:, :], key(u, j, 512 * m, 512),
                                                    ALU.mult).then_inc(term_done, 1)

                def attended(u, m):
                    s = 2 * u + m
                    dve.wait_ge(pair_done, s + 1)
                    if s >= 2:
                        dve.wait_ge(y_part, s - 1)
                    nc.vector.tensor_tensor(att[s % 2][:, :], pair[s % 2][:, 0, :], pair[s % 2][:, 1, :],
                                            ALU.add).then_inc(att_done, 1)

                products(0)
                products(1)
                softmax(0)
                for u in range(UNITS):
                    if u + 2 < UNITS:
                        products(u + 2)
                    if u >= 1:
                        attended(u - 1, 1)
                    terms(u, 0, range(J))
                    terms(u, 1, range(2))
                    if u + 1 < UNITS:
                        softmax(u + 1)
                    attended(u, 0)
                    terms(u, 1, range(2, J))
                attended(UNITS - 1, 1)
def linear_attention(nc, n, yB, wqkv, wout):
    SEG = T // P
    EPS = 1e-6
    PIECES = 12
    ELU = 8
    W = P + 2
    GROUPS = ((0, 1, 2), (3, 4, 5), (6, 7))
    NG = len(GROUPS)
    with ExitStack() as local:
        def sb(name, shape, dt=F32):
            return local.enter_context(nc.sbuf_tensor(name, shape, dt))

        def ps(name, shape):
            return local.enter_context(nc.psum_tensor(name, shape, F32))

        def sem(name):
            return local.enter_context(nc.semaphore(name))

        kk = [sb(f"kk{i}", [P, SEG, INNER]) for i in range(2)]
        vv = [sb(f"vv{i}", [P, SEG, NC, W]) for i in range(2)]
        qq = [sb(f"qq{i}", [P, NC, T]) for i in range(2)]
        ex = [sb(f"ex{i}", [P, 512]) for i in range(2)]
        rl = [sb(f"rl{i}", [P, 512]) for i in range(2)]
        kv = sb("kv", [P, NC, W])
        den = [sb(f"den{i}", [P, 3, 2]) for i in range(2)]
        rec = [sb(f"rec{i}", [P, 3, 2]) for i in range(2)]
        heads = sb("l_heads", [P, SEG, INNER])
        headsT = sb("l_headsT", [P, NC, T])
        mask = sb("mask", [P, W])
        pj = [ps(f"lpj{i}", [P, 512]) for i in range(2)]
        kv_ps = [ps(f"kv_ps{i}", [P, 3, W]) for i in range(2)]
        att_ps = [ps(f"att_ps{i}", [P, 3, W]) for i in range(2)]
        t_ps = ps("lt_ps", [P, 4, P])
        out_ps = ps("out_ps", [P, T])

        const = sem("l_const"); proj_done = sem("l_proj"); piece_kept = sem("l_kept"); elu_in = sem("l_elu_in")
        elu_done = sem("l_elu"); v_kept = sem("l_v"); kv_done = sem("l_kv"); kv_kept = sem("l_kv_kept")
        att_done = sem("l_att"); rec_step = sem("l_rec"); normed = sem("l_normed")
        turned = sem("l_turned"); turned_kept = sem("l_turned_kept"); out_done = sem("l_out"); added = sem("l_added")

        def kind(i):
            if i >= ELU:
                return "v", i - ELU
            return ("k", "q")[i // 2 % 2], 2 * (i // 4) + i % 2

        def elu_target(b, i):
            what, j = kind(i)
            if what == "k":
                return kk[b % 2][:, j // 2, 512 * (j % 2):512 * (j % 2) + 512]
            return qq[b % 2][:, 2 * j:2 * j + 2, :].rearrange("p c t -> p (c t)")

        with nc.Block() as block:

            @block.tensor
            def _(pe):
                pe.wait_ge(n.load_linear, 32)

                def project(b, i):
                    if b >= B:
                        return
                    g = PIECES * b + i
                    if g >= 2:
                        pe.wait_ge(piece_kept, g - 1)
                    what, j = kind(i)
                    if what == "q":
                        for c in range(2):
                            c0 = (2 * j + c) * P
                            mm = nc.tensor.matmul(pj[g % 2][:, T * c:T * c + T], wqkv[:, c0:c0 + P],
                                                  yB[:, T * b:T * b + T], start=True, stop=True)
                    else:
                        at = T * b + P * (j // 2)
                        c0 = INNER * (1 if what == "k" else 2) + 512 * (j % 2)
                        mm = nc.tensor.matmul(pj[g % 2][:, :], yB[:, at:at + P], wqkv[:, c0:c0 + 512],
                                              start=True, stop=True)
                    mm.then_inc(proj_done, 1)

                def key_values(b, j):
                    g = NG * b + j
                    if g >= 2:
                        pe.wait_ge(kv_kept, g - 1)
                    for k, c in enumerate(GROUPS[j]):
                        for i in range(SEG):
                            mm = nc.tensor.matmul(kv_ps[g % 2][:, k, :], kk[b % 2][:, i, P * c:P * c + P],
                                                  vv[b % 2][:, i, c, :], start=(i == 0), stop=(i == SEG - 1))
                    mm.then_inc(kv_done, 1)

                def attend(b, j):
                    i, grp = divmod(j, NG)
                    g = 2 * NG * b + j
                    pe.wait_ge(kv_kept, NG * b + grp + 1)
                    if g >= 2:
                        pe.wait_ge(normed, g - 1)
                    for k, c in enumerate(GROUPS[grp]):
                        mm = nc.tensor.matmul(att_ps[g % 2][:, k, :], qq[b % 2][:, c, P * i:P * i + P], kv[:, c, :],
                                              start=True, stop=True)
                    mm.then_inc(att_done, 1)

                def turn(b, j):
                    i, half = divmod(j, 2)
                    pe.wait_ge(normed, 2 * NG * b + NG * i + (2, 3)[half])
                    if 4 * b + j >= 1:
                        pe.wait_ge(turned_kept, 4 * b + j)
                    for k in range(4):
                        c = 4 * half + k
                        mm = nc.tensor.transpose(t_ps[:, k, :], heads[:, i, P * c:P * c + P], n.ident[:, :])
                    mm.then_inc(turned, 1)

                def outputs(b):
                    pe.wait_ge(turned_kept, 4 * (b + 1))
                    if b >= 1:
                        pe.wait_ge(added, b)
                    for c in range(NC):
                        mm = nc.tensor.matmul(out_ps[:, :], wout[:, c, :], headsT[:, c, :], start=(c == 0), stop=(c == NC - 1))
                    mm.then_inc(out_done, 1)

                pe.wait_ge(const, 1)
                for i in range(PIECES):
                    project(0, i)
                for b in range(B):
                    pe.wait_ge(elu_done, ELU * (b + 1))
                    pe.wait_ge(v_kept, 4 * (b + 1))
                    for i in range(NG):
                        key_values(b, i)
                        project(b + 1, i)
                    for i in range(NG):
                        attend(b, i)
                        project(b + 1, NG + i)
                    attend(b, 3)
                    turn(b, 0)
                    project(b + 1, 6)
                    attend(b, 4)
                    turn(b, 1)
                    project(b + 1, 7)
                    attend(b, 5)
                    project(b + 1, 8)
                    turn(b, 2)
                    project(b + 1, 9)
                    turn(b, 3)
                    project(b + 1, 10)
                    project(b + 1, 11)
                    outputs(b)

            @block.scalar
            def _(act):
                act.wait_ge(const, 1)

                def keep(b, i):
                    if b >= B:
                        return
                    g = PIECES * b + i
                    act.wait_ge(proj_done, g + 1)
                    if i >= ELU:
                        j = i - ELU
                        if b >= 2:
                            act.wait_ge(kv_done, NG * (b - 1))
                        out = vv[b % 2][:, j // 2, 4 * (j % 2):4 * (j % 2) + 4, 0:P]
                        nc.scalar.activation(out, pj[g % 2][:, :].rearrange("p (c f) -> p c f", f=P), ACT.Copy).then_inc(piece_kept, 1)
                        act.wait_ge(piece_kept, g + 1)
                        act.sem_inc(v_kept, 1)
                        return
                    e = ELU * b + i
                    if e >= 2:
                        act.wait_ge(elu_done, e - 1)
                    nc.scalar.activation(ex[e % 2][:, :], pj[g % 2][:, :], ACT.Exp).then_inc(elu_in, 1)
                    nc.scalar.activation(rl[e % 2][:, :], pj[g % 2][:, :], ACT.Relu).then_inc(elu_in, 1)
                    act.wait_ge(elu_in, 2 * (e + 1))
                    act.sem_inc(piece_kept, 1)

                def keep_turned(b, j):
                    i, half = divmod(j, 2)
                    act.wait_ge(turned, 4 * b + j + 1)
                    if b >= 1 and j == 0:
                        act.wait_ge(out_done, b)
                    nc.scalar.activation(headsT[:, 4 * half:4 * half + 4, P * i:P * i + P], t_ps[:, :, :],
                                         ACT.Copy).then_inc(turned_kept, 1)

                for i in range(PIECES):
                    keep(0, i)
                for b in range(B):
                    for i in range(6):
                        keep(b + 1, i)
                    keep_turned(b, 0)
                    keep(b + 1, 6)
                    keep_turned(b, 1)
                    keep(b + 1, 7)
                    keep(b + 1, 8)
                    keep_turned(b, 2)
                    keep(b + 1, 9)
                    keep_turned(b, 3)
                    keep(b + 1, 10)
                    keep(b + 1, 11)

            @block.vector
            def _(dve):
                for i in range(2):
                    nc.vector.memset(vv[i][:, :, :, P:W], 1.0)
                for h in range(2):
                    for other in range(2):
                        nc.vector.memset(mask[HD * h:HD * h + HD, HD * other:HD * other + HD], float(h == other))
                        m = nc.vector.memset(mask[HD * h:HD * h + HD, P + other:P + other + 1], float(h == other))
                m.then_inc(const, 1)
                dve.wait_ge(const, 1)

                def elu(b, e):
                    if b >= B:
                        return
                    g = ELU * b + e
                    dve.wait_ge(elu_in, 2 * (g + 1))
                    if b >= 2 and e == 0:
                        dve.wait_ge(kv_done, NG * (b - 1))
                    if b >= 2 and e == 2:
                        dve.wait_ge(att_done, 2 * NG * (b - 1))
                    nc.vector.scalar_tensor_tensor(elu_target(b, e), ex[g % 2][:, :], 1.0, rl[g % 2][:, :],
                                                   ALU.min, ALU.add).then_inc(elu_done, 1)

                def keep_key_values(b, j):
                    g, k = NG * b + j, len(GROUPS[j])
                    c = GROUPS[j][0]
                    dve.wait_ge(kv_done, g + 1)
                    if b >= 1 and j == 0:
                        dve.wait_ge(att_done, 2 * NG * b)
                    nc.vector.tensor_tensor(kv[:, c:c + k, :], kv_ps[g % 2][:, 0:k, :],
                                            mask[:, :].unsqueeze(1).broadcast_to([P, k, W]), ALU.mult).then_inc(kv_kept, 1)

                def normalise(b, j):
                    i, grp = divmod(j, NG)
                    g, k, c = 2 * NG * b + j, len(GROUPS[grp]), GROUPS[grp][0]
                    dve.wait_ge(att_done, g + 1)
                    if b >= 1 and j == 0:
                        dve.wait_ge(turned, 4 * b)
                    nc.vector.tensor_scalar(den[g % 2][:, 0:k, :], att_ps[g % 2][:, 0:k, P:W], EPS, None, ALU.add).then_inc(rec_step, 1)
                    dve.wait_ge(rec_step, 2 * g + 1)
                    nc.vector.reciprocal(rec[g % 2][:, 0:k, :], den[g % 2][:, 0:k, :]).then_inc(rec_step, 1)
                    dve.wait_ge(rec_step, 2 * g + 2)
                    out = heads[:, i, P * c:P * (c + k)].rearrange("p (c h d) -> p c h d", h=2, d=HD)
                    nc.vector.tensor_tensor(out, att_ps[g % 2][:, 0:k, 0:P].rearrange("p c (h d) -> p c h d", h=2),
                                            rec[g % 2][:, 0:k, :].unsqueeze(3).broadcast_to([P, k, 2, HD]),
                                            ALU.mult).then_inc(normed, 1)

                def add(b):
                    dve.wait_ge(out_done, b + 1)
                    bout = ROWS["bout"][0]
                    x = n.xT[:, :].rearrange("p (t b) -> p b t", b=B)[:, b]
                    nc.vector.scalar_tensor_tensor(x, out_ps[:, :], n.cols[:, bout:bout + 1], x,
                                                   ALU.add, ALU.add).then_inc(added, 1)

                for e in range(ELU):
                    elu(0, e)
                for b in range(B):
                    keep_key_values(b, 0)
                    elu(b + 1, 0)
                    keep_key_values(b, 1)
                    elu(b + 1, 1)
                    keep_key_values(b, 2)
                    for e in range(2, ELU):
                        elu(b + 1, e)
                        normalise(b, e - 2)
                    add(b)


def gru_scan(nc, n, a, hist, w1, w2, diffT, logits):
    G = P // B
    GROUPS = T // G
    JOBS = GROUPS * E
    SEG = T // P
    FILL = 16
    b10, b20, r0 = ROWS["b1"][0], ROWS["b2_0"][0], ROWS["router"][0]
    with ExitStack() as local:
        def sb(name, shape, dt=F32):
            return local.enter_context(nc.sbuf_tensor(name, shape, dt))

        def sem(name):
            return local.enter_context(nc.semaphore(name))

        def ps(name, shape):
            return local.enter_context(nc.psum_tensor(name, shape, F32))

        pre_r = [ps(f"pre_r{i}", [P, 512]) for i in range(2)]
        pre_z = [ps(f"pre_z{i}", [P, 512]) for i in range(2)]
        pre_n = [ps(f"pre_n{i}", [P, 512]) for i in range(2)]
        h_ps = ps("gh_ps", [P, NF, P])
        y_bank = ps("gy_ps", [P, 4, P])
        y_ps, turn_ps, diff_ps, logits_ps = (y_bank[:, i, :] for i in range(4))
        rz = [sb(f"rz{i}", [P, 32]) for i in range(2)]
        narg = [sb(f"narg{i}", [P, 16]) for i in range(2)]
        keepz = [sb(f"keepz{i}", [P, 16]) for i in range(2)]
        mix = [sb(f"mix{i}", [P, 16]) for i in range(2)]
        hid = [sb(f"ghid{i}", [P, NF, P]) for i in range(2)]
        diff, y0 = sb("g_diff", [P, D]), sb("g_y0", [P, D])
        top, mark, first_e, choice = sb("g_top", [P, 1]), sb("g_mark", [P, E]), sb("g_first", [P, 1]), sb("g_choice", [P, E])
        choiceT = sb("g_choiceT", [E, P])
        iota_m8, zero_hot = sb("g_iota", [P, E]), sb("g_zero_hot", [P, E])
        const = sem("g_const"); r_pre = sem("r_pre"); z_pre = sem("z_pre"); n_pre = sem("n_pre")
        r_done = sem("r_done"); z_done = sem("z_done"); narg_done = sem("narg_done"); n_done = sem("n_done"); z_used = sem("z_used")
        state = sem("state"); hist_zero = sem("hist_zero"); all_logits = sem("all_logits")
        h_in = sem("g_h_in"); h_done = sem("g_h_done"); y_in = sem("g_y_in"); summed = sem("g_summed")
        logits_in = sem("g_logits"); choosing = sem("g_choosing"); choice_in = sem("g_choice_in")
        choice_kept = sem("g_choice_kept"); bias_in = sem("g_bias_in"); bias_kept = sem("g_bias_kept"); back_in = sem("g_back_in"); kept = sem("g_kept")

        def gate_slot(pre, s):
            return pre[s // G % 2][:, B * (s % G):B * (s % G) + B]

        def n_slot(s):
            return pre_n[s // G % 2][:, 16 * (s % G):16 * (s % G) + 16]

        def second(ap):
            return ap.rearrange("p (b two) -> p two b", two=2)[:, 1]

        def first(ap):
            return ap.rearrange("p (b two) -> p two b", two=2)[:, 0]

        def at_step(s):
            return hist[:, 16 * s:16 * s + 16]

        def tokens(g):
            return second(hist[:, 16 * (G * g + 1):16 * (G * (g + 1) + 1)])

        def jobs_at(s):
            return divmod(s - G, G)

        STEPS = T + G + 5

        with nc.Block() as block:

            @block.sync
            def _(sp):
                sp.dma_start(w1[:, :, :], a["L0_ffn_W1"].rearrange("e d f -> d e f")).then_inc(n.load_experts, 16)
                sp.dma_start(w2[:, :, :, :], a["L0_ffn_W2"].rearrange("e (f p) d -> p e f d", p=P)).then_inc(n.load_experts, 16)

            @block.gpsimd
            def _(pool):
                pool.memset(hist[:, 16 * 40:], 0.0).then_inc(hist_zero, 1)

            @block.tensor
            def _(pe):
                pe.wait_ge(n.load_later, n.later_loads)
                pe.wait_ge(const, 4)

                def inputs(g, i):
                    if g >= 2 and i == 0:
                        pe.wait_ge(state, G * (g - 1) + 1)
                    nv = pre_n[g % 2][:, 0:256].rearrange("p (x two) -> p two x", two=2)
                    rv, zv = pre_r[g % 2][:, 0:P], pre_z[g % 2][:, 0:P]
                    out = (rv, zv, nv[:, 1], nv[:, 0], rv, zv, nv[:, 1])[i]
                    if i < 3:
                        lhsT, rhs = n.gru_w[:, i, :], n.xT[:, P * g:P * g + P]
                    else:
                        lhsT, rhs = n.gru_b[:, i - 3, :], n.ones_row[:, :]
                    nc.tensor.matmul(out, lhsT, rhs, start=(i < 3), stop=False, skip_group_check=True)

                def hidden(v):
                    g, e = divmod(v, E)
                    if v:
                        pe.wait_ge(h_done, NF * v)
                    for f in range(NF):
                        mm = nc.tensor.matmul(h_ps[:, f, :], w1[:, e, P * f:P * f + P], tokens(g), start=True, stop=True)
                    mm.then_inc(h_in, 1)

                def output(v):
                    g, e = divmod(v, E)
                    pe.wait_ge(h_done, NF * (v + 1))
                    if v:
                        pe.wait_ge(summed, v)
                    for f in range(NF):
                        mm = nc.tensor.matmul(y_ps, hid[v % 2][:, f, :], w2[:, e, f, :], start=(f == 0), stop=(f == NF - 1))
                    mm.then_inc(y_in, 1)

                def work(s):
                    g, k = jobs_at(s)
                    if g < 0:
                        for _ in range(FILL):
                            nc.tensor.matmul(y_ps, n.identb[:, :], n.identb[:, :], start=True, stop=True)
                        return
                    v = (s - G) // 2
                    if k % 2 == 0 and v < JOBS:
                        if v == 0:
                            pe.wait_ge(n.load_experts, 32)
                        hidden(v)
                    if s == G + 3:
                        pe.wait_ge(choosing, 2)
                    if k % 2 == 1 and 0 <= v - 1 < JOBS:
                        output(v - 1)
                    if k == 1 and g < GROUPS:
                        if g:
                            pe.wait_ge(bias_kept, g)
                        nc.tensor.matmul(logits_ps, tokens(g), n.cols[:, :], start=True, stop=True).then_inc(logits_in, 1)
                    if k == 3 and g:
                        pe.wait_ge(summed, E * g)
                        if g < GROUPS:
                            pe.wait_ge(choosing, 4 * g + 2)
                        nc.tensor.transpose(diff_ps, diff[:, :], n.ident[:, :])
                        nc.tensor.transpose(turn_ps, y0[:, :], n.ident[:, :]).then_inc(back_in, 1)
                    if k == 5 and g < GROUPS:
                        pe.wait_ge(choosing, 4 * (g + 1))
                        if g:
                            pe.wait_ge(kept, 2 * g)
                        nc.tensor.transpose(turn_ps[0:E, :], choice[:, :], n.ident[:, :]).then_inc(choice_in, 1)
                    if k == 7 and g < GROUPS:
                        pe.wait_ge(choice_kept, g + 1)
                        nc.tensor.matmul(turn_ps, n.b2[:, :], choiceT[:, :], start=True, stop=True).then_inc(bias_in, 1)

                for i in range(7):
                    inputs(0, i)
                for s in range(STEPS):
                    if s < T:
                        h = second(hist[:, 16 * s:16 * (s + G)]).rearrange("p (s b) -> p s b", b=B)
                        at = 16 * (s % G)
                        at8 = B * (s % G)
                        r_out, z_out = (pre[s // G % 2][:, at8:at8 + P].rearrange("p (s b) -> p s b", b=B) for pre in (pre_r, pre_z))
                        n_out = first(pre_n[s // G % 2][:, at:at + 16 * G]).rearrange("p (s b) -> p s b", b=B)
                        if s == 24:
                            pe.wait_ge(hist_zero, 1)
                        pe.wait_ge(state, s + 1)
                        for out, i, ready in ((r_out, 3, r_pre), (n_out, 5, n_pre), (z_out, 4, z_pre)):
                            nc.tensor.matmul(out, n.gru_w[:, i, :], h, start=False, stop=True,
                                             skip_group_check=True).then_inc(ready, 1)
                    elif s == T:
                        pe.wait_ge(state, T + 1)
                    work(s)
                    if T < s <= T + NBLK:
                        b, half = divmod(s - T - 1, SEG)
                        states = hist[:, 16:16 * (T + 1)].rearrange("p (t b two) -> p two b t", b=B, two=2)[:, 1]
                        mm = nc.tensor.matmul(pre_r[0][:, E * (s - T - 1):E * (s - T)], states[:, b, P * half:P * half + P],
                                              n.cols[:, r0:r0 + E], start=True, stop=True)
                        if s == T + NBLK:
                            mm.then_inc(all_logits, 1)
                    g, i = s // G + 1, s % G - 9
                    if g < GROUPS and 0 <= i < 7:
                        inputs(g, i)

            @block.scalar
            def _(act):
                act.preload_act_table(ACT.Sigmoid)
                act.wait_ge(const, 4)
                for s in range(STEPS):
                    if s < T:
                        act.wait_ge(r_pre, s + 1)
                        nc.scalar.activation(second(rz[s % 2][:, 0:16]), gate_slot(pre_r, s), ACT.Sigmoid).then_inc(r_done, 1)
                        act.wait_ge(z_pre, s + 1)
                        nc.scalar.activation(second(rz[s % 2][:, 16:32]), gate_slot(pre_z, s), ACT.Sigmoid).then_inc(z_done, 1)
                        act.wait_ge(narg_done, s + 1)
                        nc.scalar.activation(first(mix[s % 2][:, :]), second(narg[s % 2][:, :]), ACT.Tanh).then_inc(n_done, 1)
                    v, odd = divmod(s - G, 2)
                    if odd and 0 <= v < JOBS:
                        e = v % E
                        act.wait_ge(h_in, v + 1)
                        if v >= 2:
                            act.wait_ge(y_in, v - 1)
                        for f in range(NF):
                            at = b10 + NF * e + f
                            nc.scalar.activation(hid[v % 2][:, f, :], h_ps[:, f, :], ACT.Relu,
                                                 bias=n.cols[:, at:at + 1]).then_inc(h_done, 1)

            @block.vector
            def _(dve):
                V = nc.vector
                for i in range(2):
                    V.memset(rz[i][:, :], 0.0)
                    V.memset(keepz[i][:, :], 0.0)
                    last = V.memset(mix[i][:, :], 0.0)
                last.then_inc(const, 1)
                V.tensor_scalar(iota_m8[:, :], n.iota8[:, :], -float(E), None, ALU.add).then_inc(const, 1)
                V.tensor_scalar(zero_hot[:, :], n.iota8[:, :], 0.0, None, ALU.is_equal).then_inc(const, 1)
                V.memset(hist[:, 0:16 * 40], 0.0).then_inc(const, 1)
                dve.wait_ge(const, 4)
                V.tensor_copy(second(at_step(0)), n.condT).then_inc(state, 1)
                dve.wait_ge(state, 1)

                def choose(g, k):
                    dve.wait_ge(logits_in, g + 1)
                    if g or k:
                        dve.wait_ge(choosing, 4 * g + k)
                    if k == 0:
                        ins = V.tensor_reduce(top[:, :], logits_ps[:, r0:r0 + E], AX.X, ALU.max)
                    elif k == 1:
                        ins = V.scalar_tensor_tensor(mark[:, :], logits_ps[:, r0:r0 + E], top[:, 0:1], iota_m8[:, :], ALU.is_equal, ALU.mult)
                    elif k == 2:
                        ins = V.tensor_reduce(first_e[:, :], mark[:, :], AX.X, ALU.min)
                    else:
                        if g:
                            dve.wait_ge(choice_in, g)
                            dve.wait_ge(summed, E * g)
                        ins = V.scalar_tensor_tensor(choice[:, :], iota_m8[:, :], first_e[:, 0:1], zero_hot[:, :],
                                                     ALU.is_equal, ALU.subtract)
                    ins.then_inc(choosing, 1)

                def add(v):
                    g, e = divmod(v, E)
                    dve.wait_ge(y_in, v + 1)
                    if e == 0:
                        if g:
                            dve.wait_ge(back_in, g)
                        V.tensor_copy(y0[:, :], y_ps)
                        dve.wait_ge(choosing, 4 * (g + 1))
                        V.tensor_scalar(diff[:, :], y_ps, choice[:, 0:1], None, ALU.mult).then_inc(summed, 1)
                    else:
                        dve.wait_ge(summed, v)
                        V.scalar_tensor_tensor(diff[:, :], y_ps, choice[:, e:e + 1], diff[:, :],
                                               ALU.mult, ALU.add).then_inc(summed, 1)

                def keep(g):
                    cols = slice(P * g, P * g + P)
                    dve.wait_ge(back_in, g + 1)
                    V.scalar_tensor_tensor(n.xT[:, cols], turn_ps, n.cols[:, b20:b20 + 1], n.xT[:, cols],
                                           ALU.add, ALU.add).then_inc(kept, 1)
                    dve.wait_ge(bias_kept, g + 1)
                    V.tensor_tensor(diffT[:, cols], diff_ps, diffT[:, cols], ALU.add).then_inc(kept, 1)

                for s in range(STEPS):
                    if s < T:
                        p = s % 2
                        dve.wait_ge(r_done, s + 1)
                        dve.wait_ge(n_pre, s + 1)
                        V.tensor_tensor_scan(narg[p][:, :], rz[p][:, 0:16], n_slot(s), 0.0,
                                             ALU.mult, ALU.add).then_inc(narg_done, 1)
                        z = second(rz[p][:, 16:32])
                        dve.wait_ge(z_done, s + 1)
                        V.tensor_scalar(second(keepz[p][:, :]), z, -1.0, 1.0, ALU.mult, ALU.add).then_inc(z_used, 1)
                        V.tensor_tensor(second(mix[p][:, :]), z, second(at_step(s)), ALU.mult).then_inc(z_used, 1)
                        dve.wait_ge(z_used, 2 * s + 2)
                        dve.wait_ge(n_done, s + 1)
                        V.tensor_tensor_scan(at_step(s + 1), keepz[p][:, :], mix[p][:, :], 0.0,
                                             ALU.mult, ALU.add).then_inc(state, 1)
                    g, k = jobs_at(s)
                    if g < 0:
                        continue
                    if k == 4 and g:
                        keep(g - 1)
                    if k == 2 and g < GROUPS:
                        choose(g, 0)
                        choose(g, 1)
                    if k == 3 and g < GROUPS:
                        choose(g, 2)
                        choose(g, 3)
                    if k == 6 and g < GROUPS:
                        dve.wait_ge(choice_in, g + 1)
                        V.tensor_copy(choiceT[:, :], turn_ps[0:E, :]).then_inc(choice_kept, 1)
                    if k == 8 and g < GROUPS:
                        dve.wait_ge(bias_in, g + 1)
                        V.tensor_copy(diffT[:, P * g:P * g + P], turn_ps).then_inc(bias_kept, 1)
                    v = (s - G) // 2 - 2
                    if k % 2 == 0 and 0 <= v < JOBS:
                        add(v)
                    if s == T + NBLK + 1:
                        dve.wait_ge(all_logits, 1)
                        V.tensor_copy(logits[:, :, :].rearrange("p i e -> p (i e)"), pre_r[0][:, 0:NBLK * E])


def route_top1(nc, n, logits, diffT):
    with ExitStack() as local:
        def sb(name, shape, dt=F32):
            return local.enter_context(nc.sbuf_tensor(name, shape, dt))

        def sem(name):
            return local.enter_context(nc.semaphore(name))

        wide = [P, NBLK, E]
        score, prob, mark, chosen = (sb(k, wide) for k in ("r_score", "r_prob", "r_mark", "r_chosen"))
        top, total, best, first = (sb(k, [P, NBLK]) for k in ("r_top", "r_total", "r_best", "r_first"))
        mine, rest1, rest2 = (sb(k, wide) for k in ("r_mine", "r_rest1", "r_rest2"))
        parts = sb("r_parts", [P, NBLK, 3, E], BF16)
        picks = sb("r_picks", [P, NBLK, 3, E], BF16)
        partsT = sb("r_partsT", [3 * E, TOK], BF16)
        picksT = sb("r_picksT", [3 * E, TOK], BF16)
        iota_m8 = sb("iota_m8", [P, E])
        before = sb("before", [P, P])
        ones = sb("r_ones", [P, P], BF16)
        gt = [sb(f"r_gt{i}", [P, 1024], BF16) for i in range(3)]
        tied = sb("r_tied", [P, P], BF16)
        zeros = sb("r_zeros", [P, NBLK], BF16)
        cum = [sb(f"r_cum{i}", [P, NBLK * E]) for i in range(2)]
        counts = sb("r_counts", [P, 3, NBLK])
        rank, kept = sb("r_rank", [P, NBLK]), sb("r_kept", [P, NBLK])
        diag = sb("r_diag", [P, NBLK, P], BF16)
        added = [sb(f"r_added{i}", [P, 2 * T]) for i in range(4)]
        const = sem("r_const"); step = sem("r_step")
        exp_done = sem("r_exp"); turned = sem("r_turned"); turned_kept = sem("r_turned_kept")
        row_in = sem("row_in"); counted = sem("counted"); final = sem("r_final")
        diag_done = sem("r_diag_done"); spread = sem("r_spread"); totals_in = sem("r_totals"); totals_kept = sem("r_totals_kept"); adding = sem("r_adding"); summed = sem("r_summed"); added_in = sem("r_added_in");

        with ExitStack() as early:
            tp = early.enter_context(nc.psum_tensor("tp", [3 * E, TOK], BF16))
            tq = early.enter_context(nc.psum_tensor("tq", [3 * E, TOK], BF16))
            with nc.Block() as block:

                @block.gpsimd
                def _(pool):
                    pool.memset(before[:, :], 1.0).then_inc(const, 1)
                    pool.tensor_scalar(iota_m8[:, :], n.iota8[:, :], -float(E), None, ALU.add).then_inc(const, 1)
                    pool.wait_ge(const, 2)
                    pool.affine_select(out=before[:, :], in_=before[:, :], compare_op=ALU.is_gt, fill=0.0,
                                       base=0, pattern=[[-1, P]], channel_multiplier=1).then_inc(const, 1)
                    pool.memset(ones[:, :], 1.0)
                    pool.memset(zeros[:, :], 0.0)

                @block.scalar
                def _(act):
                    act.preload_act_table(ACT.Exp)
                    act.wait_ge(step, 2)
                    nc.scalar.activation(prob[:, :, :], score[:, :, :], ACT.Exp).then_inc(exp_done, 1)
                    act.wait_ge(turned, 2)
                    nc.scalar.activation(partsT[:, :], tp[:, :], ACT.Copy).then_inc(turned_kept, 1)

                @block.tensor
                def _(pe):
                    for src, dst, ready in ((picks, tq, 6), (parts, tp, 14)):
                        pe.wait_ge(step, ready)
                        for i in range(NBLK):
                            mm = nc.tensor.transpose(dst[:, P * i:P * i + P],
                                                     src[:, i, :, :].rearrange("p k e -> p (k e)"), n.identb[:, :])
                        mm.then_inc(turned, 1)

                @block.vector
                def _(dve):
                    at = [0]

                    def done(ins):
                        at[0] += 1
                        ins.then_inc(step, 1)
                        dve.wait_ge(step, at[0])

                    def per_token(ap):
                        return ap[:, :].unsqueeze(2).broadcast_to(wide)

                    V = nc.vector
                    V.memset(counts[:, :, :], 0.0)
                    done(V.tensor_reduce(top[:, :], logits[:, :, :], AX.X, ALU.max))
                    done(V.tensor_tensor(score[:, :, :], logits[:, :, :], per_token(top), ALU.subtract))
                    dve.wait_ge(const, 3)
                    ramp = iota_m8[:, :].unsqueeze(1).broadcast_to(wide)
                    done(V.scalar_tensor_tensor(mark[:, :, :], score[:, :, :], 0.0, ramp, ALU.is_equal, ALU.mult))
                    done(V.tensor_reduce(first[:, :], mark[:, :, :], AX.X, ALU.min))
                    done(V.tensor_tensor(chosen[:, :, :], ramp, per_token(first), ALU.is_equal))
                    done(V.tensor_copy(picks[:, :, :, :], chosen[:, :, :].unsqueeze(2).broadcast_to([P, NBLK, 3, E])))
                    dve.wait_ge(exp_done, 1)
                    done(V.tensor_reduce(total[:, :], prob[:, :, :], AX.X, ALU.add))
                    done(V.reciprocal(best[:, :], total[:, :]))
                    done(V.tensor_tensor(mine[:, :, :], chosen[:, :, :], per_token(best), ALU.mult))
                    done(V.tensor_copy(parts[:, :, 0, :], mine[:, :, :]))
                    done(V.tensor_tensor(rest1[:, :, :], mine[:, :, :], parts[:, :, 0, :], ALU.subtract))
                    done(V.tensor_copy(parts[:, :, 1, :], rest1[:, :, :]))
                    done(V.tensor_tensor(rest2[:, :, :], rest1[:, :, :], parts[:, :, 1, :], ALU.subtract))
                    done(V.tensor_copy(parts[:, :, 2, :], rest2[:, :, :]))
                    dve.wait_ge(turned, 1)
                    V.tensor_copy(picksT[:, :], tq[:, :]).then_inc(turned_kept, 1)

        PIECE = 1024
        pieces = [(i, c0, min(PIECE, TOK - c0), k) for i in range(NBLK) for k, c0 in enumerate(range(P * i, TOK, PIECE))]
        NP = len(pieces)
        with ExitStack() as middle:
            rows = [middle.enter_context(nc.psum_tensor(f"rows{i}", [P, PIECE], F32)) for i in range(3)]
            sums = middle.enter_context(nc.psum_tensor("r_sums", [P, 512], F32))
            later, totals = sums[:, 0:NBLK], sums[:, P:P + NBLK * E]
            with nc.Block() as block:

                @block.tensor
                def _(pe):
                    def fill(r):
                        i, c0, w, _ = pieces[r]
                        if r >= 3:
                            pe.wait_ge(counted, r - 2)
                        for at in range(0, w, 512):
                            mm = nc.tensor.matmul(rows[r % 3][:, at:min(at + 512, w)], picksT[:, P * i:P * i + P],
                                                  partsT[:, c0 + at:c0 + min(at + 512, w)], start=True, stop=True)
                        mm.then_inc(row_in, 1)

                    fill(0)
                    nc.tensor.matmul(totals, ones[:, :], picks[:, :, 0, :], start=True, stop=True).then_inc(totals_in, 1)
                    fill(1)
                    fill(2)
                    pe.wait_ge(totals_kept, 1)
                    nc.tensor.matmul(later, ones[:, :], zeros[:, :], start=True, stop=False, skip_group_check=True)
                    for r in range(NP):
                        i, c0, w, _ = pieces[r]
                        pe.wait_ge(counted, r + 1)
                        for m in range(c0 // P, (c0 + w) // P):
                            if m > i:
                                nc.tensor.matmul(later[:, m:m + 1], gt[r % 3][:, P * m - c0:P * m - c0 + P], ones[:, 0:1],
                                                 start=False, stop=True, skip_group_check=True)
                        nc.tensor.matmul(later[:, 0:1], ones[:, :], zeros[:, 0:1], start=False, stop=True,
                                         skip_group_check=True).then_inc(summed, 1)
                        if r + 3 < NP:
                            fill(r + 3)

                @block.scalar
                def _(act):
                    act.wait_ge(totals_in, 1)
                    nc.scalar.activation(cum[0][:, E:], totals[:, 0:(NBLK - 1) * E], ACT.Copy).then_inc(totals_kept, 1)

                @block.gpsimd
                def _(pool):
                    pool.memset(cum[0][:, 0:E], 0.0).then_inc(adding, 1)
                    pool.wait_ge(totals_kept, 1)
                    pool.wait_ge(adding, 1)
                    k, shift = 0, 1
                    while shift < NBLK:
                        w = shift * E
                        pool.tensor_copy(cum[1 - k % 2][:, 0:w], cum[k % 2][:, 0:w]).then_inc(adding, 1)
                        pool.tensor_tensor(cum[1 - k % 2][:, w:], cum[k % 2][:, w:], cum[k % 2][:, 0:NBLK * E - w],
                                           ALU.add).then_inc(adding, 1)
                        pool.wait_ge(adding, 2 * k + 3)
                        k, shift = k + 1, 2 * shift
                    pool.tensor_tensor(cum[1 - k % 2][:, :], cum[k % 2][:, :], chosen[:, :, :].rearrange("p i e -> p (i e)"),
                                       ALU.mult).then_inc(adding, 1)

                @block.vector
                def _(dve):
                    V = nc.vector
                    for r in range(NP):
                        i, c0, w, k = pieces[r]
                        p = best[:, i:i + 1]
                        dve.wait_ge(row_in, r + 1)
                        if r >= 3:
                            dve.wait_ge(summed, r - 2)
                        if k == 0:
                            if i:
                                dve.wait_ge(final, i)
                            V.scalar_tensor_tensor(tied[:, :], rows[r % 3][:, 0:P], p, before[:, :],
                                                   ALU.is_equal, ALU.mult, accum_out=counts[:, 2, i:i + 1]).then_inc(final, 1)
                        V.tensor_scalar(gt[r % 3][:, 0:w], rows[r % 3][:, 0:w], p, None, ALU.is_gt, ALU.add,
                                        accum_out=counts[:, k, i:i + 1]).then_inc(counted, 1)
                    dve.wait_ge(adding, 10)
                    V.tensor_reduce(kept[:, :], cum[1][:, :].rearrange("p (i e) -> p i e", e=E), AX.X, ALU.add).then_inc(final, 1)
                    dve.wait_ge(counted, NP)
                    dve.wait_ge(final, NBLK + 1)
                    V.tensor_reduce(rank[:, :], counts[:, :, :].rearrange("p k i -> p i k"), AX.X, ALU.add).then_inc(final, 1)
                    dve.wait_ge(final, NBLK + 2)
                    V.tensor_tensor(rank[:, :], rank[:, :], kept[:, :], ALU.add).then_inc(final, 1)
                    dve.wait_ge(final, NBLK + 3)
                    dve.wait_ge(summed, NP)
                    V.tensor_tensor(rank[:, :], rank[:, :], later, ALU.subtract).then_inc(final, 1)
                    dve.wait_ge(final, NBLK + 4)
                    V.tensor_scalar(kept[:, :], rank[:, :], float(CAPACITY), None, ALU.is_lt).then_inc(final, 1)
                    dve.wait_ge(final, NBLK + 5)
                    for m in range(4):
                        blocks = slice(4 * m, 4 * m + 4)
                        V.tensor_tensor(diag[:, blocks, :], n.identb[:, :].unsqueeze(1).broadcast_to([P, 4, P]),
                                        kept[:, blocks].unsqueeze(2).broadcast_to([P, 4, P]), ALU.mult).then_inc(diag_done, 1)

        keptB = [local.enter_context(nc.psum_tensor(f"keptB{m}", [P, 2 * T], F32)) for m in range(4)]
        with nc.Block() as block:

            @block.tensor
            def _(pe):
                for m in range(4):
                    pe.wait_ge(diag_done, m + 1)
                    nc.tensor.matmul(keptB[m][:, :], ones[:, :], diag[:, 4 * m:4 * m + 4, :].rearrange("p i t -> p (i t)"),
                                     start=True, stop=True).then_inc(spread, 1)

            @block.gpsimd
            def _(pool):
                for m in range(2):
                    pool.wait_ge(added_in, m + 1)
                    x = n.xT[:, :].rearrange("p (t b) -> p t b", b=B)[:, :, 2 * m:2 * m + 2]
                    pool.tensor_tensor(x, added[m][:, :].rearrange("p (t b) -> p t b", b=2), x, ALU.add)

            @block.vector
            def _(dve):
                V = nc.vector
                for m in range(4):
                    pair = slice(2 * m, 2 * m + 2)
                    dve.wait_ge(spread, m + 1)
                    V.tensor_tensor(added[m][:, :].rearrange("p (t b) -> p t b", b=2),
                                    diffT[:, :].rearrange("p (t b) -> p t b", b=B)[:, :, pair],
                                    keptB[m][:, :].rearrange("p (b t) -> p t b", b=2), ALU.mult).then_inc(added_in, 1)
                for m in range(2, 4):
                    dve.wait_ge(added_in, m + 1)
                    x = n.xT[:, :].rearrange("p (t b) -> p t b", b=B)[:, :, 2 * m:2 * m + 2]
                    V.tensor_tensor(x, added[m][:, :].rearrange("p (t b) -> p t b", b=2), x, ALU.add)


def gate_scan(nc, n, a, s2, qk, vt, wgT, wuT, wdT):
    G = 32
    HEAD = 40
    KINDS = (("L1_ffn_wg", wgT), ("L1_ffn_wu", wuT), ("L1_ffn_wd", wdT))
    jobs = [(key, dst, e) for key, dst in KINDS for e in range(E)]
    EVERY = T // len(jobs)
    RAW = 4
    FILL = 12
    INPUTS_AT = 16
    SPAN = 32
    plan, at = {}, 0
    for p in range(T // SPAN - 1):
        at = max(at, SPAN * (p + 1))
        for item in [("qk", p, k) for k in range(4)] + ([("v", p, k) for k in range(4)] if SPAN * (p + 1) == P else []):
            at += 1
            while (at - 4) % EVERY in (0, 1) or at % G == INPUTS_AT:
                at += 1
            plan[at] = (len(plan),) + item
    assert at < T
    with ExitStack() as local:
        def sb(name, shape, dt=F32):
            return local.enter_context(nc.sbuf_tensor(name, shape, dt))

        def sem(name):
            return local.enter_context(nc.semaphore(name))

        wT = sb("wT", [P, 2, D])
        leak = sb("leak", [P, 1])
        ones_w = sb("ones_w", [1, B * G])
        pairs = sb("pairs", [P, 16 * T])
        gates = [sb(f"gates{i}", [P, 16]) for i in range(2)]
        targ = [sb(f"targ{i}", [P, 16]) for i in range(2)]
        pre = [local.enter_context(nc.psum_tensor(f"s_pre{i}", [P, 512], F32)) for i in range(2)]
        w_ps = local.enter_context(nc.psum_tensor("w_ps", [P, 2, D], F32))
        raw = [sb(f"raw{i}", [P, NF, P]) for i in range(RAW)]
        tps = [local.enter_context(nc.psum_tensor(f"tps{i}", [P, NF, P], F32)) for i in range(2)]
        spare = local.enter_context(nc.psum_tensor("spare", [P, 512], F32))
        pj = [local.enter_context(nc.psum_tensor(f"s_pj{i}", [P, 256], F32)) for i in range(2)]
        pj_in = sem("s_pj_in"); pj_kept = sem("s_pj_kept")
        ld = [sem(f"raw_in{i}") for i in range(RAW)]
        jobs_turned = sem("w_turned"); jobs_kept = sem("wt_kept")
        turned = sem("s_turned"); w_kept = sem("w_kept"); const = sem("s_const"); z_in = sem("z_in"); s2_zero = sem("s2_zero")
        pre_in = sem("s_pre_in"); gate_done = sem("s_gate"); leaked = sem("leaked")
        arg_done = sem("s_arg"); state = sem("s_state")

        def second(ap):
            return ap.rearrange("p (b two) -> p two b", two=2)[:, 1]

        with nc.Block() as block:

            @block.sync
            def _(sp):
                for j, (key, dst, e) in enumerate(jobs):
                    if j >= RAW:
                        sp.wait_ge(jobs_turned, j - RAW + 1)
                    src = a[key][e]
                    src = src.rearrange("(f p) h -> p f h", p=P) if dst is not wdT else src.rearrange("h (f i) -> h f i", i=P)
                    sp.dma_start(raw[j % RAW][:, :, :], src).then_inc(ld[j % RAW], 16)

            @block.gpsimd
            def _(pool):
                pool.memset(s2[:, B * HEAD:], 0.0).then_inc(s2_zero, 1)
                for q in range(4):
                    w = TOK // 4
                    out = pairs[:, 2 * w * q:2 * w * (q + 1)].rearrange("p (x two) -> p two x", two=2)[:, 0]
                    pool.tensor_copy(out, n.xT[:, w * q:w * q + w]).then_inc(z_in, 1)

            @block.tensor
            def _(pe):
                for i in range(2):
                    mm = nc.tensor.transpose(w_ps[:, i, :], n.l1w[:, D * i:D * i + D], n.ident[:, :])
                mm.then_inc(turned, 1)
                pe.wait_ge(w_kept, 1)
                pe.wait_ge(const, 2)

                def inputs(g):
                    if g >= 2:
                        pe.wait_ge(state, G * (g - 1) + 1)
                    w = B * G
                    nc.tensor.matmul(pre[g % 2][:, 0:w], wT[:, 1, :], n.xT[:, w * g:w * g + w], start=True, stop=False,
                                     skip_group_check=True)
                    nc.tensor.matmul(pre[g % 2][:, 0:w], n.b_l1[:, :], ones_w[:, :], start=False, stop=False,
                                     skip_group_check=True)

                inputs(0)
                for s in range(T):
                    pe.wait_ge(state, s + 1)
                    if s == HEAD - P // B:
                        pe.wait_ge(s2_zero, 1)
                    at = 8 * (s % G)
                    nc.tensor.matmul(pre[s // G % 2][:, at:at + P], wT[:, 0, :], s2[:, 8 * s:8 * s + P],
                                     start=False, stop=True, skip_group_check=True).then_inc(pre_in, 1)
                    fill = FILL
                    if s % G == INPUTS_AT and s // G + 1 < T // G:
                        inputs(s // G + 1)
                        fill = 0
                    j, k = divmod(s - 4, EVERY)
                    if k == 0 and 0 <= j < len(jobs):
                        pe.wait_ge(ld[j % RAW], 16 * (j // RAW + 1))
                        if j >= 2:
                            pe.wait_ge(jobs_kept, 2 * (j - 1))
                        for f in range(NF):
                            mm = nc.tensor.transpose(tps[j % 2][:, f, :], raw[j % RAW][:, f, :], n.ident[:, :])
                        mm.then_inc(jobs_turned, 1)
                    if s in plan:
                        i, kind, p, k = plan[s]
                        if i >= 2:
                            pe.wait_ge(pj_kept, i - 1)
                        if kind == "qk":
                            w = (n.wq12, n.wq12, n.wk12, n.wk12)[k]
                            c0 = B * (SPAN * p + 1)
                            mm = nc.tensor.matmul(pj[i % 2][:, :], w[:, D * (k % 2):D * (k % 2) + D],
                                                  s2[:, c0:c0 + B * SPAN], start=True, stop=True)
                        else:
                            for j in range(2):
                                states = s2[:, B:B + B * P].rearrange("p (t b) -> p b t", b=B)[:, 2 * k + j]
                                mm = nc.tensor.matmul(pj[i % 2][:, D * j:D * j + D], states, n.wv1[:, :], start=True, stop=True)
                        mm.then_inc(pj_in, 1)
                        fill = FILL // 3
                    for _ in range(fill):
                        nc.tensor.matmul(spare[:, 0:P], n.identb[:, :], n.identb[:, :], start=True, stop=True)

            @block.scalar
            def _(act):
                act.wait_ge(turned, 1)
                act.preload_act_table(ACT.Sigmoid)
                nc.scalar.activation(wT[:, :, :], w_ps[:, :, :], ACT.Copy).then_inc(w_kept, 1)
                act.wait_ge(const, 2)
                for s in range(T):
                    act.wait_ge(pre_in, s + 1)
                    nc.scalar.activation(second(gates[s % 2][:, :]), pre[s // G % 2][:, 8 * (s % G):8 * (s % G) + 8],
                                         ACT.Sigmoid).then_inc(gate_done, 1)
                    act.wait_ge(arg_done, s + 1)
                    nc.scalar.activation(s2[:, 8 * s + 8:8 * s + 16], second(targ[s % 2][:, :]), ACT.Tanh).then_inc(state, 1)
                    j, k = divmod(s - 5, EVERY)
                    if k < 2 and 0 <= j < len(jobs):
                        dst, e = jobs[j][1:]
                        act.wait_ge(jobs_turned, j + 1)
                        out = wdT[:, e, :, :] if dst is wdT else dst[:, e, :].rearrange("p (f h) -> p f h", h=P)
                        nc.scalar.activation(out[:, 2 * k:2 * k + 2], tps[j % 2][:, 2 * k:2 * k + 2, :], ACT.Copy).then_inc(jobs_kept, 1)
                    if s - 1 in plan:
                        i, kind, p, k = plan[s - 1]
                        act.wait_ge(pj_in, i + 1)
                        if kind == "qk":
                            out = qk[:, k, :].rearrange("p (b t) -> p t b", b=B)[:, SPAN * p:SPAN * p + SPAN]
                            src = pj[i % 2][:, :].rearrange("p (t b) -> p t b", b=B)
                        else:
                            out = vt.rearrange("p (b s) d -> p s b d", s=T // P)[:, 0, 2 * k:2 * k + 2, :]
                            src = pj[i % 2][:, :].rearrange("p (b d) -> p b d", d=D)
                        nc.scalar.activation(out, src, ACT.Copy).then_inc(pj_kept, 1)

            @block.vector
            def _(dve):
                al = ROWS["alpha"][0]
                for i in range(2):
                    nc.vector.memset(gates[i][:, :], 0.0)
                nc.vector.tensor_scalar(leak[:, :], n.cols[:, al:al + 1], -1.0, 1.0, ALU.mult, ALU.add).then_inc(const, 1)
                nc.vector.memset(ones_w[:, :], 1.0)
                nc.vector.memset(s2[:, 0:B * HEAD], 0.0).then_inc(const, 1)
                dve.wait_ge(const, 2)
                nc.vector.tensor_copy(s2[:, 0:8], n.condT).then_inc(state, 1)
                for s in range(T):
                    if s % (T // 4) == 0:
                        dve.wait_ge(z_in, s // (T // 4) + 1)
                    dve.wait_ge(state, s + 1)
                    pair = pairs[:, 16 * s:16 * s + 16]
                    nc.vector.tensor_scalar(second(pair), s2[:, 8 * s:8 * s + 8], leak[:, 0:1], None, ALU.mult).then_inc(leaked, 1)
                    dve.wait_ge(leaked, s + 1)
                    dve.wait_ge(gate_done, s + 1)
                    nc.vector.tensor_tensor_scan(targ[s % 2][:, :], gates[s % 2][:, :], pair, 0.0,
                                                 ALU.mult, ALU.add).then_inc(arg_done, 1)


def diff_attention(nc, n, s2, qk, vt):
    SPAN = 32
    MOD_EPS = 1e-8
    SCALE = float(D) ** -0.25
    EPS, LAMBDA_INIT = 1e-5, 0.8
    SEG = T // P
    UNITS = B * SEG
    with ExitStack() as local:
        def sb(name, shape, dt=F32):
            return local.enter_context(nc.sbuf_tensor(name, shape, dt))

        def ps(name, shape):
            return local.enter_context(nc.psum_tensor(name, shape, F32))

        def sem(name):
            return local.enter_context(nc.semaphore(name))

        lam2 = sb("lam2", [P, 2]); lam = sb("lam", [P, 1]); lq = sb("lq", [P, 2, P])
        negmax = [sb(f"negmax{i}", [P, 2]) for i in range(2)]
        sums = [sb(f"sums{i}", [P, 2]) for i in range(2)]
        inv = [sb(f"inv{i}", [P, 2]) for i in range(2)]
        probs = [sb(f"probs{i}", [P, 2, T]) for i in range(2)]
        diff = [sb(f"diff{i}", [P, T]) for i in range(2)]
        diffT = [sb(f"diffT{i}", [P, SEG, P]) for i in range(2)]
        heads = sb("heads", [P, UNITS, D])
        junk = sb("d_junk", [P, D])
        squares = sb("squares", [P, UNITS])
        ys2, w2, dsum, mod_eps = sb("ys2", [P, B]), sb("w2", [P, D]), sb("dsum", [P, B]), sb("m_eps", [P, 1])
        rms = sb("rms", [P, UNITS]); unit = sb("unit", [P, UNITS]); eps = sb("d_eps", [P, 1])
        pj = [ps(f"dpj{i}", [P, 512]) for i in range(2)]
        s_ps = [ps(f"s_ps{i}", [P, 2, T]) for i in range(2)]
        t_ps = [ps(f"dt_ps{i}", [P, SEG, P]) for i in range(2)]
        o_ps = [ps(f"o_ps{i}", [P, D]) for i in range(2)]
        pj_in = sem("d_pj_in"); pj_kept = sem("d_pj_kept"); pre = sem("d_pre")
        lam_in = sem("lam_in"); lam_exp = sem("lam_exp"); lam_done = sem("lam_done")
        s_in = sem("d_s"); max_done = sem("d_max"); exp_done = sem("d_exp"); link = sem("d_link"); diff_done = sem("d_diff")
        t_in = sem("d_t"); t_kept = sem("d_t_kept"); o_in = sem("d_o"); o_kept = sem("d_o_kept"); sq_done = sem("d_sq")
        rms_done = sem("d_rms"); mod_ready = sem("mod_ready"); mod_in = sem("mod_in"); mod_kept = sem("mod_kept"); unit_done = sem("d_unit"); normed = sem("d_normed"); back_in = sem("d_back"); added = sem("d_added")

        with nc.Block() as block:

            @block.gpsimd
            def _(pool):
                pool.memset(mod_eps[:, :], MOD_EPS)
                pool.tensor_scalar(n.ys[:, :], n.condT, float(D) ** -0.5, None, ALU.mult).then_inc(mod_ready, 1)
                pool.tensor_tensor(w2[:, :], n.wmod[:, :], n.wmod[:, :], ALU.mult).then_inc(mod_ready, 1)
                pool.wait_ge(mod_ready, 1)
                pool.tensor_tensor(ys2[:, :], n.ys[:, :], n.ys[:, :], ALU.mult).then_inc(mod_ready, 1)

            @block.tensor
            def _(pe):
                pe.wait_ge(pre, 1)
                for i, row in enumerate(("lk1", "lk2")):
                    r0 = ROWS[row][0]
                    mm = nc.tensor.matmul(o_ps[0][:, i:i + 1], lq[:, i, :], n.cols[:, r0:r0 + 1], start=True, stop=True)
                mm.then_inc(lam_in, 1)
                pe.wait_ge(mod_ready, 3)
                nc.tensor.matmul(o_ps[1][:, 0:B], w2[:, :], ys2[:, :], start=True, stop=True).then_inc(mod_in, 1)
                for g in range(6):
                    if g >= 2:
                        pe.wait_ge(pj_kept, g - 1)
                    for i in range(2):
                        if g < 2:
                            w, c0 = (n.wq12, n.wk12)[g], B * (T - SPAN + 1)
                            mm = nc.tensor.matmul(pj[g % 2][:, 256 * i:256 * i + 256], w[:, D * i:D * i + D],
                                                  s2[:, c0:c0 + B * SPAN], start=True, stop=True)
                        else:
                            states = s2[:, B * (P + 1):B * (T + 1)].rearrange("p (t b) -> p b t", b=B)[:, 2 * (g - 2) + i]
                            mm = nc.tensor.matmul(pj[g % 2][:, D * i:D * i + D], states, n.wv1[:, :], start=True, stop=True)
                    mm.then_inc(pj_in, 1)
                pe.wait_ge(pj_kept, 6)

                def scores(u):
                    b, i = divmod(u, SEG)
                    if u >= 2:
                        pe.wait_ge(exp_done, 2 * (u - 1))
                    for m in range(2):
                        mm = nc.tensor.matmul(s_ps[u % 2][:, m, :], qk[:, m, P * u:P * u + P],
                                              qk[:, 2 + m, T * b:T * b + T], start=True, stop=True)
                    mm.then_inc(s_in, 1)

                def turn(u):
                    pe.wait_ge(diff_done, u + 1)
                    if u >= 2:
                        pe.wait_ge(t_kept, u - 1)
                    for i in range(SEG):
                        mm = nc.tensor.transpose(t_ps[u % 2][:, i, :], diff[u % 2][:, P * i:P * i + P], n.ident[:, :])
                    mm.then_inc(t_in, 1)

                def attend(u):
                    pe.wait_ge(t_kept, u + 1)
                    if u >= 2:
                        pe.wait_ge(o_kept, u - 1)
                        pe.wait_ge(sq_done, u - 1)
                    for i in range(SEG):
                        mm = nc.tensor.matmul(o_ps[u % 2][:, :], diffT[u % 2][:, i, :], vt[:, u // SEG * SEG + i, :],
                                              start=(i == 0), stop=(i == SEG - 1))
                    mm.then_inc(o_in, 1)

                pe.wait_ge(lam_exp, 1)
                pe.wait_ge(mod_kept, 1)
                scores(0)
                scores(1)
                for u in range(UNITS + 1):
                    if u + 2 < UNITS:
                        scores(u + 2)
                    if u >= 1:
                        attend(u - 1)
                    if u < UNITS:
                        turn(u)
                for g in range(4):
                    pe.wait_ge(normed, 4 * (g + 1))
                    if g >= 2:
                        pe.wait_ge(added, g - 1)
                    for i in range(4):
                        mm = nc.tensor.transpose(pj[g % 2][:, P * i:P * i + P], heads[:, 4 * g + i, :], n.ident[:, :])
                    mm.then_inc(back_in, 1)

            @block.scalar
            def _(act):
                act.wait_ge(lam_in, 1)
                nc.scalar.activation(lam2[:, :], o_ps[0][:, 0:2], ACT.Exp).then_inc(lam_exp, 1)
                act.wait_ge(mod_in, 1)
                nc.scalar.activation(dsum[:, :], o_ps[1][:, 0:B], ACT.Copy).then_inc(mod_kept, 1)
                for g in range(6):
                    act.wait_ge(pj_in, g + 1)
                    if g < 2:
                        out = qk[:, 2 * g:2 * g + 2, :].rearrange("p k (b t) -> p k t b", b=B)[:, :, T - SPAN:T]
                        for i in range(2):
                            last = nc.scalar.activation(out[:, i], pj[g % 2][:, 256 * i:256 * i + 256].rearrange("p (t b) -> p t b", b=B), ACT.Copy)
                    else:
                        out = vt.rearrange("p (b s) d -> p s b d", s=SEG)[:, 1, 2 * (g - 2):2 * (g - 2) + 2, :]
                        last = nc.scalar.activation(out, pj[g % 2][:, 0:256].rearrange("p (b d) -> p b d", d=D), ACT.Copy)
                    last.then_inc(pj_kept, 1)

                def exps(u):
                    act.wait_ge(max_done, u + 1)
                    if u >= 2:
                        act.wait_ge(diff_done, u - 1)
                    for m in range(2):
                        nc.scalar.activation(probs[u % 2][:, m, :], s_ps[u % 2][:, m, :], ACT.Exp,
                                             bias=negmax[u % 2][:, m:m + 1], scale=SCALE,
                                             accum_out=sums[u % 2][:, m:m + 1]).then_inc(exp_done, 1)

                def keep(u):
                    act.wait_ge(t_in, u + 1)
                    if u >= 2:
                        act.wait_ge(o_in, u - 1)
                    nc.scalar.activation(diffT[u % 2][:, :, :], t_ps[u % 2][:, :, :], ACT.Copy).then_inc(t_kept, 1)

                exps(0)
                for u in range(UNITS):
                    if u + 1 < UNITS:
                        exps(u + 1)
                    keep(u)
                    if u >= 1:
                        act.wait_ge(o_kept, u)
                        if u >= 2:
                            act.wait_ge(sq_done, u - 1)
                        nc.scalar.activation(junk[:, :], heads[:, u - 1, :], ACT.Square,
                                             accum_out=squares[:, u - 1:u]).then_inc(sq_done, 1)
                act.wait_ge(o_kept, UNITS)
                act.wait_ge(sq_done, UNITS - 1)
                nc.scalar.activation(junk[:, :], heads[:, UNITS - 1, :], ACT.Square,
                                     accum_out=squares[:, UNITS - 1:UNITS]).then_inc(sq_done, 1)
                act.wait_ge(sq_done, UNITS)
                nc.scalar.activation(rms[:, :], squares[:, :], ACT.Sqrt, bias=eps[:, 0:1], scale=1.0 / D).then_inc(rms_done, 1)
                act.wait_ge(mod_kept, 1)
                nc.scalar.activation(dsum[:, :], dsum[:, :], ACT.Sqrt, bias=mod_eps[:, 0:1]).then_inc(mod_kept, 1)

            @block.vector
            def _(dve):
                V = nc.vector
                for i, row in enumerate(("lq1", "lq2")):
                    r0 = ROWS[row][0]
                    last = V.tensor_copy(lq[:, i, :], n.cols[:, r0:r0 + 1].broadcast_to([P, P]))
                last.then_inc(pre, 1)
                V.memset(eps[:, :], EPS)
                dve.wait_ge(lam_exp, 1)
                V.tensor_tensor(lam[:, :], lam2[:, 1:2], lam2[:, 0:1], ALU.subtract).then_inc(lam_done, 1)
                dve.wait_ge(lam_done, 1)
                V.tensor_scalar(lam[:, :], lam[:, :], -LAMBDA_INIT, None, ALU.add).then_inc(lam_done, 1)
                dve.wait_ge(lam_done, 2)

                def maxima(u):
                    dve.wait_ge(s_in, u + 1)
                    if u >= 2:
                        dve.wait_ge(exp_done, 2 * (u - 1))
                    V.tensor_reduce(negmax[u % 2][:, :], s_ps[u % 2][:, :, :], AX.X, ALU.max).then_inc(link, 1)
                    dve.wait_ge(link, u + 1)
                    V.tensor_scalar(negmax[u % 2][:, :], negmax[u % 2][:, :], -SCALE, None, ALU.mult).then_inc(max_done, 1)

                def difference(u):
                    p = u % 2
                    dve.wait_ge(exp_done, 2 * (u + 1))
                    V.reciprocal(inv[p][:, :], sums[p][:, :]).then_inc(unit_done, 1)
                    dve.wait_ge(unit_done, 3 * u + 1)
                    V.tensor_tensor(inv[p][:, 1:2], inv[p][:, 1:2], lam[:, :], ALU.mult).then_inc(unit_done, 1)
                    if u >= 2:
                        dve.wait_ge(t_in, u - 1)
                    dve.wait_ge(unit_done, 3 * u + 2)
                    V.tensor_scalar(diff[p][:, :], probs[p][:, 0, :], inv[p][:, 0:1], None, ALU.mult).then_inc(unit_done, 1)
                    dve.wait_ge(unit_done, 3 * u + 3)
                    V.scalar_tensor_tensor(diff[p][:, :], probs[p][:, 1, :], inv[p][:, 1:2], diff[p][:, :],
                                           ALU.mult, ALU.add).then_inc(diff_done, 1)

                def keep(u):
                    dve.wait_ge(o_in, u + 1)
                    V.tensor_copy(heads[:, u, :], o_ps[u % 2][:, :]).then_inc(o_kept, 1)

                maxima(0)
                for u in range(UNITS):
                    if u + 1 < UNITS:
                        maxima(u + 1)
                    difference(u)
                    if u >= 1:
                        keep(u - 1)
                keep(UNITS - 1)
                dve.wait_ge(rms_done, 1)
                V.reciprocal(unit[:, :], rms[:, :]).then_inc(link, 1)
                dve.wait_ge(mod_kept, 2)
                V.reciprocal(n.dr[:, :], dsum[:, :])
                dve.wait_ge(link, UNITS + 1)
                for u in range(UNITS):
                    V.tensor_scalar(heads[:, u, :], heads[:, u, :], unit[:, u:u + 1], 1.0 - LAMBDA_INIT,
                                    ALU.mult, ALU.mult).then_inc(normed, 1)
                for g in range(4):
                    dve.wait_ge(back_in, g + 1)
                    x = n.xT[:, :].rearrange("p (t b) -> p b t", b=B)[:, 2 * g:2 * g + 2]
                    V.tensor_tensor(x, pj[g % 2][:, :].rearrange("p (b t) -> p b t", b=2), x, ALU.add).then_inc(added, 1)


def modulated_linear(nc, n, mB):
    with ExitStack() as local:
        def sem(name):
            return local.enter_context(nc.semaphore(name))

        xs = local.enter_context(nc.sbuf_tensor("xs", [P, TOK], F32))
        m_ps = [local.enter_context(nc.psum_tensor(f"m_ps{i}", [P, 512], F32)) for i in range(4)]
        scaled = sem("m_scaled"); lin = sem("m_lin")
        w = 512 // B

        with nc.Block() as block:

            @block.tensor
            def _(pe):
                for g in range(4):
                    pe.wait_ge(scaled, g + 1)
                    nc.tensor.matmul(m_ps[g][:, :], n.wmod[:, :], xs[:, 512 * g:512 * g + 512], start=True, stop=True).then_inc(lin, 1)

            @block.vector
            def _(dve):
                for g in range(4):
                    cols = slice(512 * g, 512 * g + 512)
                    nc.vector.tensor_tensor(xs[:, cols].rearrange("p (t b) -> p t b", b=B),
                                            n.xT[:, cols].rearrange("p (t b) -> p t b", b=B),
                                            n.ys[:, :].unsqueeze(1).broadcast_to([P, w, B]), ALU.mult).then_inc(scaled, 1)
                for g in range(4):
                    dve.wait_ge(lin, g + 1)
                    out = mB[:, :].rearrange("p (b t) -> p t b", b=B)[:, w * g:w * g + w]
                    nc.vector.tensor_tensor(out, m_ps[g][:, :].rearrange("p (t b) -> p t b", b=B),
                                            n.dr[:, :].unsqueeze(1).broadcast_to([P, w, B]), ALU.mult)


def experts_l1(nc, n, inB, wgT, wuT, wdT, out):
    TILE = 512
    TB = TILE // P
    TILES = TOK // TILE
    UNITS = TILES * E
    LATE = 2
    wide = [P, NBLK, E]
    with ExitStack() as local:
        def sb(name, shape, dt=F32):
            return local.enter_context(nc.sbuf_tensor(name, shape, dt))

        def ps(name, shape, dt=F32):
            return local.enter_context(nc.psum_tensor(name, shape, dt))

        def sem(name):
            return local.enter_context(nc.semaphore(name))

        hid = [sb(f"x_hid{i}", [P, NF, TILE]) for i in range(2)]
        acc = [sb(f"x_acc{i}", [P, TB, D]) for i in range(2)]
        gate = [sb(f"x_gate{i}", [P, TILE]) for i in range(2)]
        val, mark, one, two, comb = (sb(k, wide) for k in ("m_val", "m_mark", "m_one", "m_two", "comb"))
        v1, v2, first, pa, pb = (sb(k, [P, NBLK]) for k in ("m_v1", "m_v2", "m_first", "m_pa", "m_pb"))
        iota_m8 = sb("m_iota", [P, E])
        h_ps = [ps(f"x_h_ps{i}", [P, TILE]) for i in range(4)]
        y_ps = [ps(f"x_y_ps{i}", [P, TB, D]) for i in range(2)]
        x_ps = ps("x_x_ps", [P, TILE])
        g_ps = ps("x_g_ps", wide)
        h_in = sem("x_h_in"); gate_done = sem("x_gate_done"); h_done = sem("x_h_done"); y_in = sem("x_y_in")
        summed = sem("x_summed"); x_in = sem("x_x_in"); x_kept = sem("x_x_kept"); stored = sem("x_stored")
        logits_in = sem("x_logits"); step = sem("x_step"); exp_in = sem("x_exp_in"); exp_done = sem("x_exp_done")

        with nc.Block() as block:

            @block.tensor
            def _(pe):
                def hidden(v):
                    t, e = divmod(v, E)
                    for f in range(NF):
                        for k, w in enumerate((wgT, wuT)):
                            g = (v * NF + f) * 2 + k
                            if g >= 4:
                                pe.wait_ge(h_done, (g - 4) // 2 + 1)
                            nc.tensor.matmul(h_ps[g % 4][:, :], w[:, e, P * f:P * f + P],
                                             inB[:, TILE * t:TILE * t + TILE], start=True, stop=True).then_inc(h_in, 1)

                def output(v):
                    t, e = divmod(v, E)
                    if v >= 2:
                        pe.wait_ge(summed, TB * (v - 1))
                    pe.wait_ge(h_done, NF * (v + 1))
                    for i in range(TB):
                        for f in range(NF):
                            mm = nc.tensor.matmul(y_ps[v % 2][:, i, :], hid[v % 2][:, f, P * i:P * i + P],
                                                  wdT[:, e, f, :], start=(f == 0), stop=(f == NF - 1))
                    mm.then_inc(y_in, 1)

                def turn(t):
                    if t:
                        pe.wait_ge(x_kept, t)
                    for i in range(TB):
                        b, s = divmod(TB * t + i, T // P)
                        x = n.xT[:, :].rearrange("p (t b) -> p b t", b=B)[:, b, P * s:P * s + P]
                        mm = nc.tensor.transpose(x_ps[:, P * i:P * i + P], x, n.ident[:, :])
                    mm.then_inc(x_in, 1)

                g0 = ROWS["gate"][0]
                for i in range(NBLK):
                    mm = nc.tensor.matmul(g_ps[:, i, :], inB[:, P * i:P * i + P], n.cols[:, g0:g0 + E], start=True, stop=True)
                mm.then_inc(logits_in, 1)
                hidden(0)
                for v in range(UNITS):
                    if v % E == 0:
                        turn(v // E)
                    if v + 1 < UNITS:
                        hidden(v + 1)
                    output(v)

            @block.scalar
            def _(act):
                for v in range(UNITS):
                    if v == 2:
                        act.wait_ge(exp_in, 1)
                        nc.scalar.activation(pb[:, :], pa[:, :], ACT.Exp).then_inc(exp_done, 1)
                    for f in range(NF):
                        g = v * NF + f
                        act.wait_ge(h_in, 2 * g + 1)
                        if g >= 2:
                            act.wait_ge(h_done, g - 1)
                        nc.scalar.activation(gate[g % 2][:, :], h_ps[2 * g % 4][:, :], ACT.Silu).then_inc(gate_done, 1)

            @block.vector
            def _(dve):
                V = nc.vector
                at = [0]

                def done(ins):
                    at[0] += 1
                    ins.then_inc(step, 1)

                def after():
                    dve.wait_ge(step, at[0])

                def per_token(ap):
                    return ap[:, :].unsqueeze(2).broadcast_to(wide)

                ramp = iota_m8[:, :].unsqueeze(1).broadcast_to(wide)

                def gate_stage(k):
                    if k == 0:
                        dve.wait_ge(logits_in, 1)
                        done(V.tensor_copy(val[:, :, :], g_ps[:, :, :]))
                    top, hot = (v1, one) if k < 5 else (v2, two)
                    if k in (0, 4):
                        top = v1 if k == 0 else v2
                        after()
                        done(V.tensor_reduce(top[:, :], val[:, :, :], AX.X, ALU.max))
                    elif k in (1, 5):
                        after()
                        done(V.tensor_tensor(mark[:, :, :], val[:, :, :], per_token(top), ALU.is_equal))
                        after()
                        done(V.tensor_tensor(mark[:, :, :], mark[:, :, :], ramp, ALU.mult))
                    elif k in (2, 6):
                        after()
                        done(V.tensor_reduce(first[:, :], mark[:, :, :], AX.X, ALU.min))
                        after()
                        done(V.tensor_tensor(hot[:, :, :], ramp, per_token(first), ALU.is_equal))
                    elif k == 3:
                        after()
                        flat = val[:, :, :].rearrange("p i e -> p (i e)")
                        done(V.scalar_tensor_tensor(flat, one[:, :, :].rearrange("p i e -> p (i e)"), -3.0e38, flat,
                                                    ALU.mult, ALU.add))
                    if k == 4:
                        after()
                        V.tensor_tensor(pa[:, :], v2[:, :], v1[:, :], ALU.subtract).then_inc(exp_in, 1)
                    if k == 7:
                        dve.wait_ge(exp_done, 1)
                        done(V.tensor_scalar(v1[:, :], pb[:, :], 1.0, None, ALU.add))
                        after()
                        done(V.reciprocal(pa[:, :], v1[:, :]))
                    elif k == 8:
                        after()
                        done(V.tensor_tensor(pb[:, :], pb[:, :], pa[:, :], ALU.mult))
                        done(V.tensor_tensor(one[:, :, :], one[:, :, :], per_token(pa), ALU.mult))
                    elif k == 9:
                        after()
                        done(V.tensor_tensor(two[:, :, :], two[:, :, :], per_token(pb), ALU.mult))
                        after()
                        done(V.tensor_tensor(comb[:, :, :], one[:, :, :], two[:, :, :], ALU.add))

                def weighted(w):
                    t, e = divmod(w, E)
                    dve.wait_ge(y_in, w + 1)
                    dve.wait_ge(x_kept, t + 1)
                    if e:
                        dve.wait_ge(summed, TB * w)
                    if w == 0:
                        after()
                    for i in range(TB):
                        V.scalar_tensor_tensor(acc[t % 2][:, i, :], y_ps[w % 2][:, i, :],
                                               comb[:, TB * t + i, e:e + 1], acc[t % 2][:, i, :],
                                               ALU.mult, ALU.add).then_inc(summed, 1)

                done(V.tensor_scalar(iota_m8[:, :], n.iota8[:, :], -float(E), None, ALU.add))
                for v in range(UNITS):
                    t, e = divmod(v, E)
                    if v >= 2:
                        dve.wait_ge(y_in, v - 1)
                    for f in range(NF):
                        g = v * NF + f
                        dve.wait_ge(gate_done, g + 1)
                        dve.wait_ge(h_in, 2 * g + 2)
                        V.tensor_tensor(hid[v % 2][:, f, :], gate[g % 2][:, :], h_ps[(2 * g + 1) % 4][:, :],
                                        ALU.mult).then_inc(h_done, 1)
                        if g < 10:
                            gate_stage(g)
                    if e == 0:
                        dve.wait_ge(x_in, t + 1)
                        if t >= 2:
                            dve.wait_ge(stored, 16 * (t - 1))
                        V.tensor_copy(acc[t % 2][:, :, :].rearrange("p i d -> p (i d)"), x_ps[:, :]).then_inc(x_kept, 1)
                    if v == LATE:
                        weighted(0)
                    if v >= LATE:
                        weighted(v - 1)
                weighted(UNITS - 1)

            @block.sync
            def _(sp):
                for t in range(TILES):
                    sp.wait_ge(summed, TB * E * (t + 1))
                    dst = out.rearrange("b (s p) d -> p (b s) d", p=P)[:, TB * t:TB * t + TB]
                    sp.dma_start(dst, acc[t % 2][:, :, :]).then_inc(stored, 16)
                sp.wait_ge(stored, 16 * TILES)


def program(nc, a, out):
    with ExitStack() as ctx:
        n = allocate(nc, ctx)
        with ExitStack() as mid:
            yB = mid.enter_context(nc.sbuf_tensor("yB", [P, TOK], F32))
            wqkv = mid.enter_context(nc.sbuf_tensor("wqkv", [P, 3 * INNER], F32))
            wout = mid.enter_context(nc.sbuf_tensor("wout", [P, NC, D], F32))
            with ExitStack() as early:
                wq, wk, wv = (early.enter_context(nc.sbuf_tensor(k, [P, INNER], F32)) for k in ("wq", "wk", "wv"))
                wo = early.enter_context(nc.sbuf_tensor("wo", [P, NC, D], F32))
                setup(nc, n, a, wq, wk, wv, wo)
                local_attention(nc, n, a, yB, wq, wk, wv, wo, wqkv, wout)
            linear_attention(nc, n, yB, wqkv, wout)
        with ExitStack() as mid:
            w1 = mid.enter_context(nc.sbuf_tensor("w1", [P, E, FF], F32))
            w2 = mid.enter_context(nc.sbuf_tensor("w2e", [P, E, NF, D], F32))
            hist = mid.enter_context(nc.sbuf_tensor("hist", [P, 16 * (T + P // B)], F32))
            diffT = mid.enter_context(nc.sbuf_tensor("expert_diff", [P, TOK], F32))
            logits = mid.enter_context(nc.sbuf_tensor("logits", [P, NBLK, E], F32))
            gru_scan(nc, n, a, hist, w1, w2, diffT, logits)
            route_top1(nc, n, logits, diffT)
        wgT = ctx.enter_context(nc.sbuf_tensor("wgT", [P, E, FF], F32))
        wuT = ctx.enter_context(nc.sbuf_tensor("wuT", [P, E, FF], F32))
        wdT = ctx.enter_context(nc.sbuf_tensor("wdT", [P, E, NF, D], F32))
        with ExitStack() as mid:
            s2 = mid.enter_context(nc.sbuf_tensor("s2", [P, TOK + P], F32))
            qk = mid.enter_context(nc.sbuf_tensor("qk", [P, 4, TOK], F32))
            vt = mid.enter_context(nc.sbuf_tensor("vt", [P, NBLK, D], F32))
            gate_scan(nc, n, a, s2, qk, vt, wgT, wuT, wdT)
            diff_attention(nc, n, s2, qk, vt)
        mB = ctx.enter_context(nc.sbuf_tensor("mB", [P, TOK], F32))
        modulated_linear(nc, n, mB)
        experts_l1(nc, n, mB, wgT, wuT, wdT, out)


def kernel(**inputs):
    import numpy as np
    import concourse.bacc as bacc
    from concourse.bass_utils import run_bass_kernel_spmd

    nc = bacc.Bacc("TRN2", target_bir_lowering=False, num_devices=1)
    arrays, aps = {}, {}
    for name, value in inputs.items():
        arrays[f"in_{name}"] = np.ascontiguousarray(value)
        aps[name] = nc.dram_tensor(f"in_{name}", arrays[f"in_{name}"].shape, F32, kind="ExternalInput").ap()
    out = nc.dram_tensor("out", (B, T, D), F32, kind="ExternalOutput").ap()
    program(nc, aps, out)
    result = run_bass_kernel_spmd(nc, [arrays], core_ids=[0])
    return result.results[0]["out"]
```
